# Optimizing a Trainium2 kernel written in Bass

```python
import numpy as np
import jax
import jax.numpy as jnp

def _softmax(x, axis=-1):
    return jax.nn.softmax(x, axis=axis)

def _gelu(x):
    return jax.nn.gelu(x, approximate=True)

def _silu(x):
    return jax.nn.silu(x)

def _sigmoid(x):
    return jax.nn.sigmoid(x)

def _layernorm(x, axis=-1, eps=1e-05):
    m = jnp.mean(x, axis=axis, keepdims=True)
    v = jnp.var(x, axis=axis, keepdims=True)
    return (x - m) / jnp.sqrt(v + eps)

def _scatter_add(tgt, idx, src, axis=0):
    return tgt.at[idx].add(src)

def _segment_sum(src, seg, n):
    return jax.ops.segment_sum(src, seg, n)
kernel_name = 'mk_decoder_postln_d1_seqx_r8_6158b8'

def setup_inputs(seed: int=0):
    np.random.seed(seed)
    _w = jnp.asarray

    def _rec_inputs():
        import jax
        import jax.numpy as jnp
        _rk = jax.random.key(seed)
        x = -0.0002928 + 1 * jax.random.normal(jax.random.fold_in(_rk, 1), (32, 64, 128), jnp.float32)
        _lenS = 64 - jax.random.randint(jax.random.fold_in(_rk, 7), (32,), 0, max(1, 64 // 4) + 1, jnp.int32)
        _lenS2 = 64 - jax.random.randint(jax.random.fold_in(_rk, 8), (32,), 0, max(1, 64 // 4) + 1, jnp.int32)
        _ctx_1024P = jax.random.normal(jax.random.fold_in(_rk, 11), (32, 16, 128), jnp.float32)
        _ctx_1024c = jax.random.dirichlet(jax.random.fold_in(_rk, 511), 0.3 * jnp.ones((16,), jnp.float32), (32, 64))
        _ctx_1024t = jnp.einsum('bsk,bkd->bsd', _ctx_1024c, _ctx_1024P)
        _ctx_1024t = _ctx_1024t * jax.lax.rsqrt(jnp.mean(jnp.square(_ctx_1024t)) + 1e-12) * 0.953939
        ctx_1024 = -1.39393e-06 + 0.999914 * (_ctx_1024t + 0.3 * jax.random.normal(jax.random.fold_in(_rk, 611), (32, 64, 128), jnp.float32))
        return (x, ctx_1024)
    x, ctx_1024 = _rec_inputs()

    def _L0_attn_setup():
        import jax, jax.numpy as jnp
        import numpy as np
        NUM_HEADS = 16
        CHUNK_SIZE = 64
        NEG_INF = -1000000000.0

        def chunk_mask(seq_len, chunk_size):
            idx = jnp.arange(seq_len)
            cid = idx // chunk_size
            future = idx[None, :] > idx[:, None]
            diff_chunk = cid[None, :] != cid[:, None]
            return future & diff_chunk
        key = jax.random.key(seed)
        k1, k2, k3 = jax.random.split(key, 3)
        S, B, E = (256, 2, 128)
        x = jax.random.normal(k1, (S, B, E), dtype=jnp.float32)
        in_proj_w = jax.random.normal(k2, (3 * E, E), dtype=jnp.float32) * E ** (-0.5)
        in_proj_b = jnp.zeros((3 * E,), dtype=jnp.float32)
        out_proj_w = jax.random.normal(k3, (E, E), dtype=jnp.float32) * E ** (-0.5)
        out_proj_b = jnp.zeros((E,), dtype=jnp.float32)
        return {'x': x, 'in_proj_w': in_proj_w, 'in_proj_b': in_proj_b, 'out_proj_w': out_proj_w, 'out_proj_b': out_proj_b}
    _L0_attn_all = _L0_attn_setup()
    _L0_attn_in = {k: v for k, v in _L0_attn_all.items() if k in ('in_proj_w', 'in_proj_b', 'out_proj_w', 'out_proj_b')}
    del _L0_attn_all

    def _L0_xattn_setup():
        import jax, jax.numpy as jnp
        import numpy as np
        N, T, HID, H = (2, 256, 128, 16)
        D = HID // H
        key = jax.random.key(seed)
        ks = jax.random.split(key, 11)
        s = 1.0 / np.sqrt(HID)
        return {'q': jax.random.normal(ks[0], (N, T, HID), jnp.float32), 'k': jax.random.normal(ks[1], (N, T, HID), jnp.float32), 'v': jax.random.normal(ks[2], (N, T, HID), jnp.float32), 'Wq': jax.random.normal(ks[3], (HID, HID), jnp.float32) * s, 'bq': jnp.zeros((HID,), jnp.float32), 'Wk': jax.random.normal(ks[4], (HID, HID), jnp.float32) * s, 'bk': jnp.zeros((HID,), jnp.float32), 'Wv': jax.random.normal(ks[5], (HID, HID), jnp.float32) * s, 'bv': jnp.zeros((HID,), jnp.float32), 'Wo': jax.random.normal(ks[6], (HID, HID), jnp.float32) * s, 'bo': jnp.zeros((HID,), jnp.float32)}
    _L0_xattn_all = _L0_xattn_setup()
    _L0_xattn_in = {k: v for k, v in _L0_xattn_all.items() if k in ('Wq', 'bq', 'Wk', 'bk', 'Wv', 'bv', 'Wo', 'bo')}
    del _L0_xattn_all

    def _L0_ffn_setup():
        import jax, jax.numpy as jnp
        import numpy as np
        D_MODEL = 128
        D_FF = 512
        NUM_M = 2
        E_ROUTER = 8 * NUM_M - 1
        D_FF_R = D_FF // NUM_M
        TOP_K = NUM_M * 2 - 1
        B, T = (2, 256)

        def _expert_stack(x, W1, b1, W2, b2):
            h = jax.nn.gelu(jnp.einsum('btd,edf->ebtf', x, W1) + b1[:, None, None, :], approximate=False)
            return jnp.einsum('ebtf,efd->ebtd', h, W2) + b2[:, None, None, :]
        key = jax.random.key(seed)
        ks = jax.random.split(key, 12)
        s = lambda fan_in: 1.0 / np.sqrt(fan_in)
        x = jax.random.normal(ks[0], (B, T, D_MODEL), dtype=jnp.float32)
        sW1 = jax.random.uniform(ks[1], (1, D_MODEL, D_FF), jnp.float32, -s(D_MODEL), s(D_MODEL))
        sb1 = jax.random.uniform(ks[2], (1, D_FF), jnp.float32, -s(D_MODEL), s(D_MODEL))
        sW2 = jax.random.uniform(ks[3], (1, D_FF, D_MODEL), jnp.float32, -s(D_FF), s(D_FF))
        sb2 = jax.random.uniform(ks[4], (1, D_MODEL), jnp.float32, -s(D_FF), s(D_FF))
        rW1 = jax.random.uniform(ks[5], (E_ROUTER, D_MODEL, D_FF_R), jnp.float32, -s(D_MODEL), s(D_MODEL))
        rb1 = jax.random.uniform(ks[6], (E_ROUTER, D_FF_R), jnp.float32, -s(D_MODEL), s(D_MODEL))
        rW2 = jax.random.uniform(ks[7], (E_ROUTER, D_FF_R, D_MODEL), jnp.float32, -s(D_FF_R), s(D_FF_R))
        rb2 = jax.random.uniform(ks[8], (E_ROUTER, D_MODEL), jnp.float32, -s(D_FF_R), s(D_FF_R))
        gW = jax.random.uniform(ks[9], (D_MODEL, E_ROUTER), jnp.float32, -s(D_MODEL), s(D_MODEL))
        gb = jax.random.uniform(ks[10], (E_ROUTER,), jnp.float32, -s(D_MODEL), s(D_MODEL))
        return {'x': x, 'sW1': sW1, 'sb1': sb1, 'sW2': sW2, 'sb2': sb2, 'rW1': rW1, 'rb1': rb1, 'rW2': rW2, 'rb2': rb2, 'gW': gW, 'gb': gb}
    _L0_ffn_all = _L0_ffn_setup()
    _L0_ffn_in = {k: v for k, v in _L0_ffn_all.items() if k in ('sW1', 'sb1', 'sW2', 'sb2', 'rW1', 'rb1', 'rW2', 'rb2', 'gW', 'gb')}
    del _L0_ffn_all
    return {'x': x, 'ctx_1024': ctx_1024, 'L0_attn_in_proj_w': _L0_attn_in['in_proj_w'], 'L0_attn_in_proj_b': _L0_attn_in['in_proj_b'], 'L0_attn_out_proj_w': _L0_attn_in['out_proj_w'], 'L0_attn_out_proj_b': _L0_attn_in['out_proj_b'], 'L0_xattn_Wq': _L0_xattn_in['Wq'], 'L0_xattn_bq': _L0_xattn_in['bq'], 'L0_xattn_Wk': _L0_xattn_in['Wk'], 'L0_xattn_bk': _L0_xattn_in['bk'], 'L0_xattn_Wv': _L0_xattn_in['Wv'], 'L0_xattn_bv': _L0_xattn_in['bv'], 'L0_xattn_Wo': _L0_xattn_in['Wo'], 'L0_xattn_bo': _L0_xattn_in['bo'], 'L0_ffn_sW1': _L0_ffn_in['sW1'], 'L0_ffn_sb1': _L0_ffn_in['sb1'], 'L0_ffn_sW2': _L0_ffn_in['sW2'], 'L0_ffn_sb2': _L0_ffn_in['sb2'], 'L0_ffn_rW1': _L0_ffn_in['rW1'], 'L0_ffn_rb1': _L0_ffn_in['rb1'], 'L0_ffn_rW2': _L0_ffn_in['rW2'], 'L0_ffn_rb2': _L0_ffn_in['rb2'], 'L0_ffn_gW': _L0_ffn_in['gW'], 'L0_ffn_gb': _L0_ffn_in['gb']}

def reference(x, ctx_1024, L0_attn_in_proj_w, L0_attn_in_proj_b, L0_attn_out_proj_w, L0_attn_out_proj_b, L0_xattn_Wq, L0_xattn_bq, L0_xattn_Wk, L0_xattn_bk, L0_xattn_Wv, L0_xattn_bv, L0_xattn_Wo, L0_xattn_bo, L0_ffn_sW1, L0_ffn_sb1, L0_ffn_sW2, L0_ffn_sb2, L0_ffn_rW1, L0_ffn_rb1, L0_ffn_rW2, L0_ffn_rb2, L0_ffn_gW, L0_ffn_gb):
    import jax
    import jax.numpy as jnp

    def _L0_attn_ref(x, in_proj_w, in_proj_b, out_proj_w, out_proj_b):
        import jax, jax.numpy as jnp
        import numpy as np
        NUM_HEADS = 16
        CHUNK_SIZE = 64
        NEG_INF = -1000000000.0

        def chunk_mask(seq_len, chunk_size):
            idx = jnp.arange(seq_len)
            cid = idx // chunk_size
            future = idx[None, :] > idx[:, None]
            diff_chunk = cid[None, :] != cid[:, None]
            return future & diff_chunk
        S, B, E = x.shape
        H = NUM_HEADS
        D = E // H
        qkv = x @ in_proj_w.T + in_proj_b
        q, k, v = jnp.split(qkv, 3, axis=-1)
        q = q.reshape(S, B, H, D)
        k = k.reshape(S, B, H, D)
        v = v.reshape(S, B, H, D)
        scale = 1.0 / jnp.sqrt(jnp.asarray(D, dtype=x.dtype))
        scores = jnp.einsum('sbhd,tbhd->bhst', q * scale, k)
        mask = chunk_mask(S, CHUNK_SIZE)
        scores = jnp.where(mask[None, None, :, :], NEG_INF, scores)
        attn = jax.nn.softmax(scores, axis=-1)
        out = jnp.einsum('bhst,tbhd->sbhd', attn, v).reshape(S, B, E)
        return out @ out_proj_w.T + out_proj_b

    def _L0_xattn_ref(q, k, v, Wq, bq, Wk, bk, Wv, bv, Wo, bo):
        import jax, jax.numpy as jnp
        import numpy as np
        N, T, HID, H = (2, 256, 128, 16)
        D = HID // H
        n, t, _ = q.shape
        qh = (q @ Wq + bq).reshape(n, H, t, D)
        kh = (k @ Wk + bk).reshape(n, H, t, D)
        vh = (v @ Wv + bv).reshape(n, H, t, D)
        scores = jnp.einsum('nhtd,nhsd->nhts', qh, kh) / jnp.sqrt(jnp.float32(HID))
        attn = jax.nn.softmax(scores, axis=1)
        out = jnp.einsum('nhts,nhsd->nhtd', attn, vh).reshape(n, t, H * D)
        return out @ Wo + bo

    def _L0_ffn_ref(x, sW1, sb1, sW2, sb2, rW1, rb1, rW2, rb2, gW, gb):
        import jax, jax.numpy as jnp
        import numpy as np
        D_MODEL = 128
        D_FF = 512
        NUM_M = 2
        E_ROUTER = 8 * NUM_M - 1
        D_FF_R = D_FF // NUM_M
        TOP_K = NUM_M * 2 - 1
        B, T = (2, 256)

        def _expert_stack(x, W1, b1, W2, b2):
            h = jax.nn.gelu(jnp.einsum('btd,edf->ebtf', x, W1) + b1[:, None, None, :], approximate=False)
            return jnp.einsum('ebtf,efd->ebtd', h, W2) + b2[:, None, None, :]
        shared_enc = _expert_stack(x, sW1, sb1, sW2, sb2).sum(0)
        weights = jax.nn.softmax(x @ gW + gb, axis=-1)
        topv, topi = jax.lax.top_k(weights, TOP_K)
        gated = (jax.nn.one_hot(topi, E_ROUTER, dtype=weights.dtype) * topv[..., None]).sum(axis=-2)
        router_out = _expert_stack(x, rW1, rb1, rW2, rb2)
        router_enc = jnp.einsum('ebtd,bte->btd', router_out, gated)
        return shared_enc + router_enc + x
    x = _layernorm(x + _L0_attn_ref(x, L0_attn_in_proj_w, L0_attn_in_proj_b, L0_attn_out_proj_w, L0_attn_out_proj_b), axis=-1)
    x = _layernorm(x + _L0_xattn_ref(x, ctx_1024, ctx_1024, L0_xattn_Wq, L0_xattn_bq, L0_xattn_Wk, L0_xattn_bk, L0_xattn_Wv, L0_xattn_bv, L0_xattn_Wo, L0_xattn_bo), axis=-1)
    x = _layernorm(x + _L0_ffn_ref(x, L0_ffn_sW1, L0_ffn_sb1, L0_ffn_sW2, L0_ffn_sb2, L0_ffn_rW1, L0_ffn_rb1, L0_ffn_rW2, L0_ffn_rb2, L0_ffn_gW, L0_ffn_gb), axis=-1)
    return x

_drawn_inputs = setup_inputs


def setup_inputs(seed=0):
    import zlib

    import numpy as np

    out = dict(_drawn_inputs(seed))
    spreads = {'L0_attn_in_proj_b': (0.0, 0.1),
     'L0_attn_out_proj_b': (0.0, 0.1),
     'L0_xattn_bq': (0.0, 0.712),
     'L0_xattn_bk': (0.0, 0.605),
     'L0_xattn_bv': (0.0, 0.1),
     'L0_xattn_bo': (0.0, 0.1)}
    factors = {'L0_ffn_sb1': 6.415,
     'L0_ffn_sb2': 4.365,
     'L0_ffn_rW1': 2.716,
     'L0_ffn_rb1': 8.0,
     'L0_ffn_rb2': 8.0,
     'L0_ffn_gW': 2.772,
     'L0_ffn_gb': 8.0}
    for name, (base, spread) in spreads.items():
        noise = np.random.default_rng([zlib.crc32(name.encode()), seed]).standard_normal(out[name].shape)
        drawn = base * np.exp(spread * noise) if base else spread * noise
        out[name] = jnp.asarray(drawn.astype(out[name].dtype))
    for name, factor in factors.items():
        out[name] = (out[name] * factor).astype(out[name].dtype)
    return out
```

```python
from contextlib import ExitStack

import concourse.bass as bass
from concourse import mybir

F32 = mybir.dt.float32
BF16 = mybir.dt.bfloat16
ALU = mybir.AluOpType
ACT = mybir.ActivationFunctionType
AX_X = mybir.AxisListType.X

P = 128
E = 128
S, B = 32, 64
T = S * B
NG = T // P
NC = 4
D = 8
LAG2 = 7
NP = NG
EPS = 1e-5

W_Q, W_K, W_V, W_O, X_Q, X_K, X_V, X_O = (i * E for i in range(8))
C_ID = 0
C_HG = 128
C_H4 = 132
C_N2 = 136
C_H2 = 138
C_END = 140
R_BO, R_XQ, R_XK, R_XV, R_XO = (i * E for i in range(5))
R_END = 5 * E

NE = 15
FE = 256
NX = NE + 2
TOPK = 3


def build(nc, x_t, x_n, ctx_t, w_pack, c_pack, b_col, b_row, e_w1, e_w2, e_b1, e_b2, g_w, g_b, iota_row, out):
    v_scr = nc.dram_tensor("v_scr", [T, E], F32).ap()
    x1_scr = nc.dram_tensor("x1_scr", [T, E], F32).ap()
    ck_scr = nc.dram_tensor("ck_scr", [T * E], F32).ap()
    cv_scr = nc.dram_tensor("cv_scr", [T * E], F32).ap()
    cq_scr = nc.dram_tensor("cq_scr", [T * E], F32).ap()
    o_scr = nc.dram_tensor("o_scr", [T * E], F32).ap()

    with ExitStack() as ctx:
        def sb(name, shape, dt=F32):
            return ctx.enter_context(nc.sbuf_tensor(name, shape, dt))

        def sem(name):
            return ctx.enter_context(nc.semaphore(name))

        psum = ctx.enter_context(nc.psum_tensor("psum", [P, 8 * 512], F32))
        bank = [psum[:, 512 * i:512 * i + 512] for i in range(8)]

        w = sb("w", [P, 8 * E])
        cst = sb("cst", [P, C_END])
        bcol = sb("bcol", [P, 4])
        brow = sb("brow", [P, R_END])
        neg_id = sb("neg_id", [P, P], BF16)
        bkm = sb("bkm", [P, 4])
        wom = sb("wom", [P, 4, E])
        half = sb("half", [P, 4])

        xT = sb("xT", [P, T])
        xn = sb("xn", [P, NG, E])
        ctxT = sb("ctxT", [P, T])
        vn = sb("vn", [P, NG, E])
        vm = sb("vm", [P, B, E])
        qm = sb("qm", [P, 2, 16, 128])
        k4 = sb("k4", [P, 2, 4, 512])
        mb = sb("mb", [P, 2, 16], BF16)
        ex = sb("ex", [P, 3, 512])
        ssum = sb("ssum", [P, 2, 16])
        rs = sb("rs", [P, 2, 16])
        pt = sb("pt", [P, 2, 512])
        us = sb("us", [P, 2, 512])
        res = sb("res", [P, 2, 4, E])
        bst = sb("bst", [P, 2, 4, 6])
        mv = sb("mv", [P, 2, 4, 2])
        rstd = sb("rstd", [P, 2, 4])

        kv = sb("kv", [P, 2, NP, E])
        vx = sb("vx", [P, NP, 8, 2, 16])
        m2 = sb("m2", [P, 2, B], BF16)
        sum2 = sb("sum2", [P, 2, B])
        r2 = sb("r2", [P, 2, B])
        res2 = sb("res2", [P, 2, 4, E])
        bst2 = sb("bst2", [P, 2, 4, 6])
        mv2 = sb("mv2", [P, 2, 4, 2])
        rstd2 = sb("rstd2", [P, 2, 4])
        w1 = sb("w1", [P, NX, FE])
        w2 = sb("w2", [P, NX, 2, E])
        b1 = sb("b1", [P, NX, 2])
        b2 = sb("b2", [NE + 1, E])
        gw = sb("gw", [P, NE])
        gb = sb("gb", [P, NE])
        iota = sb("iota", [P, NE])
        lg = sb("lg", [P, NG, NE])
        lmax = sb("lmax", [P, NG])
        lsum = sb("lsum", [P, NG])
        top = sb("top", [P, NG, 8])
        topi = sb("topi", [P, NG, 8], mybir.dt.uint32)
        topf = sb("topf", [P, NG, 8])
        oh = sb("oh", [P, NG, TOPK, NE])
        gates = sb("gates", [P, NG, NX])
        mv3 = sb("mv3", [P, NG, 2])
        bst3 = sb("bst3", [P, NG, 6])
        rstd3 = sb("rstd3", [P, NG])
        half3 = sb("half3", [P, NG])
        x1 = xT[:, :].rearrange("p (g e) -> p g e", e=E)
        qs = vn
        qm_room = qm[:, :, :, :].rearrange("p a b c -> p (a b c)")
        k4_room = k4[:, :, :, :].rearrange("p a b c -> p (a b c)")
        vm_room = vm[:, :, :].rearrange("p b e -> p (b e)")
        x1T = qm_room[:, 0:1024].rearrange("p (a b) -> p a b", a=2)
        km = qm_room[:, 1024:2048].rearrange("p (a h b) -> p a h b", a=2, h=4)
        q4 = qm_room[:, 2048:3072].rearrange("p (a h b) -> p a h b", a=2, h=4)
        ota = qm_room[:, 3072:3328].rearrange("p (a b) -> p a b", a=2)
        ot = qm_room[:, 3328:3584].rearrange("p (a b) -> p a b", a=2)
        on = qm_room[:, 3584:4096].rearrange("p (a b) -> p a b", a=2)
        e2 = k4_room[:, 0:3072].rearrange("p (a b) -> p a b", a=3)
        orow = vm_room[:, 0:2048].rearrange("p (g e) -> p g e", e=E)
        x2 = vm_room[:, 2048:4096].rearrange("p (g e) -> p g e", e=E)
        qn = res
        acc = vm_room[:, 4096:6144].rearrange("p (g e) -> p g e", e=E)
        yg = vm_room[:, 6144:7168].rearrange("p (a b) -> p a b", a=2)
        x2T = ctxT
        gT = qm_room[0:NE + 1, 0:2048]
        hb = xn[:, :, :].rearrange("p g e -> p (g e)").rearrange("p (a b c) -> p a b c", a=2, b=2)

        ident = cst[:, C_ID:C_ID + P]
        m_n2 = cst[:, C_N2:C_N2 + 2]
        m_h2 = cst[:, C_H2:C_H2 + 2]
        m_hg = cst[:, C_HG:C_HG + 4]
        m_h4 = cst[:, C_H4:C_H4 + 4]

        s_const = sem("s_const")
        s_xT = [sem(f"s_xT{c}") for c in range(NC)]
        s_xn = sem("s_xn")
        s_prep = sem("s_prep")
        s_xb = sem("s_xb")
        s_brow = sem("s_brow")
        s_zero_d = sem("s_zero_d")
        s_zero_p = sem("s_zero_p")
        s_vproj = sem("s_vproj")
        s_vn = sem("s_vn")
        s_vst = [sem(f"s_vst{c}") for c in range(NC)]
        s_vm = [sem(f"s_vm{c}") for c in range(NC)]
        s_qp = sem("s_qp")
        s_kp = sem("s_kp")
        s_qm = sem("s_qm")
        s_k4 = sem("s_k4")
        s_sc = sem("s_sc")
        s_mb = sem("s_mb")
        s_sub = sem("s_sub")
        s_ex = sem("s_ex")
        s_sum = sem("s_sum")
        s_rs = sem("s_rs")
        s_pn = sem("s_pn")
        s_pt = sem("s_pt")
        s_u = sem("s_u")
        s_us = sem("s_us")
        s_y = sem("s_y")
        s_res = sem("s_res")
        s_bst = sem("s_bst")
        s_mv = sem("s_mv")
        s_ve = sem("s_ve")
        s_rstd = sem("s_rstd")
        s_x1 = sem("s_x1")
        s_x1st = [sem(f"s_x1st{c}") for c in range(NC)]

        s_ffw = sem("s_ffw")
        s_small = sem("s_small")
        s_x2t = sem("s_x2t")
        s_x2T = sem("s_x2T")
        s_lg = sem("s_lg")
        s_rt = sem("s_rt")
        s_gt = sem("s_gt")
        s_gT = sem("s_gT")
        s_b2 = sem("s_b2")
        s_acc = sem("s_acc")
        s_h = sem("s_h")
        s_ge = sem("s_ge")
        s_ye = sem("s_ye")
        s_yg = sem("s_yg")
        s_l3 = sem("s_l3")
        s_mv3 = sem("s_mv3")
        s_rstd3 = sem("s_rstd3")
        s_ctx = sem("s_ctx")
        s_out = sem("s_out")
        s_ckp = sem("s_ckp")
        s_ck = sem("s_ck")
        s_ckst = [sem(f"s_ckst{c}") for c in range(2 * NC)]
        s_ckl = [sem(f"s_ckl{c}") for c in range(NC)]
        s_cvl = [sem(f"s_cvl{c}") for c in range(NC)]
        s_vx = sem("s_vx")
        s_x1l = [sem(f"s_x1l{c}") for c in range(NC)]
        s_x1t = sem("s_x1t")
        s_x1T = sem("s_x1T")
        s_cqp = sem("s_cqp")
        s_cq = sem("s_cq")
        s_cqst = [sem(f"s_cqst{c}") for c in range(NC)]
        s_cql = [sem(f"s_cql{p}") for p in range(NP)]
        s_kqt = sem("s_kqt")
        s_km = sem("s_km")
        s_q4 = sem("s_q4")
        s_sc2 = sem("s_sc2")
        s_m2 = sem("s_m2")
        s_sub2 = sem("s_sub2")
        s_ex2 = sem("s_ex2")
        s_sum2 = sem("s_sum2")
        s_r2 = sem("s_r2")
        s_pn2 = sem("s_pn2")
        s_pv2 = sem("s_pv2")
        s_ota = sem("s_ota")
        s_ot = sem("s_ot")
        s_ont = sem("s_ont")
        s_on = sem("s_on")
        s_ost = [sem(f"s_ost{k}") for k in range(2)]
        s_orl = [sem(f"s_orl{c}") for c in range(NC)]
        s_ort = sem("s_ort")
        s_orT = sem("s_orT")
        s_y2 = sem("s_y2")
        s_xb2 = sem("s_xb2")
        s_res2 = sem("s_res2")
        s_bst2 = sem("s_bst2")
        s_mv2 = sem("s_mv2")
        s_ve2 = sem("s_ve2")
        s_rstd2 = sem("s_rstd2")
        s_x2 = sem("s_x2")

        block = ctx.enter_context(nc.Block())
        SCALE2 = float(E) ** -0.5

        def by_token(scratch, n):
            return scratch[n * B * E:(n + 1) * B * E].rearrange("(h t d) -> t h d", t=B, d=D)

        def by_row(scratch):
            return scratch.rearrange("(g p e) -> p g e", p=P, e=E)
        SCALE1 = float(D) ** -0.5

        @block.sync
        def _(sp):
            sp.dma_start(w[:, 0:4 * E], w_pack[:, 0:4 * E]).then_inc(s_const, 16)
            for c in range(NC):
                sp.dma_start(xT[:, 512 * c:512 * c + 512], x_t[:, 512 * c:512 * c + 512]).then_inc(s_xT[c], 16)
            sp.dma_start(w[:, 4 * E:8 * E], w_pack[:, 4 * E:8 * E]).then_inc(s_const, 16)
            sp.dma_start(ctxT[:, :], ctx_t).then_inc(s_ctx, 16)
            sp.dma_start(xn[:, :, :], x_n).then_inc(s_xn, 16)
            for c in range(NC):
                sp.wait_ge(s_vn, c + 1)
                sp.dma_start(v_scr.rearrange("(g p) e -> p g e", p=P)[:, 4 * c:4 * c + 4, :],
                             vn[:, 4 * c:4 * c + 4, :]).then_inc(s_vst[c], 16)
            sp.wait_ge(s_zero_d, 1)
            sp.wait_ge(s_zero_p, 1)
            for c in range(NC):
                sp.wait_ge(s_vst[c], 16)
                for g in range(4):
                    src = v_scr.rearrange("(b t) e -> t b e", t=S)[:, 16 * c:16 * c + 16, 32 * g:32 * g + 32]
                    sp.dma_start(vm[32 * g:32 * g + 32, 16 * c:16 * c + 16, 32 * g:32 * g + 32],
                                 src).then_inc(s_vm[c], 16)
            for c in range(2 * NC):
                i, h = c // 2, c % 2
                sp.wait_ge(s_ck, c + 1)
                sp.dma_start(by_row((ck_scr, cv_scr)[h])[:, 4 * i:4 * i + 4, :],
                             kv[:, h, 4 * i:4 * i + 4, :]).then_inc(s_ckst[c], 16)
            for p in range(NP):
                for h in range(2):
                    sp.wait_ge(s_ckst[2 * (p // 4) + h], 16)
                    for n in range(2):
                        sp.dma_start(kv[64 * n:64 * n + 64, h, p, :].rearrange("t (h d) -> t h d", d=D),
                                     by_token((ck_scr, cv_scr)[h], 2 * p + n)).then_inc((s_ckl, s_cvl)[h][p // 4], 16)
            sp.dma_start(w1[:, :, :], e_w1.rearrange("x p f -> p x f")).then_inc(s_ffw, 16)
            sp.dma_start(w2[:, :, :, :].rearrange("p x a e -> p x (a e)"),
                         e_w2.rearrange("x p a e -> p x (a e)")).then_inc(s_ffw, 16)
            for c in range(NC):
                for j in range(4):
                    g = 4 * c + j
                    sp.wait_ge(s_x1, g + 1)
                    dst = x1_scr.rearrange("(s b) e -> b s e", b=B)[4 * g:4 * g + 4, :, :]
                    sp.dma_start(dst, res[:, c % 2, j, :]).then_inc(s_x1st[c], 16)
            for c in range(NC):
                sp.wait_ge(s_x1st[c], 64)
            for c in range(NC):
                sp.dma_start(x1[:, 4 * c:4 * c + 4, :],
                             x1_scr.rearrange("(g p) e -> p g e", p=P)[:, 4 * c:4 * c + 4, :]).then_inc(s_x1l[c], 16)
            for c in range(NC):
                sp.wait_ge(s_cq, c + 1)
                sp.dma_start(by_row(cq_scr)[:, 4 * c:4 * c + 4, :], qn[:, c % 2, :, :]).then_inc(s_cqst[c], 16)
            for p in range(NP):
                sp.wait_ge(s_cqst[p // 4], 16)
                for n in range(2):
                    sp.dma_start(qs[64 * n:64 * n + 64, p, :].rearrange("t (h d) -> t h d", d=D),
                                 by_token(cq_scr, 2 * p + n)).then_inc(s_cql[p], 16)
            for i in range(NP + 1):
                if i < NP:
                    sp.wait_ge(s_on, i + 1)
                    for n in range(2):
                        sp.dma_start(by_token(o_scr, 2 * i + n),
                                     on[0:64, i % 2, 128 * n:128 * n + 128].rearrange("t (h d) -> t h d", d=D)
                                     ).then_inc(s_ost[i % 2], 16)
                if i >= 1:
                    sp.wait_ge(s_ost[(i - 1) % 2], 32 * ((i - 1) // 2 + 1))
                    sp.dma_start(orow[:, i - 1, :], by_row(o_scr)[:, i - 1, :]).then_inc(s_orl[(i - 1) // 4], 16)
            for c in range(NC):
                sp.wait_ge(s_l3, 33 + 4 * (c + 1))
                sp.dma_start(out.rearrange("s b e -> (s b) e").rearrange("(g p) e -> p g e", p=P)[:, 4 * c:4 * c + 4, :],
                             acc[:, 4 * c:4 * c + 4, :]).then_inc(s_out, 16)
            sp.wait_ge(s_out, 16 * NC)

        @block.tensor
        def _(pe):
            pe.wait_ge(s_const, 64)

            def proj_v(c):
                pe.wait_ge(s_xT[c], 16)
                if c >= 2:
                    pe.wait_ge(s_vn, c - 1)
                for j in range(4):
                    g = 4 * c + j
                    mm = pe.matmul(bank[6 + c % 2][:, E * j:E * j + E], xT[:, P * g:P * g + P], w[:, W_V:W_V + E],
                                   start=True, stop=True)
                mm.then_inc(s_vproj, 1)

            def proj_qk(c):
                if c >= 1:
                    pe.wait_ge(s_qm, c)
                    pe.wait_ge(s_k4, c)
                pe.matmul(bank[0][:, :], w[:, W_Q:W_Q + E], xT[:, 512 * c:512 * c + 512],
                          start=True, stop=True).then_inc(s_qp, 1)
                pe.matmul(bank[1][:, :], w[:, W_K:W_K + E], xT[:, 512 * c:512 * c + 512],
                          start=True, stop=True).then_inc(s_kp, 1)

            def scores(g):
                c, j = g // 4, g % 4
                pe.wait_ge(s_qm, c + 1)
                pe.wait_ge(s_k4, c + 1)
                if g >= 2:
                    pe.wait_ge(s_ex, g - 1)
                for b in range(4):
                    o = 128 * j + 32 * b
                    mm = pe.matmul(bank[2 + g % 2][:, 128 * b:128 * b + 128], qm[:, c % 2, 4 * j + b, :],
                                   k4[:, c % 2, :, o:o + 32], start=(b == 0), stop=False, skip_group_check=True)
                mm.then_inc(s_sc, 1)

            def subtract_max(g):
                pe.wait_ge(s_mb, g + 1)
                pe.matmul(bank[2 + g % 2][:, :], neg_id[:, :], mb[:, g % 2, :].unsqueeze(2).broadcast_to([P, 16, 32]),
                          start=False, stop=True, skip_group_check=True).then_inc(s_sub, 1)

            def weighted(g):
                pe.wait_ge(s_pt, g + 1)
                pe.wait_ge(s_vm[g // 4], 64)
                if g >= 2:
                    pe.wait_ge(s_us, g - 1)
                for b in range(4):
                    mm = pe.matmul(bank[4 + g % 2][:, 128 * b:128 * b + 128], vm[:, 4 * g + b, :],
                                   pt[:, g % 2, 128 * b:128 * b + 128], start=True, stop=True)
                mm.then_inc(s_u, 1)

            def out_proj(g):
                c, j = g // 4, g % 4
                pe.wait_ge(s_us, g + 1)
                if j == 0 and c >= 2:
                    pe.wait_ge(s_res, c - 1)
                u = us[:, g % 2, :].rearrange("p (h t) -> p h t", h=4)
                for h in range(4):
                    mm = pe.matmul(bank[6 + c % 2][:, E * j:E * j + E], u[:, h, :], wom[:, h, :],
                                   start=(h == 0), stop=(h == 3))
                mm.then_inc(s_y, 1)

            def proj_ctx(c):
                i, h = c // 2, c % 2
                if c >= 4:
                    pe.wait_ge(s_ck, c - 3)
                for j in range(4):
                    g = 4 * i + j
                    mm = pe.matmul(bank[2 + c % 4][:, E * j:E * j + E], ctxT[:, P * g:P * g + P],
                                   w[:, (X_K, X_V)[h]:(X_K, X_V)[h] + E], start=True, stop=True)
                mm.then_inc(s_ckp, 1)

            for c in range(NC):
                proj_v(c)
            proj_qk(0)
            pe.wait_ge(s_ctx, 16)
            for c in range(2 * NC):
                proj_ctx(c)
            pe.wait_ge(s_ck, 2 * NC)
            pe.wait_ge(s_vn, NC)
            pe.wait_ge(s_prep, 3)
            for i in range(NG + 4):
                if i < NG:
                    scores(i)
                if 3 <= i < NG + 3:
                    weighted(i - 3)
                if i < NG:
                    subtract_max(i)
                if i % 4 == 1 and i // 4 + 1 < NC:
                    proj_qk(i // 4 + 1)
                if i >= 4:
                    out_proj(i - 4)

            def x1_turned(c):
                pe.wait_ge(s_x1l[c], 16)
                for j in range(4):
                    mm = pe.transpose(bank[c][:, P * j:P * j + P], x1[:, 4 * c + j, :], ident)
                mm.then_inc(s_x1t, 1)

            def proj_cq(c):
                pe.wait_ge(s_x1T, c + 1)
                for j in range(4):
                    mm = pe.matmul(bank[4 + c][:, E * j:E * j + E], x1T[:, c % 2, P * j:P * j + P],
                                   w[:, X_Q:X_Q + E], start=True, stop=True)
                mm.then_inc(s_cqp, 1)

            def kq_turned(p):
                pe.wait_ge(s_ckl[p // 4], 128)
                pe.wait_ge(s_cql[p], 32)
                if p >= 1:
                    pe.wait_ge(s_km, p)
                    pe.wait_ge(s_q4, p)
                pe.transpose(bank[4][:, 0:P], kv[:, 0, p, :], ident)
                pe.transpose(bank[5][:, 0:P], qs[:, p, :], ident).then_inc(s_kqt, 1)

            def scores2(p):
                pe.wait_ge(s_km, p + 1)
                pe.wait_ge(s_q4, p + 1)
                if p >= 2:
                    pe.wait_ge(s_ex2, p - 1)
                for h in range(4):
                    for n in range(2):
                        o = 256 * (h % 2)
                        mm = pe.matmul(bank[2 * (p % 2) + h // 2][64 * n:64 * n + 64, o:o + 256],
                                       km[:, p % 2, h, 64 * n:64 * n + 64], q4[:, p % 2, :, 64 * n:64 * n + 64],
                                       start=(h % 2 == 0), stop=False, skip_group_check=True)
                mm.then_inc(s_sc2, 1)

            def subtract_max2(p):
                pe.wait_ge(s_m2, p + 1)
                for k in range(2):
                    mm = pe.matmul(bank[2 * (p % 2) + k], neg_id[:, :], m2[:, p % 2, :].unsqueeze(1).broadcast_to([P, 8, B]),
                                   start=False, stop=True, skip_group_check=True)
                mm.then_inc(s_sub2, 1)

            def weighted2(p):
                pe.wait_ge(s_pn2, p + 1)
                pe.wait_ge(s_vx, p + 1)
                if p >= 1:
                    pe.wait_ge(s_ot, p)
                for j in range(8):
                    mm = pe.matmul(bank[6][32 * (j % 4):32 * (j % 4) + 32, 128 * (j // 4):128 * (j // 4) + 128],
                                   vx[:, p, j, :, :].rearrange("p a b -> p (a b)"), e2[:, p % 3, 128 * j:128 * j + 128],
                                   start=True, stop=True)
                mm.then_inc(s_pv2, 1)

            def o_by_token(p):
                pe.wait_ge(s_ot, p + 1)
                if p >= 1:
                    pe.wait_ge(s_on, p)
                if p >= 8 and p % 4 == 0:
                    pe.wait_ge(s_res2, p // 4 - 1)
                for j in range(2):
                    mm = pe.transpose(bank[7][0:64, P * j:P * j + P], ot[:, p % 2, 64 * j:64 * j + 64], ident)
                mm.then_inc(s_ont, 1)

            def orow_turned(c, lastp):
                pe.wait_ge(s_on, lastp)
                pe.wait_ge(s_orl[c], 64)
                if c >= 1:
                    pe.wait_ge(s_res2, c)
                for j in range(4):
                    mm = pe.transpose(bank[7][:, P * j:P * j + P], orow[:, 4 * c + j, :], ident)
                mm.then_inc(s_ort, 1)

            def out_proj2(c):
                pe.wait_ge(s_orT, c + 1)
                for j in range(4):
                    mm = pe.matmul(bank[7][:, E * j:E * j + E], x1T[:, c % 2, P * j:P * j + P], w[:, X_O:X_O + E],
                                   start=True, stop=True)
                mm.then_inc(s_y2, 1)

            for c in range(NC):
                x1_turned(c)
                if c >= 1:
                    proj_cq(c - 1)
            proj_cq(NC - 1)
            pe.wait_ge(s_x1T, NC)
            pe.wait_ge(s_cq, NC)
            kq_turned(0)
            for i in range(NP + LAG2):
                if i < NP:
                    scores2(i)
                if 2 <= i < NP + 2:
                    weighted2(i - 2)
                if i + 1 < NP:
                    kq_turned(i + 1)
                if i < NP:
                    subtract_max2(i)
                if 3 <= i < NP + 3:
                    o_by_token(i - 3)
                if i >= 10 and (i - 10) % 4 == 0:
                    c = (i - 10) // 4
                    orow_turned(c, min(i - 2, NP))
                    out_proj2(c)

            for c in range(NC):
                pe.wait_ge(s_x2, 4 * c + 4)
                if c == 0:
                    pe.wait_ge(s_ex2, NP)
                for j in range(4):
                    mm = pe.transpose(bank[c][:, P * j:P * j + P], x2[:, 4 * c + j, :], ident)
                mm.then_inc(s_x2t, 1)
            pe.wait_ge(s_small, 80)
            pe.wait_ge(s_ot, NP)
            for c in range(NC):
                pe.wait_ge(s_x2T, c + 1)
                for j in range(4):
                    g = 4 * c + j
                    mm = pe.matmul(bank[6][:, 16 * g:16 * g + NE], x2T[:, P * g:P * g + P], gw[:, :], start=True, stop=True)
            mm.then_inc(s_lg, 1)
            pe.wait_ge(s_ffw, 32)

            def expert_in(k):
                e, c = k // NC, k % NC
                if k >= 2:
                    pe.wait_ge(s_ge, 2 * (k - 1))
                for a in range(2):
                    pe.matmul(bank[2 * (k % 2) + a], w1[:, e, P * a:P * a + P], x2T[:, 512 * c:512 * c + 512],
                              start=True, stop=True).then_inc(s_h, 1)

            def expert_out(k):
                e, c = k // NC, k % NC
                pe.wait_ge(s_ge, 2 * k + 2)
                if k >= 2:
                    pe.wait_ge(s_yg, k - 1)
                for j in range(4):
                    for a in range(2):
                        mm = pe.matmul(bank[4 + k % 2][:, E * j:E * j + E], hb[:, k % 2, a, P * j:P * j + P], w2[:, e, a, :],
                                       start=(a == 0), stop=(a == 1))
                mm.then_inc(s_ye, 1)

            pe.wait_ge(s_rt, 15)
            pe.wait_ge(s_on, NP)
            for c in range(NC):
                if c >= 1:
                    pe.wait_ge(s_gT, c)
                for j in range(4):
                    mm = pe.transpose(bank[7][0:NE + 1, P * j:P * j + P], gates[:, 4 * c + j, 0:NE + 1], ident)
                mm.then_inc(s_gt, 1)
            for c in range(NC):
                pe.wait_ge(s_gT, c + 1)
                if c == 1:
                    pe.wait_ge(s_gT, NC)
                if c >= 2:
                    pe.wait_ge(s_acc, c - 1)
                for j in range(4):
                    mm = pe.matmul(bank[6 + c % 2][:, E * j:E * j + E], gT[:, 128 * (4 * c + j):128 * (4 * c + j) + 128], b2[:, :],
                                   start=True, stop=True)
                mm.then_inc(s_b2, 1)
            pe.wait_ge(s_x2T, NC)
            expert_in(0)
            for k in range(NX * NC):
                if k + 1 < NX * NC:
                    expert_in(k + 1)
                expert_out(k)

        @block.scalar
        def _(act):
            act.dma_start(cst[:, :], c_pack).then_inc(s_const, 16)
            act.dma_start(bcol[:, :], b_col).then_inc(s_const, 16)
            act.dma_start(b1[:, :, :], e_b1).then_inc(s_small, 16)
            act.dma_start(b2[:, :], e_b2).then_inc(s_small, 16)
            act.dma_start(gw[:, :], g_w).then_inc(s_small, 16)
            act.dma_start(gb[:, :], g_b.partition_broadcast(P)).then_inc(s_small, 16)
            act.dma_start(iota[:, :], iota_row.partition_broadcast(P)).then_inc(s_small, 16)
            act.dma_start(brow[:, :], b_row.partition_broadcast(P)).then_inc(s_brow, 16)

            def k_masked(c):
                act.wait_ge(s_kp, c + 1)
                if c >= 2:
                    act.wait_ge(s_sc, 4 * (c - 1))
                for h in range(4):
                    a = act.activation(k4[:, c % 2, h, :], bank[1][:, :], ACT.Identity, bias=bkm[:, h:h + 1],
                                       scale=m_h4[:, h:h + 1])
                a.then_inc(s_k4, 1)

            def exps(g):
                act.wait_ge(s_sub, g + 1)
                if g >= 3:
                    act.wait_ge(s_pt, g - 2)
                act.activation(ex[:, g % 3, :], bank[2 + g % 2][:, :], ACT.Exp, scale=SCALE1).then_inc(s_ex, 1)

            def u_out(g):
                act.wait_ge(s_u, g + 1)
                if g >= 2:
                    act.wait_ge(s_y, g - 1)
                act.activation(us[:, g % 2, :].rearrange("p (h b s) -> p b h s", h=4, b=4),
                               bank[4 + g % 2][:, :].rearrange("p (b h s) -> p b h s", b=4, h=4), ACT.Identity, bias=bcol[:, 2:3]).then_inc(s_us, 1)

            act.wait_ge(s_const, 64)
            act.mul(neg_id[:, :], ident, -1.0).then_inc(s_prep, 1)
            act.wait_ge(s_prep, 3)
            for c in range(2):
                act.wait_ge(s_vproj, 2 * c + 1)
                act.copy(vn[:, 8 * c:8 * c + 4, :].rearrange("p g e -> p (g e)"), bank[6][:, :]).then_inc(s_vn, 1)
                act.wait_ge(s_vproj, 2 * c + 2)
                act.copy(vn[:, 8 * c + 4:8 * c + 8, :].rearrange("p g e -> p (g e)"), bank[7][:, :]).then_inc(s_vn, 1)
            k_masked(0)
            for i in range(NG + 3):
                if i < NG:
                    exps(i)
                if i % 4 == 1 and i // 4 + 1 < NC:
                    k_masked(i // 4 + 1)
                if i >= 3:
                    u_out(i - 3)

            def x1T_out(c):
                act.wait_ge(s_x1t, c + 1)
                if c >= 2:
                    act.wait_ge(s_cqp, c - 1)
                act.copy(x1T[:, c % 2, :], bank[c]).then_inc(s_x1T, 1)

            def k_masked2(p):
                act.wait_ge(s_kqt, p + 1)
                if p >= 2:
                    act.wait_ge(s_sc2, p - 1)
                for h in range(4):
                    a = act.activation(km[:, p % 2, h, :], bank[4][:, 0:P], ACT.Copy, scale=m_hg[:, h:h + 1])
                a.then_inc(s_km, 1)

            def exps2(p):
                act.wait_ge(s_sub2, p + 1)
                if p >= 3:
                    act.wait_ge(s_pv2, p - 2)
                act.activation(e2[:, p % 3, :], psum[:, 1024 * (p % 2):1024 * (p % 2) + 1024], ACT.Exp,
                               scale=SCALE2).then_inc(s_ex2, 1)

            def ot_first(p):
                act.wait_ge(s_pv2, p + 1)
                if p >= 2:
                    act.wait_ge(s_ot, p - 1)
                act.activation(ota[:, p % 2, :].rearrange("p (j t) -> p j t", j=2),
                               bank[6][:, 0:256].rearrange("p (j h t) -> p j h t", j=2, h=2)[:, :, 0, :],
                               ACT.Copy, scale=m_h2[:, 0:1]).then_inc(s_ota, 1)

            def on_out(p):
                act.wait_ge(s_ont, p + 1)
                if p >= 2:
                    act.wait_ge(s_ost[p % 2], 32 * (p // 2))
                act.copy(on[0:64, p % 2, :].rearrange("t (n j c) -> t j n c", n=2, j=8),
                         bank[7][0:64, 0:256].rearrange("t (j n c) -> t j n c", n=2, j=8)).then_inc(s_on, 1)

            def orT_out(c):
                act.wait_ge(s_ort, c + 1)
                if c >= 2:
                    act.wait_ge(s_y2, c - 1)
                act.copy(x1T[:, c % 2, :], bank[7]).then_inc(s_orT, 1)

            for c in range(NC):
                x1T_out(c)
            k_masked2(0)
            for i in range(NP + LAG2):
                if 2 <= i < NP + 2:
                    ot_first(i - 2)
                if i + 1 < NP:
                    k_masked2(i + 1)
                if i < NP:
                    exps2(i)
                if 3 <= i < NP + 3:
                    on_out(i - 3)
                if i >= 10 and (i - 10) % 4 == 0:
                    orT_out((i - 10) // 4)

            for c in range(NC):
                act.wait_ge(s_x2t, c + 1)
                act.copy(x2T[:, 512 * c:512 * c + 512], bank[c]).then_inc(s_x2T, 1)
            act.wait_ge(s_rt, 3)
            act.activation(lg[:, :, :], lg[:, :, :], ACT.Exp).then_inc(s_rt, 1)
            for k in range(NX * NC):
                for a in range(2):
                    act.wait_ge(s_h, 2 * k + a + 1)
                    if k >= 2:
                        act.wait_ge(s_ye, k - 1)
                    act.activation(hb[:, k % 2, a, :], bank[2 * (k % 2) + a], ACT.Gelu, bias=b1[:, k // NC, a:a + 1]).then_inc(s_ge, 1)

        @block.vector
        def _(dve):
            dve.memset(vm[:, 0:B // 2, :].rearrange("p b e -> p (b e)"), 0.0).then_inc(s_zero_d, 1)
            dve.wait_ge(s_const, 64)
            dve.tensor_scalar(bkm[:, :], m_h4, bcol[:, 1:2], None, ALU.mult).then_inc(s_prep, 1)
            for h in range(4):
                ins = dve.tensor_scalar(wom[:, h, :], w[:, W_O:W_O + E], m_h4[:, h:h + 1], None, ALU.mult)
            ins.then_inc(s_prep, 1)

            def ctx_out(c):
                i, h = c // 2, c % 2
                dve.wait_ge(s_ckp, c + 1)
                r = (R_XK, R_XV)[h]
                dve.tensor_tensor(kv[:, h, 4 * i:4 * i + 4, :],
                                  bank[2 + c % 4].rearrange("p (g e) -> p g e", e=E),
                                  brow[:, r:r + E].unsqueeze(1).broadcast_to([P, 4, E]), ALU.add).then_inc(s_ck, 1)

            def q_masked(c):
                dve.wait_ge(s_qp, c + 1)
                if c >= 2:
                    dve.wait_ge(s_sc, 4 * (c - 1))
                for h in range(4):
                    ins = dve.tensor_scalar(qm[:, c % 2, :, 32 * h:32 * h + 32],
                                            bank[0][:, :].rearrange("p (b s) -> p b s", s=S),
                                            bcol[:, 0:1], m_hg[:, h:h + 1], ALU.add, ALU.mult)
                ins.then_inc(s_qm, 1)

            def row_max(g):
                dve.wait_ge(s_sc, g + 1)
                if g >= 2:
                    dve.wait_ge(s_sub, g - 1)
                with nc.allow_low_precision(reason="any shift near the maximum serves the softmax"):
                    dve.tensor_reduce(mb[:, g % 2, :], bank[2 + g % 2][:, :].rearrange("p (a t) -> p a t", t=S),
                                      AX_X, ALU.max).then_inc(s_mb, 1)

            def row_sum(g):
                dve.wait_ge(s_ex, g + 1)
                dve.tensor_reduce(ssum[:, g % 2, :], ex[:, g % 3, :].rearrange("p (a t) -> p a t", t=S),
                                  AX_X, ALU.add).then_inc(s_sum, 1)
                dve.wait_ge(s_sum, g + 1)
                if g >= 2:
                    dve.wait_ge(s_pn, g - 1)
                dve.reciprocal(rs[:, g % 2, :], ssum[:, g % 2, :]).then_inc(s_rs, 1)

            def turn(g):
                dve.wait_ge(s_pn, g + 1)
                if g >= 2:
                    dve.wait_ge(s_u, g - 1)
                dve.transpose(pt[:, g % 2, :], ex[:, g % 3, :]).then_inc(s_pt, 1)

            def ln1_stats(c):
                dve.wait_ge(s_y, 4 * c + 4)
                if c >= 2:
                    dve.wait_ge(s_x1, 4 * (c - 1))
                    dve.wait_ge(s_x1st[c - 2], 64)
                dve.tensor_tensor(res[:, c % 2, :, :].rearrange("p g e -> p (g e)"), bank[6 + c % 2][:, :],
                                  xn[:, 4 * c:4 * c + 4, :].rearrange("p g e -> p (g e)"), ALU.add).then_inc(s_res, 1)
                dve.wait_ge(s_res, c + 1)
                for j in range(4):
                    ins = dve.bn_stats(bst[:, c % 2, j, :], res[:, c % 2, j, :])
                ins.then_inc(s_bst, 1)
                dve.wait_ge(s_bst, c + 1)
                for j in range(4):
                    ins = dve.bn_aggr(mv[:, c % 2, j, :], bst[:, c % 2, j, :])
                ins.then_inc(s_mv, 1)

            def ln1_apply(c):
                dve.wait_ge(s_rstd, c + 1)
                for j in range(4):
                    dve.tensor_scalar(res[:, c % 2, j, :], res[:, c % 2, j, :], mv[:, c % 2, j, 0:1],
                                      rstd[:, c % 2, j:j + 1], ALU.subtract, ALU.mult).then_inc(s_x1, 1)

            q_masked(0)
            dve.wait_ge(s_brow, 16)
            for c in range(2 * NC):
                ctx_out(c)
            for i in range(NG + 6):
                if i < NG:
                    row_max(i)
                if 2 <= i < NG + 2:
                    turn(i - 2)
                if 1 <= i < NG + 1:
                    row_sum(i - 1)
                if i % 4 == 1 and i // 4 + 1 < NC:
                    q_masked(i // 4 + 1)
                if i >= 8 and i % 4 == 0:
                    ln1_stats(i // 4 - 2)
                if i >= 9 and i % 4 == 1:
                    ln1_apply(i // 4 - 2)

            def cq_out(c):
                dve.wait_ge(s_cqp, c + 1)
                if c >= 2:
                    dve.wait_ge(s_cqst[c - 2], 16)
                dve.tensor_tensor(qn[:, c % 2, :, :], bank[4 + c].rearrange("p (g e) -> p g e", e=E),
                                  brow[:, R_XQ:R_XQ + E].unsqueeze(1).broadcast_to([P, 4, E]), ALU.add).then_inc(s_cq, 1)

            def q_masked2(p):
                dve.wait_ge(s_kqt, p + 1)
                if p >= 2:
                    dve.wait_ge(s_sc2, p - 1)
                dve.tensor_tensor(q4[:, p % 2, :, :], bank[5][:, 0:P].unsqueeze(1).broadcast_to([P, 4, P]),
                                  m_h4.unsqueeze(2).broadcast_to([P, 4, P]), ALU.mult).then_inc(s_q4, 1)

            def head_max(p):
                dve.wait_ge(s_sc2, p + 1)
                if p >= 2:
                    dve.wait_ge(s_sub2, p - 1)
                with nc.allow_low_precision(reason="any shift near the maximum serves the softmax"):
                    dve.tensor_reduce(m2[:, p % 2, :],
                                      psum[:, 1024 * (p % 2):1024 * (p % 2) + 1024].rearrange("p (h t) -> p t h", t=B),
                                      AX_X, ALU.max).then_inc(s_m2, 1)

            def head_sum(p):
                dve.wait_ge(s_ex2, p + 1)
                dve.tensor_reduce(sum2[:, p % 2, :], e2[:, p % 3, :].rearrange("p (h t) -> p t h", t=B),
                                  AX_X, ALU.add).then_inc(s_sum2, 1)
                dve.wait_ge(s_sum2, p + 1)
                if p >= 2:
                    dve.wait_ge(s_pn2, p - 1)
                dve.reciprocal(r2[:, p % 2, :], sum2[:, p % 2, :]).then_inc(s_r2, 1)

            def ot_second(p):
                dve.wait_ge(s_ota, p + 1)
                if p >= 2:
                    dve.wait_ge(s_ont, p - 1)
                dve.scalar_tensor_tensor(out=ot[:, p % 2, :].rearrange("p (j t) -> p j t", j=2),
                                         in0=bank[6][:, 0:256].rearrange("p (j h t) -> p j h t", j=2, h=2)[:, :, 1, :],
                                         scalar=m_h2[:, 1:2], in1=ota[:, p % 2, :].rearrange("p (j t) -> p j t", j=2),
                                         op0=ALU.mult, op1=ALU.add).then_inc(s_ot, 1)

            def ln2_stats(c):
                dve.wait_ge(s_y2, c + 1)
                dve.wait_ge(s_xb2, c + 1)
                if c >= 2:
                    dve.wait_ge(s_x2, 4 * (c - 1))
                dve.tensor_tensor(res2[:, c % 2, :, :].rearrange("p g e -> p (g e)"), bank[7],
                                  x1[:, 4 * c:4 * c + 4, :].rearrange("p g e -> p (g e)"), ALU.add).then_inc(s_res2, 1)
                dve.wait_ge(s_res2, c + 1)
                for j in range(4):
                    ins = dve.bn_stats(bst2[:, c % 2, j, :], res2[:, c % 2, j, :])
                ins.then_inc(s_bst2, 1)
                dve.wait_ge(s_bst2, c + 1)
                for j in range(4):
                    ins = dve.bn_aggr(mv2[:, c % 2, j, :], bst2[:, c % 2, j, :])
                ins.then_inc(s_mv2, 1)

            def ln2_apply(c):
                dve.wait_ge(s_rstd2, c + 1)
                for j in range(4):
                    dve.tensor_scalar(x2[:, 4 * c + j, :], res2[:, c % 2, j, :], mv2[:, c % 2, j, 0:1],
                                      rstd2[:, c % 2, j:j + 1], ALU.subtract, ALU.mult).then_inc(s_x2, 1)

            for c in range(NC):
                cq_out(c)
            q_masked2(0)
            for i in range(NP + LAG2 + 1):
                if i < NP:
                    head_max(i)
                if 2 <= i < NP + 2:
                    ot_second(i - 2)
                if i + 1 < NP:
                    q_masked2(i + 1)
                if 1 <= i < NP + 1:
                    head_sum(i - 1)
                if i >= 10 and (i - 10) % 4 == 0:
                    ln2_stats((i - 10) // 4)
                if i >= 11 and (i - 11) % 4 == 0:
                    ln2_apply((i - 11) // 4)

            step = [0]

            def routed(ins):
                step[0] += 1
                ins.then_inc(s_rt, 1)
                dve.wait_ge(s_rt, step[0])

            dve.wait_ge(s_lg, 1)
            dve.wait_ge(s_small, 80)
            lgp = bank[6][:, 0:256].rearrange("p (g e) -> p g e", e=16)[:, :, 0:NE]
            routed(dve.tensor_tensor(lg[:, :, :], lgp, gb[:, :].unsqueeze(1).broadcast_to([P, NG, NE]), ALU.add))
            routed(dve.tensor_reduce(lmax[:, :], lg[:, :, :], AX_X, ALU.max))
            routed(dve.tensor_tensor(lg[:, :, :], lg[:, :, :], lmax[:, :].unsqueeze(2).broadcast_to([P, NG, NE]), ALU.subtract))
            step[0] = 4
            dve.wait_ge(s_rt, 4)
            routed(dve.tensor_reduce(lsum[:, :], lg[:, :, :], AX_X, ALU.add))
            routed(dve.reciprocal(lsum[:, :], lsum[:, :]))
            routed(dve.tensor_tensor(lg[:, :, :], lg[:, :, :], lsum[:, :].unsqueeze(2).broadcast_to([P, NG, NE]), ALU.mult))
            for g in range(NG):
                ins = dve.max(top[:, g, :], lg[:, g, :])
            routed(ins)
            for g in range(NG):
                ins = dve.max_index(topi[:, g, :], top[:, g, :], lg[:, g, :])
            routed(ins)
            routed(dve.tensor_copy(topf[:, :, :], topi[:, :, :]))
            for k in range(TOPK):
                ins = dve.tensor_tensor(oh[:, :, k, :], iota[:, :].unsqueeze(1).broadcast_to([P, NG, NE]),
                                        topf[:, :, k].unsqueeze(2).broadcast_to([P, NG, NE]), ALU.is_equal)
            routed(ins)
            for k in range(TOPK):
                ins = dve.tensor_tensor(oh[:, :, k, :], oh[:, :, k, :],
                                        top[:, :, k].unsqueeze(2).broadcast_to([P, NG, NE]), ALU.mult)
            routed(ins)
            routed(dve.tensor_tensor(gates[:, :, 0:NE], oh[:, :, 0, :], oh[:, :, 1, :], ALU.add))
            routed(dve.tensor_tensor(gates[:, :, 0:NE], gates[:, :, 0:NE], oh[:, :, 2, :], ALU.add))
            dve.memset(gates[:, :, NE:NX], 1.0).then_inc(s_rt, 1)
            for c in range(NC):
                dve.wait_ge(s_gt, c + 1)
                dve.tensor_copy(gT[:, 512 * c:512 * c + 512], bank[7][0:NE + 1, :]).then_inc(s_gT, 1)
            for c in range(NC):
                dve.wait_ge(s_b2, c + 1)
                dve.scalar_tensor_tensor(out=acc[:, 4 * c:4 * c + 4, :].rearrange("p g e -> p (g e)"),
                                         in0=x2[:, 4 * c:4 * c + 4, :].rearrange("p g e -> p (g e)"), scalar=2.0,
                                         in1=bank[6 + c % 2], op0=ALU.mult, op1=ALU.add).then_inc(s_acc, 1)
            for k in range(NX * NC):
                e, c = k // NC, k % NC
                dve.wait_ge(s_ye, k + 1)
                if k >= 2:
                    dve.wait_ge(s_acc, NC + k - 1)
                dve.tensor_tensor(yg[:, k % 2, :].rearrange("p (g e) -> p g e", e=E), bank[4 + k % 2].rearrange("p (g e) -> p g e", e=E),
                                  gates[:, 4 * c:4 * c + 4, e].unsqueeze(2).broadcast_to([P, 4, E]), ALU.mult).then_inc(s_yg, 1)
                dve.wait_ge(s_yg, k + 1)
                dve.wait_ge(s_acc, max(NC, NC + k - 3))
                dve.tensor_tensor(acc[:, 4 * c:4 * c + 4, :].rearrange("p g e -> p (g e)"),
                                  acc[:, 4 * c:4 * c + 4, :].rearrange("p g e -> p (g e)"), yg[:, k % 2, :], ALU.add).then_inc(s_acc, 1)
            dve.wait_ge(s_acc, NC + NX * NC)
            for g in range(NG):
                dve.bn_stats(bst3[:, g, :], acc[:, g, :]).then_inc(s_l3, 1)
            dve.wait_ge(s_l3, NG)
            for g in range(NG):
                dve.bn_aggr(mv3[:, g, :], bst3[:, g, :]).then_inc(s_l3, 1)
            dve.wait_ge(s_l3, 33)
            for g in range(NG):
                dve.tensor_scalar(acc[:, g, :], acc[:, g, :], mv3[:, g, 0:1], rstd3[:, g:g + 1],
                                  ALU.subtract, ALU.mult).then_inc(s_l3, 1)

        @block.gpsimd
        def _(pool):
            pool.memset(vm[:, B // 2:B, :].rearrange("p b e -> p (b e)"), 0.0).then_inc(s_zero_p, 1)
            pool.memset(half[:, :], -0.5)
            pool.wait_ge(s_xn, 16)
            pool.wait_ge(s_brow, 16)
            pool.tensor_tensor(xn[:, :, :], xn[:, :, :],
                               brow[:, R_BO:R_BO + E].unsqueeze(1).broadcast_to([P, NG, E]), ALU.add).then_inc(s_xb, 1)

            def normalise(g):
                pool.wait_ge(s_rs, g + 1)
                pool.tensor_tensor(ex[:, g % 3, :].rearrange("p (a t) -> p a t", t=S),
                                   ex[:, g % 3, :].rearrange("p (a t) -> p a t", t=S),
                                   rs[:, g % 2, :].unsqueeze(2).broadcast_to([P, 16, S]), ALU.mult).then_inc(s_pn, 1)

            def rsqrt1(c):
                pool.wait_ge(s_mv, c + 1)
                pool.tensor_scalar(rstd[:, c % 2, :], mv[:, c % 2, :, 1], EPS, None, ALU.add).then_inc(s_ve, 1)
                pool.wait_ge(s_ve, c + 1)
                pool.tensor_tensor(rstd[:, c % 2, :], rstd[:, c % 2, :], half[:, :], ALU.pow).then_inc(s_rstd, 1)

            def v_apart(p):
                pool.wait_ge(s_cvl[p // 4], 128)
                pool.tensor_tensor(vx[:, p, :, :, :],
                                   kv[:, 1, p, :].rearrange("p (j c) -> p j c", j=8).unsqueeze(2).broadcast_to([P, 8, 2, 16]),
                                   m_n2.unsqueeze(1).unsqueeze(3).broadcast_to([P, 8, 2, 16]), ALU.mult).then_inc(s_vx, 1)

            def normalise2(p):
                pool.wait_ge(s_r2, p + 1)
                pool.tensor_tensor(e2[:, p % 3, :].rearrange("p (h t) -> p h t", t=B),
                                   e2[:, p % 3, :].rearrange("p (h t) -> p h t", t=B),
                                   r2[:, p % 2, :].unsqueeze(1).broadcast_to([P, 16, B]), ALU.mult).then_inc(s_pn2, 1)

            def x1_biased(c):
                pool.wait_ge(s_x1t, c + 1)
                pool.tensor_tensor(x1[:, 4 * c:4 * c + 4, :], x1[:, 4 * c:4 * c + 4, :],
                                   brow[:, R_XO:R_XO + E].unsqueeze(1).broadcast_to([P, 4, E]), ALU.add).then_inc(s_xb2, 1)

            def rsqrt2(c):
                pool.wait_ge(s_mv2, c + 1)
                pool.tensor_scalar(rstd2[:, c % 2, :], mv2[:, c % 2, :, 1], EPS, None, ALU.add).then_inc(s_ve2, 1)
                pool.wait_ge(s_ve2, c + 1)
                pool.tensor_tensor(rstd2[:, c % 2, :], rstd2[:, c % 2, :], half[:, :], ALU.pow).then_inc(s_rstd2, 1)

            for i in range(1, NG + 4):
                if i <= NG:
                    normalise(i - 1)
                if i >= 8 and i % 4 == 0:
                    rsqrt1(i // 4 - 2)
                if i >= 6:
                    v_apart(i - 6)
            rsqrt1(NC - 1)
            for p in range(NG - 2, NP):
                v_apart(p)
            for c in range(NC):
                x1_biased(c)
            for i in range(1, NP + LAG2 + 1):
                if i <= NP:
                    normalise2(i - 1)
                if i >= 10 and (i - 10) % 4 == 0:
                    rsqrt2((i - 10) // 4)
            pool.memset(half3[:, :], -0.5).then_inc(s_mv3, 1)
            pool.wait_ge(s_l3, 32)
            pool.tensor_scalar(rstd3[:, :], mv3[:, :, 1], EPS, None, ALU.add).then_inc(s_mv3, 1)
            pool.wait_ge(s_mv3, 2)
            pool.tensor_tensor(rstd3[:, :], rstd3[:, :], half3[:, :], ALU.pow).then_inc(s_l3, 1)


def layout(inputs):
    import numpy as np

    def f(name):
        return np.asarray(inputs[name])

    x, c = f("x"), f("ctx_1024")
    p = np.arange(P)
    w_in = f("L0_attn_in_proj_w").T
    a = {}
    a["x_t"] = x.transpose(2, 1, 0).reshape(E, T)
    a["x_n"] = x.transpose(1, 0, 2).reshape(NG, P, E).transpose(1, 0, 2)
    a["ctx_t"] = c.reshape(T, E).T
    a["w_pack"] = np.concatenate([w_in, f("L0_attn_out_proj_w").T, f("L0_xattn_Wq"), f("L0_xattn_Wk"),
                                  f("L0_xattn_Wv"), f("L0_xattn_Wo")], axis=1)
    a["c_pack"] = np.concatenate(
        [np.eye(P)] + [(p // 32 == g)[:, None] for g in range(4)] + [((p // 8) % 4 == h)[:, None] for h in range(4)]
        + [(p // 64 == n)[:, None] for n in range(2)] + [((p // 8) % 2 == h)[:, None] for h in range(2)],
        axis=1).astype(np.float32)
    bi = f("L0_attn_in_proj_b")
    a["b_col"] = np.stack([bi[0:E], bi[E:2 * E], bi[2 * E:3 * E], bi[0:E]], axis=1)
    a["b_row"] = np.concatenate([f("L0_attn_out_proj_b"), f("L0_xattn_bq"), f("L0_xattn_bk"), f("L0_xattn_bv"),
                                 f("L0_xattn_bo")])
    w1 = np.concatenate([f("L0_ffn_rW1"), f("L0_ffn_sW1").reshape(E, 2, FE).transpose(1, 0, 2)])
    w2 = np.concatenate([f("L0_ffn_rW2"), f("L0_ffn_sW2").reshape(2, FE, E)])
    a["e_w1"] = w1
    a["e_w2"] = w2.reshape(NX, 2, P, E).transpose(0, 2, 1, 3)
    a["e_b1"] = np.concatenate([f("L0_ffn_rb1"), f("L0_ffn_sb1").reshape(2, FE)]).reshape(NX, 2, P).transpose(2, 0, 1)
    a["e_b2"] = np.concatenate([f("L0_ffn_rb2"), f("L0_ffn_sb2")])
    a["g_w"] = f("L0_ffn_gW")
    a["g_b"] = f("L0_ffn_gb")
    a["iota_row"] = np.arange(NE, dtype=np.float32)
    return {k: np.ascontiguousarray(v) for k, v in a.items()}


def kernel(**inputs):
    import numpy as np
    import concourse.bacc as bacc
    from concourse.bass_utils import run_bass_kernel_spmd

    nc = bacc.Bacc("TRN2", target_bir_lowering=False, num_devices=1)
    arrays = layout(inputs)
    args = [nc.dram_tensor(n, a.shape, mybir.dt.from_np(a.dtype), kind="ExternalInput").ap()
            for n, a in arrays.items()]
    out = nc.dram_tensor("out", (S, B, E), F32, kind="ExternalOutput").ap()
    build(nc, *args, out)
    r = run_bass_kernel_spmd(nc, [arrays], core_ids=[0])
    return r.results[0]["out"]
```

```python
from contextlib import ExitStack

import concourse.bass as bass
from concourse import mybir

F32 = mybir.dt.float32
I32 = mybir.dt.int32
BF16 = mybir.dt.bfloat16
ALU = mybir.AluOpType
ACT = mybir.ActivationFunctionType
AX_X = mybir.AxisListType.X

P = 128
E = 128
S, B = 32, 64
T = S * B
NG = T // P
NC = 4
D = 8
NP = NG
STEPS1 = NG + 8
STEPS2 = NP + 3
TURN = (11, 15, 17)
EPS = 1e-5

W_Q, W_K, W_V, W_O, X_Q, X_K, X_V, X_O = (i * E for i in range(8))
C_ID = 0
C_HG = 128
C_H4 = 132
C_N2 = 136
C_H2 = 138
C_TRI = 140
C_END = C_TRI + P
R_BO, R_XQ, R_XK, R_XV, R_XO = (i * E for i in range(5))
R_END = 5 * E

NE = 15
FE = 256
NX = NE + 2
TOPK = 3
EW = FE + 2 * E + 2
ROOM = T + P
NT = TOPK * T // P + NE
NT += -NT % 4
NB = 8
XW = E + 2
ROWS = NE * ROOM + P
K_IOTA, K_BASE, K_T, K_TP, K_J = 0, NE, 2 * NE, 2 * NE + NT, 2 * NE + 2 * NT
K_L = K_J + T // P
K_END = K_L + NE * NE


def build(nc, x_t, x_n, ctx_t, w_pack, c_pack, b_col, b_row, e_w, e_b2, g_w, g_b, k_row, dst_rows, out):
    v_scr = nc.dram_tensor("v_scr", [T, E], F32).ap()
    x1_scr = nc.dram_tensor("x1_scr", [T, E], F32).ap()
    ck_scr = nc.dram_tensor("ck_scr", [T * E], F32).ap()
    cv_scr = nc.dram_tensor("cv_scr", [T * E], F32).ap()
    cq_scr = nc.dram_tensor("cq_scr", [T * E], F32).ap()
    o_scr = nc.dram_tensor("o_scr", [T * E], F32).ap()
    x_srt = nc.dram_tensor("x_srt", [ROWS, XW], F32).ap()
    y_tok = nc.dram_tensor("y_tok", [NT * P + TOPK * T, E], F32).ap()

    with ExitStack() as ctx:
        def sb(name, shape, dt=F32):
            return ctx.enter_context(nc.sbuf_tensor(name, shape, dt))

        def sem(name):
            return ctx.enter_context(nc.semaphore(name))

        psum = ctx.enter_context(nc.psum_tensor("psum", [P, 8 * 512], F32))
        bank = [psum[:, 512 * i:512 * i + 512] for i in range(8)]

        w = sb("w", [P, 8 * E])
        cst = sb("cst", [P, C_END])
        bcol = sb("bcol", [P, 4])
        brow = sb("brow", [P, R_END])
        id_h2 = sb("id_h2", [P, 2, P])
        neg_id = sb("neg_id", [P, P], BF16)
        bkm = sb("bkm", [P, 4])
        bqm = sb("bqm", [P, 4])
        wom = sb("wom", [P, 4, E])
        half = sb("half", [P, 4])

        xT = sb("xT", [P, T])
        xn = sb("xn", [P, NG, E])
        ctxT = sb("ctxT", [P, T])
        vn = sb("vn", [P, NG, E])
        vm = sb("vm", [P, B, E])
        qm = sb("qm", [P, 2, 16, 128])
        k4 = sb("k4", [P, 2, 4, 512])
        mb = sb("mb", [P, 2, 16], BF16)
        ex = sb("ex", [P, 3, 512])
        ssum = sb("ssum", [P, 2, 16])
        rs = sb("rs", [P, 2, 16])
        pt = sb("pt", [P, 2, 512])
        us = sb("us", [P, 2, 512])
        res = sb("res", [P, 2, 4, E])
        bst = sb("bst", [P, 2, 4, 6])
        mv = sb("mv", [P, 2, 4, 2])
        rstd = sb("rstd", [P, 2, 4])

        kv = sb("kv", [P, 2, NP, E])
        vx = sb("vx", [P, NP, 8, 2, 16])
        m2 = sb("m2", [P, 2, B], BF16)
        sum2 = sb("sum2", [P, 2, B])
        r2 = sb("r2", [P, 2, B])
        res2 = sb("res2", [P, 2, 4, E])
        bst2 = sb("bst2", [P, 2, 4, 6])
        mv2 = sb("mv2", [P, 2, 4, 2])
        rstd2 = sb("rstd2", [P, 2, 4])
        ew = sb("ew", [P, NX, EW])
        b2 = sb("b2", [NE + 1, E])
        gw = sb("gw", [P, NE])
        gb = sb("gb", [P, NE])
        kr = sb("kr", [P, K_END])
        dst = sb("dst", [P, NG * TOPK + NT], I32)
        tri = sb("tri", [P, P], BF16)
        ones = sb("ones", [P, P], BF16)
        pad = sb("pad", [P, XW])
        lg = sb("lg", [P, 4, NE])
        msk = sb("msk", [P, NG, NE], BF16)
        mskf = sb("mskf", [P, NE])
        carry = sb("carry", [P, NC + 1, NE], BF16)
        rank = sb("rank", [P, 4, NE])
        sel = sb("sel", [P, 4 * TOPK, NE])
        idx = sb("idx", [P, NT], I32)
        slot = sb("slot", [P, NG * TOPK], mybir.dt.uint32)
        cnt = sb("cnt", [P, NE])
        ends = sb("ends", [P, NE], I32)
        nt = sb("nt", [P, NE])
        te = sb("te", [P, NT])
        tprev = sb("tprev", [P, NT])
        t_expert = sb("t_expert", [1, NT], I32)
        t_row = sb("t_row", [1, NT], I32)
        lmax = sb("lmax", [P, NG])
        lsum = sb("lsum", [P, NG])
        top = sb("top", [P, 4, 8])
        topi = sb("topi", [P, 4, 8], mybir.dt.uint32)
        oh = sb("oh", [P, 4, TOPK, NE])
        gates = sb("gates", [P, NG, NE + 1])
        mv3 = sb("mv3", [P, NG, 2])
        bst3 = sb("bst3", [P, NG, 6])
        rstd3 = sb("rstd3", [P, NG])
        x1 = xT[:, :].rearrange("p (g e) -> p g e", e=E)
        qs = vn
        qm_room = qm[:, :, :, :].rearrange("p a b c -> p (a b c)")
        k4_room = k4[:, :, :, :].rearrange("p a b c -> p (a b c)")
        vm_room = vm[:, :, :].rearrange("p b e -> p (b e)")
        orT = qm_room[:, 0:1024].rearrange("p (a b) -> p a b", a=2)
        x1T = xn[:, :, :].rearrange("p (c g) e -> p c (g e)", c=NC)
        km = qm_room[:, 1024:2048].rearrange("p (a h b) -> p a h b", a=2, h=4)
        q4 = qm_room[:, 2048:3072].rearrange("p (a h b) -> p a h b", a=2, h=4)
        ut = qm_room[:, 3072:3584].rearrange("p (a b) -> p a b", a=2)
        on = qm_room[:, 3584:4096].rearrange("p (a b) -> p a b", a=2)
        e2 = k4_room[:, 0:3072].rearrange("p (a b) -> p a b", a=3)
        orow = vm_room[:, NG * TOPK * XW:NG * TOPK * XW + 8 * E].rearrange("p (g e) -> p g e", e=E)
        pay = vm_room[:, 0:NG * TOPK * XW].rearrange("p (g k e) -> p g k e", g=NG, k=TOPK)
        x2 = pay[:, :, 0, 0:E]
        qn = res2
        acc = xT[:, :].rearrange("p (g e) -> p g e", e=E)
        kv_room = kv[:, :, :, :].rearrange("p h g e -> p (h g e)")
        vx_room = vx[:, :, :, :, :].rearrange("p g a b c -> p (g a b c)")
        routed_y = [kv_room[:, 0:2048].rearrange("p (g e) -> p g e", e=E),
                    kv_room[:, 2048:4096].rearrange("p (g e) -> p g e", e=E),
                    vx_room[:, 0:2048].rearrange("p (g e) -> p g e", e=E)]
        x2T = ctxT
        gT = kv_room[0:NE + 1, 3072:4096].rearrange("p (a b) -> p a b", a=2)
        xn_room = xn[:, :, :].rearrange("p g e -> p (g e)")
        hb = xn_room[:, 0:2048].rearrange("p (a b c) -> p a b c", a=2, b=2)
        big = k4_room[0:1, 3072:3072 + NT * NE]
        stage = kv_room[:, 0:5 * EW].rearrange("p (a b) -> p a b", a=5)
        xin = k4_room[:, 0:NB * XW].rearrange("p (a b) -> p a b", a=NB)
        o = NB * XW
        xinT = k4_room[:, o:o + 2 * P].rearrange("p (a b) -> p a b", a=2)
        o += 2 * P
        hl = k4_room[:, o:o + 4 * P].rearrange("p (a f b) -> p a f b", a=2, f=2)
        o += 4 * P
        yl = k4_room[:, o:o + NB * E].rearrange("p (a b) -> p a b", a=NB)
        ident = cst[:, C_ID:C_ID + P]
        m_n2 = cst[:, C_N2:C_N2 + 2]
        m_h2 = cst[:, C_H2:C_H2 + 2]
        m_hg = cst[:, C_HG:C_HG + 4]
        m_h4 = cst[:, C_H4:C_H4 + 4]

        s_const = sem("s_const")
        s_xT = [sem(f"s_xT{c}") for c in range(NC)]
        s_xn = sem("s_xn")
        s_prep = sem("s_prep")
        s_xb = sem("s_xb")
        s_brow = sem("s_brow")
        s_zero_d = sem("s_zero_d")
        s_zero_p = sem("s_zero_p")
        s_vproj = sem("s_vproj")
        s_vn = sem("s_vn")
        s_vst = [sem(f"s_vst{c}") for c in range(NC)]
        s_vm = [sem(f"s_vm{c}") for c in range(NC)]
        s_qp = sem("s_qp")
        s_kp = sem("s_kp")
        s_qm = sem("s_qm")
        s_k4 = sem("s_k4")
        s_sc = sem("s_sc")
        s_mb = sem("s_mb")
        s_sub = sem("s_sub")
        s_ex = sem("s_ex")
        s_recip = sem("s_recip")
        s_pn = sem("s_pn")
        s_pt = sem("s_pt")
        s_u = sem("s_u")
        s_us = sem("s_us")
        s_y = sem("s_y")
        s_ln1 = sem("s_ln1")
        s_rstd = sem("s_rstd")
        s_x1 = sem("s_x1")
        s_x1st = [sem(f"s_x1st{c}") for c in range(2)]

        s_ffw = sem("s_ffw")
        s_small = sem("s_small")
        s_rtc = sem("s_rtc")
        s_x2t = sem("s_x2t")
        s_x2T = sem("s_x2T")
        s_lg = sem("s_lg")
        s_lgs = sem("s_lgs")
        s_lge = sem("s_lge")
        s_rt = sem("s_rt")
        s_msk = sem("s_msk")
        s_pre = sem("s_pre")
        s_slot = sem("s_slot")
        s_pay = sem("s_pay")
        s_scat = sem("s_scat")
        s_cnt = sem("s_cnt")
        s_ends = sem("s_ends")
        s_fill = sem("s_fill")
        s_tab = sem("s_tab")
        s_xin = [sem(f"s_xin{k}") for k in range(NB)]
        s_xit = sem("s_xit")
        s_xiT = sem("s_xiT")
        s_stage = sem("s_stage")
        s_hl = sem("s_hl")
        s_gl = sem("s_gl")
        s_yo = sem("s_yo")
        s_idx = sem("s_idx")
        s_yl = sem("s_yl")
        s_ysc = [sem(f"s_ysc{k}") for k in range(NB)]
        s_ytl = [sem(f"s_ytl{c}") for c in range(NC)]
        s_sum3 = sem("s_sum3")
        s_gates = sem("s_gates")
        s_gt = sem("s_gt")
        s_gT = sem("s_gT")
        s_acc = sem("s_acc")
        s_h = sem("s_h")
        s_ge = sem("s_ge")
        s_ye = sem("s_ye")
        s_l3 = sem("s_l3")
        s_rstd3 = sem("s_rstd3")
        s_fin = sem("s_fin")
        s_ctx = sem("s_ctx")
        s_out = sem("s_out")
        s_ckp = sem("s_ckp")
        s_ck = sem("s_ck")
        s_ckst = [sem(f"s_ckst{c}") for c in range(NC)]
        s_kvl = [sem(f"s_kvl{c}") for c in range(NC)]
        s_vx = sem("s_vx")
        s_x1l = [sem(f"s_x1l{c}") for c in range(NC)]
        s_x1t = sem("s_x1t")
        s_x1T = sem("s_x1T")
        s_cqp = sem("s_cqp")
        s_cq = sem("s_cq")
        s_cqst = [sem(f"s_cqst{c}") for c in range(NC)]
        s_cql = [sem(f"s_cql{p}") for p in range(NP // 2)]
        s_kqt = sem("s_kqt")
        s_km = sem("s_km")
        s_sc2 = sem("s_sc2")
        s_m2 = sem("s_m2")
        s_sub2 = sem("s_sub2")
        s_ex2 = sem("s_ex2")
        s_recip2 = sem("s_recip2")
        s_pn2 = sem("s_pn2")
        s_pv2 = sem("s_pv2")
        s_ot = sem("s_ot")
        s_ont = sem("s_ont")
        s_on = sem("s_on")
        s_ost = [sem(f"s_ost{k}") for k in range(2)]
        s_orl = [sem(f"s_orl{c}") for c in range(NC)]
        s_ort = sem("s_ort")
        s_orT = sem("s_orT")
        s_y2 = sem("s_y2")
        s_xb2 = sem("s_xb2")
        s_ln2 = sem("s_ln2")
        s_rstd2 = sem("s_rstd2")
        s_x2 = sem("s_x2")

        block = ctx.enter_context(nc.Block())
        SCALE2 = float(E) ** -0.5
        SP = mybir.EngineType.SP

        def by_token(scratch, n):
            return scratch[n * B * E:(n + 1) * B * E].rearrange("(h t d) -> t h d", t=B, d=D)

        def by_row(scratch):
            return scratch.rearrange("(g p e) -> p g e", p=P, e=E)
        SCALE1 = float(D) ** -0.5
        CTX_STEPS = (1, 2, 3, 5, 6, 7, 9, 10)

        @block.sync
        def _(sp):
            sp.dma_start(w[:, 0:4 * E], w_pack[:, 0:4 * E]).then_inc(s_const, 16)
            for c in range(NC):
                sp.dma_start(xT[:, 512 * c:512 * c + 512], x_t[:, 512 * c:512 * c + 512]).then_inc(s_xT[c], 16)
            sp.dma_start(xn[:, :, :], x_n).then_inc(s_xn, 16)
            sp.dma_start(w[:, 4 * E:8 * E], w_pack[:, 4 * E:8 * E]).then_inc(s_ctx, 16)
            sp.dma_start(ctxT[:, :], ctx_t).then_inc(s_ctx, 16)
            for c in range(NC):
                sp.wait_ge(s_vn, c + 1)
                sp.dma_start(v_scr.rearrange("(g p) e -> p g e", p=P)[:, 4 * c:4 * c + 4, :],
                             vn[:, 4 * c:4 * c + 4, :]).then_inc(s_vst[c], 16)
            sp.wait_ge(s_zero_d, 1)
            sp.wait_ge(s_zero_p, 1)
            for c in range(NC):
                sp.wait_ge(s_vst[c], 16)
                for g in range(4):
                    src = v_scr.rearrange("(b t) e -> t b e", t=S)[:, 16 * c:16 * c + 16, 32 * g:32 * g + 32]
                    sp.dma_start(vm[32 * g:32 * g + 32, 16 * c:16 * c + 16, 32 * g:32 * g + 32],
                                 src).then_inc(s_vm[c], 16)

            def kv_by_token(c):
                for h in range(2):
                    sp.wait_ge(s_ck, 2 * c + h + 1)
                    sp.dma_start(by_row((ck_scr, cv_scr)[h])[:, 4 * c:4 * c + 4, :],
                                 kv[:, h, 4 * c:4 * c + 4, :]).then_inc(s_ckst[c], 16)
                sp.wait_ge(s_ckst[c], 32)
                for p in range(4 * c, 4 * c + 4):
                    for h in range(2):
                        for n in range(2):
                            sp.dma_start(kv[64 * n:64 * n + 64, h, p, :].rearrange("t (h d) -> t h d", d=D),
                                         by_token((ck_scr, cv_scr)[h], 2 * p + n)).then_inc(s_kvl[c], 16)

            def cq_to_rows(c):
                sp.wait_ge(s_cq, c + 1)
                for j in range(4):
                    g = 4 * c + j
                    dst_rows = cq_scr.rearrange("(s b e) -> b s e", b=B, e=E)[4 * g:4 * g + 4, :, :]
                    sp.dma_start(dst_rows, qn[:, c % 2, j, :]).then_inc(s_cqst[c], 16)

            kv_by_token(0)
            kv_by_token(1)
            kv_by_token(2)
            cq_to_rows(0)
            kv_by_token(3)
            for c in range(1, NC):
                cq_to_rows(c)
            for c in range(NC):
                sp.wait_ge(s_cqst[c], 64)
            for p in range(NP):
                for n in range(2):
                    sp.dma_start(qs[64 * n:64 * n + 64, p, :].rearrange("t (h d) -> t h d", d=D),
                                 by_token(cq_scr, 2 * p + n)).then_inc(s_cql[p // 2], 16)
                if p == 3:
                    for c in range(2):
                        sp.wait_ge(s_x1st[c], 64 * NC // 2)
                    for c in range(NC):
                        sp.dma_start(x1[:, 4 * c:4 * c + 4, :],
                                     x1_scr.rearrange("(g p) e -> p g e", p=P)[:, 4 * c:4 * c + 4, :]).then_inc(s_x1l[c], 16)
            sp.dma_start(ew[:, :, :], e_w.rearrange("x p f -> p x f")).then_inc(s_ffw, 16)
            for i in range(NP + 1):
                if i < NP:
                    sp.wait_ge(s_on, i + 1)
                    for n in range(2):
                        sp.dma_start(by_token(o_scr, 2 * i + n),
                                     on[0:64, i % 2, 128 * n:128 * n + 128].rearrange("t (h d) -> t h d", d=D)
                                     ).then_inc(s_ost[i % 2], 16)
                if i >= 1:
                    sp.wait_ge(s_ost[(i - 1) % 2], 32 * ((i - 1) // 2 + 1))
                    if i - 1 >= 8:
                        sp.wait_ge(s_ort, (i - 1) // 4 - 1)
                    sp.dma_start(orow[:, (i - 1) % 8, :], by_row(o_scr)[:, i - 1, :]).then_inc(s_orl[(i - 1) // 4], 16)
            sp.wait_ge(s_rtc, 6)
            sp.dma_start(x_srt[NE * ROOM:ROWS, :], pad[:, :]).then_inc(s_fill, 16)
            sp.wait_ge(s_ends, 1)
            for e in range(0, NE, 4):
                k = min(4, NE - e)
                ends_of = nc.values_load_multi_w_load_instructions(
                    ends[0:1, e:e + k], engines=[SP], min_val=0, max_val=NE * ROOM - P)[1]
                for j in range(k):
                    sp.dma_start(x_srt[bass.ds(ends_of[j], P), :], pad[:, :]).then_inc(s_fill, 16)
            sp.wait_ge(s_fill, 16 * (NE + 1))
            sp.wait_ge(s_scat, 16 * NG * TOPK)
            sp.wait_ge(s_tab, 1)
            for t in range(NT):
                if t % 4 == 0:
                    row_of = nc.values_load_multi_w_load_instructions(
                        t_row[0:1, t:t + 4], engines=[SP], min_val=0, max_val=NE * ROOM)[1]
                if t >= NB:
                    sp.wait_ge(s_yl, t - NB + 1)
                    sp.wait_ge(s_idx, (t - NB) // 4 + 1)
                sp.dma_start(xin[:, t % NB, :], x_srt[bass.ds(row_of[t % 4], P), :]).then_inc(s_xin[t % NB], 16)
            for k in range(NB):
                sp.wait_ge(s_ysc[k], 16 * (NT // NB))
            for c in range(NC):
                for k in range(TOPK):
                    sp.dma_start(routed_y[k][:, 4 * c:4 * c + 4, :],
                                 y_tok[NT * P:NT * P + TOPK * T, :].rearrange("(k g p) e -> k p g e", g=NG, p=P)[k][:, 4 * c:4 * c + 4, :]
                                 ).then_inc(s_ytl[c], 16)
            for c in range(NC):
                sp.wait_ge(s_fin, c + 1)
                sp.dma_start(out.rearrange("s b e -> (s b) e").rearrange("(g p) e -> p g e", p=P)[:, 4 * c:4 * c + 4, :],
                             acc[:, 4 * c:4 * c + 4, :]).then_inc(s_out, 16)
            sp.wait_ge(s_out, 16 * NC)

        @block.tensor
        def _(pe):
            pe.wait_ge(s_const, 48)

            def proj_v(c):
                pe.wait_ge(s_xT[c], 16)
                if c >= 2:
                    pe.wait_ge(s_vn, c - 1)
                for j in range(4):
                    g = 4 * c + j
                    mm = pe.matmul(bank[6 + c % 2][:, E * j:E * j + E], xT[:, P * g:P * g + P], w[:, W_V:W_V + E],
                                   start=True, stop=True)
                mm.then_inc(s_vproj, 1)

            bank0_reader = [None]

            def bank0_free():
                if bank0_reader[0]:
                    pe.wait_ge(*bank0_reader[0])

            def proj_q(c):
                bank0_free()
                bank0_reader[0] = (s_qm, c + 1)
                pe.matmul(bank[0][:, :], w[:, W_Q:W_Q + E], xT[:, 512 * c:512 * c + 512],
                          start=True, stop=True).then_inc(s_qp, 1)

            def proj_k(c):
                if c >= 1:
                    pe.wait_ge(s_k4, c)
                pe.matmul(bank[1][:, :], w[:, W_K:W_K + E], xT[:, 512 * c:512 * c + 512],
                          start=True, stop=True).then_inc(s_kp, 1)

            def scores(g):
                c, j = g // 4, g % 4
                pe.wait_ge(s_qm, c + 1)
                pe.wait_ge(s_k4, c + 1)
                if g >= 2:
                    pe.wait_ge(s_ex, g - 1)
                for b in range(4):
                    o = 128 * j + 32 * b
                    mm = pe.matmul(bank[2 + g % 2][:, 128 * b:128 * b + 128], qm[:, c % 2, 4 * j + b, :],
                                   k4[:, c % 2, :, o:o + 32], start=(b == 0), stop=False, skip_group_check=True)
                mm.then_inc(s_sc, 1)

            def subtract_max(g):
                pe.wait_ge(s_mb, g + 1)
                pe.matmul(bank[2 + g % 2][:, :], neg_id[:, :], mb[:, g % 2, :].unsqueeze(2).broadcast_to([P, 16, 32]),
                          start=False, stop=True, skip_group_check=True).then_inc(s_sub, 1)

            def weighted(g):
                pe.wait_ge(s_pt, g + 1)
                pe.wait_ge(s_vm[g // 4], 64)
                if g >= 2:
                    pe.wait_ge(s_us, g - 1)
                for b in range(4):
                    mm = pe.matmul(bank[4 + g % 2][:, 128 * b:128 * b + 128], vm[:, 4 * g + b, :],
                                   pt[:, g % 2, 128 * b:128 * b + 128], start=True, stop=True)
                mm.then_inc(s_u, 1)

            def out_proj(g):
                c, j = g // 4, g % 4
                pe.wait_ge(s_us, g + 1)
                if j == 0 and c >= 2:
                    pe.wait_ge(s_cq, c - 1)
                u = us[:, g % 2, :].rearrange("p (h t) -> p h t", h=4)
                for h in range(4):
                    mm = pe.matmul(bank[6 + c % 2][:, E * j:E * j + E], u[:, h, :], wom[:, h, :],
                                   start=(h == 0), stop=(h == 3))
                mm.then_inc(s_y, 1)

            def proj_ctx(c):
                i, h = c // 2, c % 2
                bank0_free()
                bank0_reader[0] = (s_ck, c + 1)
                for j in range(4):
                    g = 4 * i + j
                    mm = pe.matmul(bank[0][:, E * j:E * j + E], ctxT[:, P * g:P * g + P],
                                   w[:, (X_K, X_V)[h]:(X_K, X_V)[h] + E], start=True, stop=True)
                mm.then_inc(s_ckp, 1)

            def x1_turned(c):
                pe.wait_ge(s_x1, 4 * c + 4)
                for j in range(4):
                    mm = pe.transpose(bank[6 + c % 2][:, P * j:P * j + P], res[:, c % 2, j, :], ident)
                mm.then_inc(s_x1t, 1)

            def proj_cq(c):
                pe.wait_ge(s_x1T, c + 1)
                for j in range(4):
                    mm = pe.matmul(bank[6 + c % 2][:, E * j:E * j + E], x1T[:, c, P * j:P * j + P],
                                   w[:, X_Q:X_Q + E], start=True, stop=True)
                mm.then_inc(s_cqp, 1)

            pe.wait_ge(s_xT[0], 16)
            proj_q(0)
            proj_k(0)
            for c in range(NC):
                proj_v(c)
            pe.wait_ge(s_vn, NC)
            pe.wait_ge(s_prep, 3)
            for i in range(STEPS1):
                if i == 0:
                    scores(0)
                if i < NG:
                    subtract_max(i)
                if i + 1 < NG:
                    scores(i + 1)
                if 3 <= i < NG + 3:
                    weighted(i - 3)
                if i % 4 == 0 and i // 4 + 1 < NC:
                    proj_q(i // 4 + 1)
                if i % 4 == 1 and i // 4 + 1 < NC:
                    proj_k(i // 4 + 1)
                if i == CTX_STEPS[0]:
                    pe.wait_ge(s_ctx, 32)
                if i in CTX_STEPS:
                    proj_ctx(CTX_STEPS.index(i))
                if 4 <= i < NG + 4:
                    out_proj(i - 4)
                if i >= 10 and i % 4 == 2:
                    x1_turned(i // 4 - 2)
                if i >= 11 and i % 4 == 3:
                    proj_cq(i // 4 - 2)

            def kq_turned(p):
                pe.wait_ge(s_kvl[p // 4], 256)
                pe.wait_ge(s_cql[p // 2], 64)
                if p >= 1:
                    pe.wait_ge(s_km, p)
                pe.transpose(bank[4][:, 0:P], kv[:, 0, p, :], ident)
                pe.transpose(bank[4][:, P:2 * P], qs[:, p, :], ident).then_inc(s_kqt, 1)

            def scores2(p):
                pe.wait_ge(s_km, p + 1)
                if p >= 2:
                    pe.wait_ge(s_ex2, p - 1)
                for h in range(4):
                    for n in range(2):
                        o = 256 * (h % 2)
                        mm = pe.matmul(bank[2 * (p % 2) + h // 2][64 * n:64 * n + 64, o:o + 256],
                                       km[:, p % 2, h, 64 * n:64 * n + 64], q4[:, p % 2, :, 64 * n:64 * n + 64],
                                       start=(h % 2 == 0), stop=False, skip_group_check=True)
                mm.then_inc(s_sc2, 1)

            def subtract_max2(p):
                pe.wait_ge(s_m2, p + 1)
                for k in range(2):
                    mm = pe.matmul(bank[2 * (p % 2) + k], neg_id[:, :], m2[:, p % 2, :].unsqueeze(1).broadcast_to([P, 8, B]),
                                   start=False, stop=True, skip_group_check=True)
                mm.then_inc(s_sub2, 1)

            def weighted2(p):
                pe.wait_ge(s_pn2, p + 1)
                pe.wait_ge(s_vx, p + 1)
                if p >= 1:
                    pe.wait_ge(s_ot, p)
                for j in range(8):
                    mm = pe.matmul(bank[6][32 * (j % 4):32 * (j % 4) + 32, 128 * (j // 4):128 * (j // 4) + 128],
                                   vx[:, p, j, :, :].rearrange("p a b -> p (a b)"), e2[:, p % 3, 128 * j:128 * j + 128],
                                   start=True, stop=True)
                mm.then_inc(s_pv2, 1)

            bank5_reader = [None]

            def bank5_free():
                if bank5_reader[0]:
                    pe.wait_ge(*bank5_reader[0])
                    bank5_reader[0] = None

            def o_by_token(p):
                if p == 0:
                    pe.wait_ge(s_rtc, 6)
                pe.wait_ge(s_ot, p + 1)
                if p >= 1:
                    pe.wait_ge(s_on, p)
                for j in range(2):
                    for h in range(2):
                        o = P * j + B * h
                        mm = pe.matmul(bank[7][0:64, P * j:P * j + P], ut[:, p % 2, o:o + B], id_h2[:, h, :],
                                       start=(h == 0), stop=(h == 1))
                mm.then_inc(s_ont, 1)

            def orow_turned(c):
                pe.wait_ge(s_orl[c], 64)
                bank5_free()
                for j in range(4):
                    mm = pe.transpose(bank[5][:, P * j:P * j + P], orow[:, (4 * c + j) % 8, :], ident)
                mm.then_inc(s_ort, 1)

            def out_proj2(c):
                pe.wait_ge(s_orT, c + 1)
                for j in range(4):
                    mm = pe.matmul(bank[5][:, E * j:E * j + E], orT[:, c % 2, P * j:P * j + P], w[:, X_O:X_O + E],
                                   start=True, stop=True)
                mm.then_inc(s_y2, 1)
                bank5_reader[0] = (s_ln2, 3 * c + 1)

            def x2_turned(c):
                pe.wait_ge(s_x2, 4 * c + 4)
                bank5_free()
                for j in range(4):
                    mm = pe.transpose(bank[5][:, P * j:P * j + P], x2[:, 4 * c + j, :], ident)
                mm.then_inc(s_x2t, 1)
                bank5_reader[0] = (s_x2T, c + 1)

            def logits(c):
                bank5_free()
                for j in range(4):
                    g = 4 * c + j
                    mm = pe.matmul(bank[5][:, 16 * j:16 * j + NE], x2T[:, P * g:P * g + P], gw[:, :], start=True, stop=True)
                mm.then_inc(s_lg, 1)
                bank5_reader[0] = (s_lgs, 3 * c + 1)

            def ranks(c):
                pe.wait_ge(s_msk, c + 1)
                bank5_free()
                for j in range(4):
                    o = bank[5][:, 16 * j:16 * j + NE]
                    pe.matmul(o, tri[:, :], msk[:, 4 * c + j, :], start=True, stop=False)
                    for i in range(j):
                        pe.matmul(o, ones[:, :], msk[:, 4 * c + i, :], start=False, stop=False)
                    mm = pe.matmul(o, ones[:, :], carry[:, c, :], start=False, stop=True)
                mm.then_inc(s_pre, 1)
                bank5_reader[0] = (s_slot, 3 * c + 1)

            def gates_turned(c):
                pe.wait_ge(s_gates, c + 1)
                if c >= 1:
                    pe.wait_ge(s_gT, c)
                for j in range(4):
                    mm = pe.transpose(bank[6][0:NE + 1, P * j:P * j + P], gates[:, 4 * c + j, :], ident)
                mm.then_inc(s_gt, 1)

            def shared_in(k):
                c, h = k // 2, k % 2
                if k >= 2:
                    pe.wait_ge(s_ge, 2 * (k - 1))
                for a in range(2):
                    pe.matmul(bank[2 * (k % 2) + a], ew[:, NE + h, P * a:P * a + P], x2T[:, 512 * c:512 * c + 512],
                              start=True, stop=True).then_inc(s_h, 1)

            def shared_out(c, j):
                if j == 0:
                    pe.wait_ge(s_ge, 4 * c + 4)
                    pe.wait_ge(s_gT, c + 1)
                    if c >= 2:
                        pe.wait_ge(s_acc, c - 1)
                o = bank[(4, 7)[c % 2]][:, E * j:E * j + E]
                for k in range(2 * c, 2 * c + 2):
                    for a in range(2):
                        pe.matmul(o, hb[:, k % 2, a, P * j:P * j + P],
                                  ew[:, NE + k % 2, FE + E * a:FE + E * a + E], start=(k % 2 == 0 and a == 0), stop=False)
                mm = pe.matmul(o, gT[:, c % 2, P * j:P * j + P], b2[:, :], start=False, stop=True)
                if j == 3:
                    mm.then_inc(s_ye, 1)

            pe.wait_ge(s_qm, NC)
            pe.wait_ge(s_k4, NC)
            pe.wait_ge(s_ck, 2 * NC)
            pe.wait_ge(s_ex, NG)
            pe.wait_ge(s_us, NG)
            pe.wait_ge(s_cq, NC)
            kq_turned(0)
            kq_turned(1)
            scores2(0)
            for i in range(STEPS2):
                if 3 <= i < NP + 3:
                    weighted2(i - 3)
                if i < NP:
                    subtract_max2(i)
                if i + 2 < NP:
                    kq_turned(i + 2)
                if i + 1 < NP:
                    scores2(i + 1)
                if i >= 4:
                    o_by_token(i - 4)
                if i - 2 in TURN[:2]:
                    x2_turned(TURN.index(i - 2))
                    logits(TURN.index(i - 2))
                if i - 3 in TURN[:2]:
                    ranks(TURN.index(i - 3))
                if i in TURN:
                    orow_turned(TURN.index(i))
                    out_proj2(TURN.index(i))

            o_by_token(NP - 1)
            x2_turned(2)
            pe.wait_ge(s_ex2, NP)
            pe.wait_ge(s_ot, NP)
            gates_turned(0)
            pe.wait_ge(s_ffw, 16)
            shared_in(0)
            logits(2)
            shared_in(1)
            for j in range(4):
                shared_out(0, j)
            ranks(2)
            orow_turned(3)
            shared_in(2)
            out_proj2(3)
            gates_turned(1)
            shared_in(3)
            pe.wait_ge(s_on, NP)
            for j in range(4):
                shared_out(1, j)
            x2_turned(3)
            gates_turned(2)
            shared_in(4)
            logits(3)
            shared_in(5)
            for j in range(3):
                shared_out(2, j)
            ranks(3)
            pe.matmul(bank[5][:, 64:64 + NE], ones[:, :], carry[:, NC, :], start=True, stop=True).then_inc(s_cnt, 1)
            shared_out(2, 3)

            gates_turned(NC - 1)
            for k in (6, 7):
                shared_in(k)
            for j in range(4):
                shared_out(NC - 1, j)

            def tile_turned(t):
                pe.wait_ge(s_xin[t % NB], 16 * (t // NB + 1))
                if t >= 2:
                    pe.wait_ge(s_xiT, t - 1)
                pe.transpose(bank[t % 2][:, 0:P], xin[:, t % NB, 0:E], ident).then_inc(s_xit, 1)

            def tile_in(t):
                pe.wait_ge(s_xiT, t + 1)
                pe.wait_ge(s_stage, t + 1)
                if t >= 2:
                    pe.wait_ge(s_gl, t - 1)
                for a in range(2):
                    mm = pe.matmul(bank[2 + t % 2][:, P * a:P * a + P], stage[:, t % 5, P * a:P * a + P],
                                   xinT[:, t % 2, :], start=True, stop=True)
                mm.then_inc(s_hl, 1)

            def tile_out(t):
                pe.wait_ge(s_gl, t + 1)
                if t >= 2:
                    pe.wait_ge(s_yl, t - 1)
                for a in range(2):
                    mm = pe.matmul(bank[6 + t % 2][:, 0:E], hl[:, t % 2, a, :],
                                   stage[:, t % 5, FE + E * a:FE + E * a + E], start=(a == 0), stop=(a == 1))
                mm.then_inc(s_yo, 1)

            pe.wait_ge(s_ge, 4 * NC)
            for i in range(NT + 2):
                if i < NT:
                    tile_turned(i)
                if 1 <= i < NT + 1:
                    tile_in(i - 1)
                if i >= 2:
                    tile_out(i - 2)

        @block.scalar
        def _(act):
            act.dma_start(cst[:, :], c_pack).then_inc(s_const, 16)
            act.dma_start(bcol[:, :], b_col).then_inc(s_const, 16)
            act.dma_start(b2[:, :], e_b2).then_inc(s_small, 16)
            act.dma_start(gw[:, :], g_w).then_inc(s_small, 16)
            act.dma_start(gb[:, :], g_b.partition_broadcast(P)).then_inc(s_small, 16)
            act.dma_start(kr[:, :], k_row.partition_broadcast(P)).then_inc(s_small, 16)
            act.dma_start(dst[:, :], dst_rows).then_inc(s_small, 16)
            act.dma_start(brow[:, :], b_row.partition_broadcast(P)).then_inc(s_brow, 16)

            def q_masked(c):
                act.wait_ge(s_qp, c + 1)
                if c >= 2:
                    act.wait_ge(s_sc, 4 * (c - 1))
                for h in range(4):
                    a = act.activation(qm[:, c % 2, :, 32 * h:32 * h + 32],
                                       bank[0][:, :].rearrange("p (b s) -> p b s", s=S), ACT.Identity,
                                       bias=bqm[:, h:h + 1], scale=m_hg[:, h:h + 1])
                a.then_inc(s_qm, 1)

            def k_masked(c):
                act.wait_ge(s_kp, c + 1)
                if c >= 2:
                    act.wait_ge(s_sc, 4 * (c - 1))
                for h in range(4):
                    a = act.activation(k4[:, c % 2, h, :], bank[1][:, :], ACT.Identity, bias=bkm[:, h:h + 1],
                                       scale=m_h4[:, h:h + 1])
                a.then_inc(s_k4, 1)

            def exps(g):
                act.wait_ge(s_sub, g + 1)
                if g >= 3:
                    act.wait_ge(s_pt, g - 2)
                act.activation(ex[:, g % 3, :], bank[2 + g % 2][:, :], ACT.Exp, scale=SCALE1).then_inc(s_ex, 1)

            def u_out(g):
                act.wait_ge(s_u, g + 1)
                if g >= 2:
                    act.wait_ge(s_y, g - 1)
                act.activation(us[:, g % 2, :].rearrange("p (h b s) -> p b h s", h=4, b=4),
                               bank[4 + g % 2][:, :].rearrange("p (b h s) -> p b h s", b=4, h=4), ACT.Identity, bias=bcol[:, 2:3]).then_inc(s_us, 1)

            act.wait_ge(s_const, 48)
            act.mul(neg_id[:, :], ident, -1.0).then_inc(s_prep, 1)
            act.wait_ge(s_prep, 3)
            q_masked(0)
            k_masked(0)
            for c in range(2):
                act.wait_ge(s_vproj, 2 * c + 1)
                act.copy(vn[:, 8 * c:8 * c + 4, :].rearrange("p g e -> p (g e)"), bank[6][:, :]).then_inc(s_vn, 1)
                act.wait_ge(s_vproj, 2 * c + 2)
                act.copy(vn[:, 8 * c + 4:8 * c + 8, :].rearrange("p g e -> p (g e)"), bank[7][:, :]).then_inc(s_vn, 1)

            def x1T_out(c):
                act.wait_ge(s_x1t, c + 1)
                act.copy(x1T[:, c, :], bank[6 + c % 2]).then_inc(s_x1T, 1)

            for i in range(STEPS1):
                if i < NG:
                    exps(i)
                if i % 4 == 0 and i // 4 + 1 < NC:
                    q_masked(i // 4 + 1)
                if i % 4 == 1 and i // 4 + 1 < NC:
                    k_masked(i // 4 + 1)
                if 3 <= i < NG + 3:
                    u_out(i - 3)
                if i >= 10 and i % 4 == 2:
                    x1T_out(i // 4 - 2)

            def k_masked2(p):
                act.wait_ge(s_kqt, p + 1)
                if p >= 2:
                    act.wait_ge(s_sc2, p - 1)
                for h in range(4):
                    act.activation(km[:, p % 2, h, :], bank[4][:, 0:P], ACT.Copy, scale=m_hg[:, h:h + 1])
                for h in range(4):
                    a = act.activation(q4[:, p % 2, h, :], bank[4][:, P:2 * P], ACT.Copy, scale=m_h4[:, h:h + 1])
                a.then_inc(s_km, 1)

            def exps2(p):
                act.wait_ge(s_sub2, p + 1)
                if p >= 3:
                    act.wait_ge(s_pv2, p - 2)
                act.activation(e2[:, p % 3, :], psum[:, 1024 * (p % 2):1024 * (p % 2) + 1024], ACT.Exp,
                               scale=SCALE2).then_inc(s_ex2, 1)

            def u2_out(p):
                act.wait_ge(s_pv2, p + 1)
                if p >= 2:
                    act.wait_ge(s_ont, p - 1)
                act.copy(ut[:, p % 2, :], bank[6][:, 0:256]).then_inc(s_ot, 1)

            def on_out(p):
                act.wait_ge(s_ont, p + 1)
                if p >= 2:
                    act.wait_ge(s_ost[p % 2], 32 * (p // 2))
                act.copy(on[0:64, p % 2, :].rearrange("t (n j c) -> t j n c", n=2, j=8),
                         bank[7][0:64, 0:256].rearrange("t (j n c) -> t j n c", n=2, j=8)).then_inc(s_on, 1)

            def x2T_out(c):
                act.wait_ge(s_x2t, c + 1)
                act.copy(x2T[:, 512 * c:512 * c + 512], bank[5]).then_inc(s_x2T, 1)

            def exp_logits(c):
                act.wait_ge(s_lgs, 3 * c + 3)
                act.activation(lg[:, :, :], lg[:, :, :], ACT.Exp).then_inc(s_lge, 1)

            def payload(c):
                act.wait_ge(s_x2, 4 * c + 4)
                for k in range(1, TOPK):
                    act.copy(pay[:, 4 * c:4 * c + 4, k, 0:E], x2[:, 4 * c:4 * c + 4, :]).then_inc(s_pay, 1)

            def orT_out(c):
                act.wait_ge(s_ort, c + 1)
                if c >= 2:
                    act.wait_ge(s_y2, c - 1)
                act.copy(orT[:, c % 2, :], bank[5]).then_inc(s_orT, 1)

            def shared_gelu(k):
                for a in range(2):
                    act.wait_ge(s_h, 2 * k + a + 1)
                    if k >= 2 and a == 0:
                        act.wait_ge(s_ye, k // 2)
                    act.activation(hb[:, k % 2, a, :], bank[2 * (k % 2) + a], ACT.Gelu,
                                   bias=ew[:, NE + k % 2, EW - 2 + a:EW - 1 + a]).then_inc(s_ge, 1)

            k_masked2(0)
            k_masked2(1)
            for i in range(STEPS2):
                if 3 <= i < NP + 3:
                    u2_out(i - 3)
                if i < NP:
                    exps2(i)
                if i + 2 < NP:
                    k_masked2(i + 2)
                if i >= 4:
                    on_out(i - 4)
                if i - 2 in TURN[:2]:
                    x2T_out(TURN.index(i - 2))
                    exp_logits(TURN.index(i - 2))
                if i - 3 in TURN[:2]:
                    payload(TURN.index(i - 3))
                if i in TURN:
                    orT_out(TURN.index(i))

            on_out(NP - 1)
            x2T_out(2)
            shared_gelu(0)
            exp_logits(2)
            shared_gelu(1)
            payload(2)
            orT_out(3)
            shared_gelu(2)
            shared_gelu(3)
            x2T_out(3)
            shared_gelu(4)
            exp_logits(3)
            shared_gelu(5)
            payload(3)
            shared_gelu(6)
            shared_gelu(7)

            for i in range(NT + 1):
                if i < NT:
                    t = i
                    act.wait_ge(s_hl, t + 1)
                    if t >= 2:
                        act.wait_ge(s_yo, t - 1)
                    for a in range(2):
                        ins = act.activation(hl[:, t % 2, a, :], bank[2 + t % 2][:, P * a:P * a + P], ACT.Gelu,
                                             bias=stage[:, t % 5, EW - 2 + a:EW - 1 + a])
                    ins.then_inc(s_gl, 1)
                if i >= 1:
                    t = i - 1
                    act.wait_ge(s_yo, t + 1)
                    if t >= NB:
                        act.wait_ge(s_ysc[t % NB], 16 * (t // NB))
                    act.activation(yl[:, t % NB, :], bank[6 + t % 2][:, 0:E], ACT.Copy,
                                   scale=xin[:, t % NB, E:E + 1]).then_inc(s_yl, 1)

        @block.vector
        def _(dve):
            dve.memset(vm[:, 0:B // 2, :].rearrange("p b e -> p (b e)"), 0.0).then_inc(s_zero_d, 1)
            dve.wait_ge(s_const, 48)
            dve.tensor_scalar(bqm[:, :], m_hg, bcol[:, 0:1], None, ALU.mult)
            dve.tensor_scalar(bkm[:, :], m_h4, bcol[:, 1:2], None, ALU.mult).then_inc(s_prep, 1)
            for h in range(4):
                ins = dve.tensor_scalar(wom[:, h, :], w[:, W_O:W_O + E], m_h4[:, h:h + 1], None, ALU.mult)
            ins.then_inc(s_prep, 1)

            def ctx_out(c):
                i, h = c // 2, c % 2
                dve.wait_ge(s_ckp, c + 1)
                r = (R_XK, R_XV)[h]
                dve.tensor_tensor(kv[:, h, 4 * i:4 * i + 4, :],
                                  bank[0].rearrange("p (g e) -> p g e", e=E),
                                  brow[:, r:r + E].unsqueeze(1).broadcast_to([P, 4, E]), ALU.add).then_inc(s_ck, 1)

            def row_max(g):
                dve.wait_ge(s_sc, g + 1)
                if g >= 2:
                    dve.wait_ge(s_sub, g - 1)
                with nc.allow_low_precision(reason="any shift near the maximum serves the softmax"):
                    dve.tensor_reduce(mb[:, g % 2, :], bank[2 + g % 2][:, :].rearrange("p (a t) -> p a t", t=S),
                                      AX_X, ALU.max).then_inc(s_mb, 1)

            def row_sum(g):
                dve.wait_ge(s_ex, g + 1)
                dve.tensor_reduce(ssum[:, g % 2, :], ex[:, g % 3, :].rearrange("p (a t) -> p a t", t=S),
                                  AX_X, ALU.add).then_inc(s_recip, 1)
                dve.wait_ge(s_recip, 2 * (g + 1) - 1)
                if g >= 2:
                    dve.wait_ge(s_pn, g - 1)
                dve.reciprocal(rs[:, g % 2, :], ssum[:, g % 2, :]).then_inc(s_recip, 1)

            def turn(g):
                dve.wait_ge(s_pn, g + 1)
                if g >= 2:
                    dve.wait_ge(s_u, g - 1)
                dve.transpose(pt[:, g % 2, :], ex[:, g % 3, :]).then_inc(s_pt, 1)

            def ln1_stats(c):
                dve.wait_ge(s_y, 4 * c + 4)
                if c >= 2:
                    dve.wait_ge(s_x1, 4 * (c - 1))
                    dve.wait_ge(s_x1st[c % 2], 64 * (c // 2))
                    dve.wait_ge(s_x1t, c - 1)
                dve.tensor_tensor(res[:, c % 2, :, :].rearrange("p g e -> p (g e)"), bank[6 + c % 2][:, :],
                                  xn[:, 4 * c:4 * c + 4, :].rearrange("p g e -> p (g e)"), ALU.add).then_inc(s_ln1, 1)
                dve.wait_ge(s_ln1, 3 * (c + 1) - 2)
                for j in range(4):
                    ins = dve.bn_stats(bst[:, c % 2, j, :], res[:, c % 2, j, :])
                ins.then_inc(s_ln1, 1)
                dve.wait_ge(s_ln1, 3 * (c + 1) - 1)
                for j in range(4):
                    ins = dve.bn_aggr(mv[:, c % 2, j, :], bst[:, c % 2, j, :])
                ins.then_inc(s_ln1, 1)

            def ln1_apply(c):
                dve.wait_ge(s_rstd, 2 * (c + 1))
                for j in range(4):
                    dve.tensor_scalar(res[:, c % 2, j, :], res[:, c % 2, j, :], mv[:, c % 2, j, 0:1],
                                      rstd[:, c % 2, j:j + 1], ALU.subtract, ALU.mult).then_inc(s_x1, 1)

            def cq_out(c):
                dve.wait_ge(s_cqp, c + 1)
                if c >= 2:
                    dve.wait_ge(s_cqst[c - 2], 64)
                dve.tensor_tensor(qn[:, c % 2, :, :], bank[6 + c % 2].rearrange("p (g e) -> p g e", e=E),
                                  brow[:, R_XQ:R_XQ + E].unsqueeze(1).broadcast_to([P, 4, E]), ALU.add).then_inc(s_cq, 1)

            dve.wait_ge(s_brow, 16)
            for i in range(STEPS1):
                if i == 0:
                    row_max(0)
                if 1 <= i < NG + 1:
                    row_sum(i - 1)
                if i + 1 < NG:
                    row_max(i + 1)
                if 2 <= i < NG + 2:
                    turn(i - 2)
                if i in CTX_STEPS:
                    ctx_out(CTX_STEPS.index(i))
                if i >= 8 and i % 4 == 0 and i // 4 - 2 < NC:
                    ln1_stats(i // 4 - 2)
                if i >= 9 and i % 4 == 1 and i // 4 - 2 < NC:
                    ln1_apply(i // 4 - 2)
                if i >= 11 and i % 4 == 3:
                    cq_out(i // 4 - 2)

            def head_max(p):
                dve.wait_ge(s_sc2, p + 1)
                if p >= 2:
                    dve.wait_ge(s_sub2, p - 1)
                with nc.allow_low_precision(reason="any shift near the maximum serves the softmax"):
                    dve.tensor_reduce(m2[:, p % 2, :],
                                      psum[:, 1024 * (p % 2):1024 * (p % 2) + 1024].rearrange("p (h t) -> p t h", t=B),
                                      AX_X, ALU.max).then_inc(s_m2, 1)

            def head_sum(p):
                dve.wait_ge(s_ex2, p + 1)
                dve.tensor_reduce(sum2[:, p % 2, :], e2[:, p % 3, :].rearrange("p (h t) -> p t h", t=B),
                                  AX_X, ALU.add).then_inc(s_recip2, 1)
                dve.wait_ge(s_recip2, 2 * (p + 1) - 1)
                if p >= 2:
                    dve.wait_ge(s_pn2, p - 1)
                dve.reciprocal(r2[:, p % 2, :], sum2[:, p % 2, :]).then_inc(s_recip2, 1)

            def ln2_stats(c):
                dve.wait_ge(s_y2, c + 1)
                dve.wait_ge(s_xb2, c + 1)
                if c >= 2:
                    dve.wait_ge(s_x2, 4 * (c - 1))
                dve.tensor_tensor(res2[:, c % 2, :, :].rearrange("p g e -> p (g e)"), bank[5],
                                  x1[:, 4 * c:4 * c + 4, :].rearrange("p g e -> p (g e)"), ALU.add).then_inc(s_ln2, 1)
                dve.wait_ge(s_ln2, 3 * (c + 1) - 2)
                for j in range(4):
                    ins = dve.bn_stats(bst2[:, c % 2, j, :], res2[:, c % 2, j, :])
                ins.then_inc(s_ln2, 1)
                dve.wait_ge(s_ln2, 3 * (c + 1) - 1)
                for j in range(4):
                    ins = dve.bn_aggr(mv2[:, c % 2, j, :], bst2[:, c % 2, j, :])
                ins.then_inc(s_ln2, 1)

            def ln2_apply(c):
                dve.wait_ge(s_rstd2, 2 * (c + 1))
                for j in range(4):
                    dve.tensor_scalar(x2[:, 4 * c + j, :], res2[:, c % 2, j, :], mv2[:, c % 2, j, 0:1],
                                      rstd2[:, c % 2, j:j + 1], ALU.subtract, ALU.mult).then_inc(s_x2, 1)

            step = [0]

            def routed(ins):
                step[0] += 1
                ins.then_inc(s_rt, 1)
                dve.wait_ge(s_rt, step[0])

            def route_logits(c):
                lc = lg[:, 0:4, :]
                dve.wait_ge(s_lg, c + 1)
                dve.tensor_tensor(lc, bank[5][:, 0:64].rearrange("p (g e) -> p g e", e=16)[:, :, 0:NE],
                                  gb[:, :].unsqueeze(1).broadcast_to([P, 4, NE]), ALU.add).then_inc(s_lgs, 1)
                dve.wait_ge(s_lgs, 3 * c + 1)
                dve.tensor_reduce(lmax[:, 4 * c:4 * c + 4], lc, AX_X, ALU.max).then_inc(s_lgs, 1)
                dve.wait_ge(s_lgs, 3 * c + 2)
                dve.tensor_tensor(lc, lc, lmax[:, 4 * c:4 * c + 4].unsqueeze(2).broadcast_to([P, 4, NE]),
                                  ALU.subtract).then_inc(s_lgs, 1)

            def route_top(c):
                lc = lg[:, 0:4, :]
                lsc = lsum[:, 4 * c:4 * c + 4]
                dve.wait_ge(s_lge, c + 1)
                routed(dve.tensor_reduce(lsc, lc, AX_X, ALU.add))
                routed(dve.reciprocal(lsc, lsc))
                routed(dve.tensor_tensor(lc, lc, lsc.unsqueeze(2).broadcast_to([P, 4, NE]), ALU.mult))
                for g in range(4 * c, 4 * c + 4):
                    ins = dve.max(top[:, g % 4, :], lg[:, g % 4, :])
                routed(ins)
                for g in range(4 * c, 4 * c + 4):
                    ins = dve.max_index(topi[:, g % 4, :], top[:, g % 4, :], lg[:, g % 4, :])
                routed(ins)
                o4 = oh[:, :, :, :]
                routed(dve.tensor_tensor(o4, kr[:, K_IOTA:K_IOTA + NE].unsqueeze(1).unsqueeze(1).broadcast_to([P, 4, TOPK, NE]),
                                         topi[:, :, 0:TOPK].unsqueeze(3).broadcast_to([P, 4, TOPK, NE]), ALU.is_equal))
                with nc.allow_low_precision(reason="zeros and ones"):
                    routed(dve.tensor_reduce(msk[:, 4 * c:4 * c + 4, :], o4.rearrange("p g k e -> p g e k"), AX_X, ALU.add))
                with nc.allow_low_precision(reason="small whole numbers"):
                    routed(dve.tensor_reduce(mskf[:, :], msk[:, 4 * c:4 * c + 4, :].rearrange("p g e -> p e g"), AX_X, ALU.add))
                    dve.tensor_tensor(carry[:, c + 1, :], carry[:, c, :], mskf[:, :], ALU.add).then_inc(s_msk, 1)

            def route_slots(c):
                o4 = oh[:, 0:4, :, :]
                dve.wait_ge(s_pre, c + 1)
                if c == NC - 1:
                    dve.wait_ge(s_cnt, 1)
                dve.tensor_tensor(rank[:, :, :], bank[5][:, 0:64].rearrange("p (g e) -> p g e", e=16)[:, :, 0:NE],
                                  kr[:, K_BASE:K_BASE + NE].unsqueeze(1).broadcast_to([P, 4, NE]), ALU.add).then_inc(s_slot, 1)
                dve.wait_ge(s_slot, 3 * c + 1)
                routed(dve.tensor_tensor(sel[:, :, :].rearrange("p (g k) e -> p g k e", k=TOPK), o4,
                                         rank[:, :, :].unsqueeze(2).broadcast_to([P, 4, TOPK, NE]), ALU.mult))
                dve.tensor_copy(pay[:, 4 * c:4 * c + 4, :, E], top[:, 0:4, 0:TOPK]).then_inc(s_slot, 1)
                with nc.allow_low_precision(reason="whole numbers below 2**24"):
                    dve.tensor_reduce(slot[:, 12 * c:12 * c + 12], sel[:, :, :], AX_X, ALU.add).then_inc(s_slot, 1)
                routed(dve.tensor_tensor(o4, o4, top[:, :, 0:TOPK].unsqueeze(3).broadcast_to([P, 4, TOPK, NE]), ALU.mult))
                dve.tensor_reduce(gates[:, 4 * c:4 * c + 4, 0:NE], o4.rearrange("p g k e -> p g e k"),
                                  AX_X, ALU.add).then_inc(s_gates, 1)

            for h in range(2):
                ins = dve.tensor_scalar(id_h2[:, h, :], ident, m_h2[:, h:h + 1], None, ALU.mult)
            ins.then_inc(s_rtc, 1)
            dve.tensor_copy(tri[:, :], cst[:, C_TRI:C_TRI + P]).then_inc(s_rtc, 1)
            dve.memset(ones[:, :], 1.0).then_inc(s_rtc, 1)
            dve.memset(gates[:, :, NE:NE + 1], 1.0)
            dve.memset(carry[:, 0, :], 0.0).then_inc(s_rtc, 1)
            dve.memset(pad[:, :], 0.0).then_inc(s_rtc, 1)
            dve.wait_ge(s_small, 80)
            dve.wait_ge(s_u, NG)
            dve.tensor_copy(pay[:, :, :, E + 1].bitcast(I32),
                            dst[:, 0:NG * TOPK].rearrange("p (g k) -> p g k", k=TOPK)).then_inc(s_rtc, 1)
            dve.wait_ge(s_rtc, 6)
            def gates_out(c):
                dve.wait_ge(s_gt, c + 1)
                if c >= 2:
                    dve.wait_ge(s_ye, c - 1)
                dve.tensor_copy(gT[:, c % 2, :], bank[6][0:NE + 1, :]).then_inc(s_gT, 1)

            def shared_result(c):
                dve.wait_ge(s_ye, c + 1)
                dve.scalar_tensor_tensor(out=acc[:, 4 * c:4 * c + 4, :],
                                         in0=x2[:, 4 * c:4 * c + 4, :], scalar=2.0,
                                         in1=bank[(4, 7)[c % 2]].rearrange("p (g e) -> p g e", e=E),
                                         op0=ALU.mult, op1=ALU.add).then_inc(s_acc, 1)

            for i in range(STEPS2):
                if i == 0:
                    head_max(0)
                if 1 <= i < NP + 1:
                    head_sum(i - 1)
                if i + 1 < NP:
                    head_max(i + 1)
                if i - 1 in TURN:
                    ln2_apply(TURN.index(i - 1))
                if i - 2 in TURN[:2]:
                    route_logits(TURN.index(i - 2))
                if i - 3 in TURN[:2]:
                    route_top(TURN.index(i - 3))
                    route_slots(TURN.index(i - 3))
                if i in TURN:
                    ln2_stats(TURN.index(i))
            gates_out(0)
            route_logits(2)
            route_top(2)
            route_slots(2)
            shared_result(0)
            ln2_stats(3)
            gates_out(1)
            ln2_apply(3)
            shared_result(1)
            gates_out(2)
            route_logits(3)
            route_top(3)
            route_slots(3)

            dve.wait_ge(s_cnt, 1)
            routed(dve.tensor_copy(cnt[:, :], bank[5][:, 64:64 + NE]))
            routed(dve.tensor_tensor(rank[:, 0, :], cnt[:, :], kr[:, K_BASE:K_BASE + NE], ALU.add))
            dve.tensor_copy(ends[:, :], rank[:, 0, :]).then_inc(s_ends, 1)
            shared_result(2)
            gates_out(3)
            NJ = T // P
            routed(dve.tensor_tensor(big[:, 0:NE * NJ].rearrange("p (e j) -> p e j", j=NJ),
                                     cnt[0:1, :].unsqueeze(2).broadcast_to([1, NE, NJ]),
                                     kr[0:1, K_J:K_J + NJ].unsqueeze(1).broadcast_to([1, NE, NJ]), ALU.is_gt))
            routed(dve.tensor_reduce(nt[0:1, :], big[:, 0:NE * NJ].rearrange("p (e j) -> p e j", j=NJ), AX_X, ALU.add))
            routed(dve.tensor_tensor(big[:, 0:NE * NE].rearrange("p (e j) -> p e j", j=NE),
                                     nt[0:1, :].unsqueeze(1).broadcast_to([1, NE, NE]),
                                     kr[0:1, K_L:K_END].rearrange("p (e j) -> p e j", j=NE), ALU.mult))
            routed(dve.tensor_reduce(cnt[0:1, :], big[:, 0:NE * NE].rearrange("p (e j) -> p e j", j=NE), AX_X, ALU.add))
            big_te = big[:, 0:NT * NE].rearrange("p (t e) -> p t e", e=NE)
            routed(dve.tensor_tensor(big_te, cnt[0:1, :].unsqueeze(1).broadcast_to([1, NT, NE]),
                                     kr[0:1, K_T:K_T + NT].unsqueeze(2).broadcast_to([1, NT, NE]), ALU.is_le))
            routed(dve.tensor_reduce(te[0:1, :], big_te, AX_X, ALU.add))
            routed(dve.tensor_tensor(big_te, big_te, nt[0:1, :].unsqueeze(1).broadcast_to([1, NT, NE]), ALU.mult))
            routed(dve.tensor_reduce(tprev[0:1, :], big_te, AX_X, ALU.add))
            routed(dve.scalar_tensor_tensor(out=tprev[0:1, :], in0=tprev[0:1, :], scalar=-float(P),
                                            in1=kr[0:1, K_TP:K_TP + NT], op0=ALU.mult, op1=ALU.add))
            routed(dve.scalar_tensor_tensor(out=tprev[0:1, :], in0=te[0:1, :], scalar=float(ROOM),
                                            in1=tprev[0:1, :], op0=ALU.mult, op1=ALU.add))
            routed(dve.tensor_scalar(tprev[0:1, :], tprev[0:1, :], float(NE * ROOM), None, ALU.min))
            routed(dve.tensor_copy(t_row[:, :], tprev[0:1, :]))
            dve.tensor_copy(t_expert[:, :], te[0:1, :]).then_inc(s_tab, 1)

            shared_result(3)
            dve.wait_ge(s_tab, 1)
            for i in range(-2, NT):
                if i >= 0 and i % 4 == 0:
                    for t in range(i, i + 4):
                        dve.wait_ge(s_xin[t % NB], 16 * (t // NB + 1))
                    dve.tensor_tensor(idx[:, i:i + 4], xin[:, i % NB:i % NB + 4, E + 1].bitcast(I32),
                                      dst[:, NG * TOPK + i:NG * TOPK + i + 4], ALU.max).then_inc(s_idx, 1)
                if i >= 0:
                    t = i
                    dve.wait_ge(s_xit, t + 1)
                    if t >= 2:
                        dve.wait_ge(s_hl, t - 1)
                    dve.tensor_copy(xinT[:, t % 2, :], bank[t % 2][:, 0:P]).then_inc(s_xiT, 1)
                if i + 2 < NT:
                    t = i + 2
                    if t % 4 == 0:
                        expert_of = nc.values_load_multi_w_load_instructions(
                            t_expert[0:1, t:t + 4], engines=[mybir.EngineType.DVE], min_val=0, max_val=NE)[1]
                    if t >= 5:
                        dve.wait_ge(s_yo, t - 4)
                    dve.tensor_copy(stage[:, t % 5, :],
                                    ew[:, bass.ds(expert_of[t % 4], 1), :].rearrange("p a b -> p (a b)")).then_inc(s_stage, 1)

            for c in range(NC + 1):
                if c < NC:
                    a = acc[:, 4 * c:4 * c + 4, :]
                    dve.wait_ge(s_ytl[c], 16 * TOPK)
                    for k in range(TOPK):
                        dve.tensor_tensor(a, a, routed_y[k][:, 4 * c:4 * c + 4, :], ALU.add).then_inc(s_sum3, 1)
                        dve.wait_ge(s_sum3, TOPK * c + k + 1)
                    for j in range(4):
                        ins = dve.bn_stats(bst3[:, 4 * c + j, :], acc[:, 4 * c + j, :])
                    ins.then_inc(s_l3, 1)
                    dve.wait_ge(s_l3, 2 * c + 1)
                    for j in range(4):
                        ins = dve.bn_aggr(mv3[:, 4 * c + j, :], bst3[:, 4 * c + j, :])
                    ins.then_inc(s_l3, 1)
                if c >= 1:
                    dve.wait_ge(s_rstd3, 2 * c)
                    for j in range(4):
                        g = 4 * (c - 1) + j
                        ins = dve.tensor_scalar(acc[:, g, :], acc[:, g, :], mv3[:, g, 0:1], rstd3[:, g:g + 1],
                                                ALU.subtract, ALU.mult)
                    ins.then_inc(s_fin, 1)

        @block.gpsimd
        def _(pool):
            pool.memset(vm[:, B // 2:B, :].rearrange("p b e -> p (b e)"), 0.0).then_inc(s_zero_p, 1)
            pool.memset(half[:, :], -0.5)
            pool.wait_ge(s_xn, 16)
            pool.wait_ge(s_brow, 16)
            pool.tensor_tensor(xn[:, :, :], xn[:, :, :],
                               brow[:, R_BO:R_BO + E].unsqueeze(1).broadcast_to([P, NG, E]), ALU.add).then_inc(s_xb, 1)

            def normalise(g):
                pool.wait_ge(s_recip, 2 * (g + 1))
                pool.tensor_tensor(ex[:, g % 3, :].rearrange("p (a t) -> p a t", t=S),
                                   ex[:, g % 3, :].rearrange("p (a t) -> p a t", t=S),
                                   rs[:, g % 2, :].unsqueeze(2).broadcast_to([P, 16, S]), ALU.mult).then_inc(s_pn, 1)

            def rsqrt1(c):
                pool.wait_ge(s_ln1, 3 * (c + 1))
                pool.tensor_scalar(rstd[:, c % 2, :], mv[:, c % 2, :, 1], EPS, None, ALU.add).then_inc(s_rstd, 1)
                pool.wait_ge(s_rstd, 2 * (c + 1) - 1)
                pool.tensor_tensor(rstd[:, c % 2, :], rstd[:, c % 2, :], half[:, :], ALU.pow).then_inc(s_rstd, 1)

            def v_apart(p):
                pool.wait_ge(s_kvl[p // 4], 256)
                pool.tensor_tensor(vx[:, p, :, :, :],
                                   kv[:, 1, p, :].rearrange("p (j c) -> p j c", j=8).unsqueeze(2).broadcast_to([P, 8, 2, 16]),
                                   m_n2.unsqueeze(1).unsqueeze(3).broadcast_to([P, 8, 2, 16]), ALU.mult).then_inc(s_vx, 1)

            def x1_out(g):
                pool.wait_ge(s_x1, g + 1)
                pool.dma_start(x1_scr.rearrange("(s b) e -> b s e", b=B)[4 * g:4 * g + 4, :, :],
                               res[:, g // 4 % 2, g % 4, :]).then_inc(s_x1st[g // 4 % 2], 16)

            def normalise2(p):
                pool.wait_ge(s_recip2, 2 * (p + 1))
                pool.tensor_tensor(e2[:, p % 3, :].rearrange("p (h t) -> p h t", t=B),
                                   e2[:, p % 3, :].rearrange("p (h t) -> p h t", t=B),
                                   r2[:, p % 2, :].unsqueeze(1).broadcast_to([P, 16, B]), ALU.mult).then_inc(s_pn2, 1)

            def x1_biased(c):
                pool.wait_ge(s_x1l[c], 16)
                pool.tensor_tensor(x1[:, 4 * c:4 * c + 4, :], x1[:, 4 * c:4 * c + 4, :],
                                   brow[:, R_XO:R_XO + E].unsqueeze(1).broadcast_to([P, 4, E]), ALU.add).then_inc(s_xb2, 1)

            def rsqrt2(c):
                pool.wait_ge(s_ln2, 3 * (c + 1))
                pool.tensor_scalar(rstd2[:, c % 2, :], mv2[:, c % 2, :, 1], EPS, None, ALU.add).then_inc(s_rstd2, 1)
                pool.wait_ge(s_rstd2, 2 * (c + 1) - 1)
                pool.tensor_tensor(rstd2[:, c % 2, :], rstd2[:, c % 2, :], half[:, :], ALU.pow).then_inc(s_rstd2, 1)

            for i in range(1, NG + 4):
                if i <= NG:
                    normalise(i - 1)
                if i >= 8 and i % 4 == 0:
                    rsqrt1(i // 4 - 2)
                if i >= 6:
                    v_apart(i - 6)
                if i >= 10:
                    x1_out(i - 10)
            rsqrt1(NC - 1)
            for g in range(NG - 6, NG):
                x1_out(g)
            for p in range(NG - 2, NP):
                v_apart(p)
            def scatter(c):
                pool.wait_ge(s_slot, 3 * c + 3)
                pool.wait_ge(s_pay, 2 * c + 2)
                for g in range(4 * c, 4 * c + 4):
                    for k in range(TOPK):
                        pool.indirect_dma_start(out=x_srt, out_offset=bass.IndirectOffsetOnAxis(
                            ap=slot[:, TOPK * g + k:TOPK * g + k + 1], axis=0),
                            in_=pay[:, g, k, :], in_offset=None).then_inc(s_scat, 16)

            for c in range(NC):
                x1_biased(c)
            for i in range(1, STEPS2):
                if i <= NP:
                    normalise2(i - 1)
                if i in TURN:
                    rsqrt2(TURN.index(i))
            scatter(0)
            scatter(1)
            rsqrt2(3)
            scatter(2)
            scatter(3)
            for t in range(NT):
                pool.wait_ge(s_yl, t + 1)
                pool.wait_ge(s_idx, t // 4 + 1)
                pool.indirect_dma_start(out=y_tok, out_offset=bass.IndirectOffsetOnAxis(
                    ap=idx[:, t:t + 1].bitcast(mybir.dt.uint32), axis=0),
                    in_=yl[:, t % NB, :], in_offset=None).then_inc(s_ysc[t % NB], 16)
            for c in range(NC):
                pool.wait_ge(s_l3, 2 * c + 2)
                pool.tensor_scalar(rstd3[:, 4 * c:4 * c + 4], mv3[:, 4 * c:4 * c + 4, 1], EPS, None, ALU.add).then_inc(s_rstd3, 1)
                pool.wait_ge(s_rstd3, 2 * (c + 1) - 1)
                pool.tensor_tensor(rstd3[:, 4 * c:4 * c + 4], rstd3[:, 4 * c:4 * c + 4], half[:, :], ALU.pow).then_inc(s_rstd3, 1)


def layout(inputs):
    import numpy as np

    def f(name):
        return np.asarray(inputs[name])

    x, c = f("x"), f("ctx_1024")
    p = np.arange(P)
    w_in = f("L0_attn_in_proj_w").T
    a = {}
    a["x_t"] = x.transpose(2, 1, 0).reshape(E, T)
    a["x_n"] = x.transpose(1, 0, 2).reshape(NG, P, E).transpose(1, 0, 2)
    a["ctx_t"] = c.reshape(T, E).T
    a["w_pack"] = np.concatenate([w_in, f("L0_attn_out_proj_w").T, f("L0_xattn_Wq"), f("L0_xattn_Wk"),
                                  f("L0_xattn_Wv"), f("L0_xattn_Wo")], axis=1)
    a["c_pack"] = np.concatenate(
        [np.eye(P)] + [(p // 32 == g)[:, None] for g in range(4)] + [((p // 8) % 4 == h)[:, None] for h in range(4)]
        + [(p // 64 == n)[:, None] for n in range(2)] + [((p // 8) % 2 == h)[:, None] for h in range(2)]
        + [p[:, None] < p[None, :]],
        axis=1).astype(np.float32)
    bi = f("L0_attn_in_proj_b")
    a["b_col"] = np.stack([bi[0:E], bi[E:2 * E], bi[2 * E:3 * E], bi[0:E]], axis=1)
    a["b_row"] = np.concatenate([f("L0_attn_out_proj_b"), f("L0_xattn_bq"), f("L0_xattn_bk"), f("L0_xattn_bv"),
                                 f("L0_xattn_bo")])
    w1 = np.concatenate([f("L0_ffn_rW1"), f("L0_ffn_sW1").reshape(E, 2, FE).transpose(1, 0, 2)])
    w2 = np.concatenate([f("L0_ffn_rW2"), f("L0_ffn_sW2").reshape(2, FE, E)])
    w2 = w2.reshape(NX, 2, P, E).transpose(0, 2, 1, 3).reshape(NX, P, 2 * E)
    b1 = np.concatenate([f("L0_ffn_rb1"), f("L0_ffn_sb1").reshape(2, FE)]).reshape(NX, 2, P).transpose(0, 2, 1)
    a["e_w"] = np.concatenate([w1, w2, b1], axis=2)
    a["e_b2"] = np.concatenate([f("L0_ffn_rb2"), f("L0_ffn_sb2")])
    a["g_w"] = f("L0_ffn_gW")
    a["g_b"] = f("L0_ffn_gb")
    e, t = np.arange(NE), np.arange(NT)
    a["k_row"] = np.concatenate([e, ROOM * e, t, P * t, P * np.arange(T // P),
                                 (e[None, :] <= e[:, None]).ravel()]).astype(np.float32)
    rows = NT * P + np.arange(TOPK)[None, None, :] * T + P * np.arange(NG)[None, :, None] + p[:, None, None]
    a["dst_rows"] = np.concatenate([rows.reshape(P, NG * TOPK), P * t[None, :] + p[:, None]], axis=1).astype(np.int32)
    return {k: np.ascontiguousarray(v) for k, v in a.items()}


def kernel(**inputs):
    import numpy as np
    import concourse.bacc as bacc
    from concourse.bass_utils import run_bass_kernel_spmd

    nc = bacc.Bacc("TRN2", target_bir_lowering=False, num_devices=1)
    arrays = layout(inputs)
    args = [nc.dram_tensor(n, a.shape, mybir.dt.from_np(a.dtype), kind="ExternalInput").ap()
            for n, a in arrays.items()]
    out = nc.dram_tensor("out", (S, B, E), F32, kind="ExternalOutput").ap()
    build(nc, *args, out)
    r = run_bass_kernel_spmd(nc, [arrays], core_ids=[0])
    return r.results[0]["out"]
```

```python
from contextlib import ExitStack

import concourse.bass as bass
from concourse import mybir

F32 = mybir.dt.float32
I32 = mybir.dt.int32
BF16 = mybir.dt.bfloat16
ALU = mybir.AluOpType
ACT = mybir.ActivationFunctionType
AX_X = mybir.AxisListType.X

P = 128
E = 128
S, B = 32, 64
T = S * B
NG = T // P
NC = 4
D = 8
NP = NG
STEPS1 = NG + 8
STEPS2 = NP + 3
TURN = (10, 14)
EPS = 1e-5

W_Q, W_K, W_V, W_O, X_Q, X_K, X_V, X_O = (i * E for i in range(8))
C_ID = 0
C_HG = 128
C_H4 = 132
C_N2 = 136
C_TRI = 138
C_END = C_TRI + P
R_BO, R_XQ, R_XK, R_XV, R_XO = (i * E for i in range(5))
R_END = 5 * E

NE = 15
FE = 256
NX = NE + 2
TOPK = 3
EW = FE + 2 * E + 2
ROOM = T + P
NT = (TOPK * T + NE * (P - 1)) // P
TABLE = NT + -NT % 4
NB = 8
NS = 5
XW = E + 2
ROWS = NE * ROOM + P
K_IOTA, K_BASE, K_T, K_TP, K_J = 0, NE, 2 * NE, 2 * NE + TABLE, 2 * NE + 2 * TABLE
K_L = K_J + T // P
K_END = K_L + NE * NE


def build(nc, x_t, x_n, ctx_t, w_pack, c_pack, b_col, b_row, e_w, e_b2, g_w, g_b, k_row, dst_rows, out):
    v_scr = nc.dram_tensor("v_scr", [T, E], F32).ap()
    x1_scr = nc.dram_tensor("x1_scr", [T, E], F32).ap()
    ck_scr = nc.dram_tensor("ck_scr", [T * E], F32).ap()
    cv_scr = nc.dram_tensor("cv_scr", [T * E], F32).ap()
    cq_scr = nc.dram_tensor("cq_scr", [T * E], F32).ap()
    o_scr = nc.dram_tensor("o_scr", [T * E], F32).ap()
    x_srt = nc.dram_tensor("x_srt", [ROWS, XW], F32).ap()
    y_tok = nc.dram_tensor("y_tok", [NT * P + TOPK * T, E], F32).ap()

    with ExitStack() as ctx:
        def sb(name, shape, dt=F32):
            return ctx.enter_context(nc.sbuf_tensor(name, shape, dt))

        def sem(name):
            return ctx.enter_context(nc.semaphore(name))

        psum = ctx.enter_context(nc.psum_tensor("psum", [P, 8 * 512], F32))
        bank = [psum[:, 512 * i:512 * i + 512] for i in range(8)]

        weights = sb("weights", [P, 8 * E])
        consts = sb("consts", [P, C_END])
        bias_cols = sb("bias_cols", [P, 3])
        bias_rows = sb("bias_rows", [P, R_END])
        neg_id = sb("neg_id", [P, P], BF16)
        bias_k_masked = sb("bias_k_masked", [P, 4])
        bias_q_masked = sb("bias_q_masked", [P, 4])
        w_out_masked = sb("w_out_masked", [P, 4, E])
        minus_half = sb("minus_half", [P, 4])

        xT = sb("xT", [P, T])
        x_rows = sb("x_rows", [P, NG, E])
        ctxT = sb("ctxT", [P, T])
        v_rows = sb("v_rows", [P, NG, E])
        v_blocks = sb("v_blocks", [P, B, E])
        q_heads = sb("q_heads", [P, 2, 16, 128])
        k_heads = sb("k_heads", [P, 2, 4, 512])
        maxes = sb("maxes", [P, 2, 16], BF16)
        probs = sb("probs", [P, 3, 512])
        prob_sums = sb("prob_sums", [P, 2, 16])
        inv_sums = sb("inv_sums", [P, 2, 16])
        probs_turned = sb("probs_turned", [P, 2, 512])
        head_out = sb("head_out", [P, 2, 512])
        x1_pre = sb("x1_pre", [P, 2, 4, E])
        bn1 = sb("bn1", [P, 2, 4, 6])
        mean_var1 = sb("mean_var1", [P, 2, 4, 2])
        rstd1 = sb("rstd1", [P, 2, 4])

        ctx_kv = sb("ctx_kv", [P, 2, NP, E])
        v_pairs = sb("v_pairs", [P, NP, 8, 2, 16])
        maxes2 = sb("maxes2", [P, 2, B], BF16)
        prob_sums2 = sb("prob_sums2", [P, 2, B])
        inv_sums2 = sb("inv_sums2", [P, 2, B])
        x2_pre = sb("x2_pre", [P, 2, 4, E])
        bn2 = sb("bn2", [P, 2, 4, 6])
        mean_var2 = sb("mean_var2", [P, 2, 4, 2])
        rstd2 = sb("rstd2", [P, 2, 4])
        expert_w = sb("expert_w", [P, NX, EW])
        expert_b2 = sb("expert_b2", [NE + 1, E])
        router_w = sb("router_w", [P, NE])
        router_b = sb("router_b", [P, NE])
        row_consts = sb("row_consts", [P, K_END])
        result_rows = sb("result_rows", [P, NG * TOPK + TABLE], I32)
        tri = sb("tri", [P, P], BF16)
        ones = sb("ones", [P, P], BF16)
        pad = sb("pad", [P, XW])
        router_probs = sb("router_probs", [P, 4, NE])
        chosen = sb("chosen", [P, NG, NE], BF16)
        chosen_sum = sb("chosen_sum", [P, NE])
        carry = sb("carry", [P, NC + 1, NE], BF16)
        sorted_rank = sb("sorted_rank", [P, 4, NE])
        selected = sb("selected", [P, 4 * TOPK, NE])
        y_rows = sb("y_rows", [P, TABLE], I32)
        slot = sb("slot", [P, NG * TOPK], mybir.dt.uint32)
        counts = sb("counts", [P, NE])
        ends = sb("ends", [P, NE], I32)
        tiles_of = sb("tiles_of", [P, NE])
        tile_expert_f = sb("tile_expert_f", [P, TABLE])
        tile_row_f = sb("tile_row_f", [P, TABLE])
        t_expert = sb("t_expert", [1, TABLE], I32)
        t_row = sb("t_row", [1, TABLE], I32)
        logit_max = sb("logit_max", [P, NG])
        logit_sum = sb("logit_sum", [P, NG])
        top_gates = sb("top_gates", [P, 4, 8])
        top_experts = sb("top_experts", [P, 4, 8], mybir.dt.uint32)
        one_hot = sb("one_hot", [P, 4, TOPK, NE])
        gates = sb("gates", [P, NG, NE + 1])
        mean_var3 = sb("mean_var3", [P, NG, 2])
        bn3 = sb("bn3", [P, NG, 6])
        rstd3 = sb("rstd3", [P, NG])
        nmean3 = slot[:, 0:NG].bitcast(F32)
        x1 = xT[:, :].rearrange("p (g e) -> p g e", e=E)
        cq_rows = v_rows
        q_heads_room = q_heads[:, :, :, :].rearrange("p a b c -> p (a b c)")
        k_heads_room = k_heads[:, :, :, :].rearrange("p a b c -> p (a b c)")
        v_blocks_room = v_blocks[:, :, :].rearrange("p b e -> p (b e)")
        o_rowsT = q_heads_room[:, 0:1024].rearrange("p (a b) -> p a b", a=2)
        x1T = x_rows[:, :, :].rearrange("p (c g) e -> p c (g e)", c=NC)
        k_heads2 = q_heads_room[:, 1024:2048].rearrange("p (a h b) -> p a h b", a=2, h=4)
        q_heads2 = q_heads_room[:, 2048:3072].rearrange("p (a h b) -> p a h b", a=2, h=4)
        out_cols = q_heads_room[:, 3072:3584].rearrange("p (a b) -> p a b", a=2)
        out_rows = q_heads_room[:, 3584:4096].rearrange("p (a b) -> p a b", a=2)
        qT = k_heads_room[:, 3072:3328].rearrange("p (a b) -> p a b", a=2)
        probs2 = k_heads_room[:, 0:3072].rearrange("p (a b) -> p a b", a=3)
        o_rows = v_blocks_room[:, NG * TOPK * XW:NG * TOPK * XW + 8 * E].rearrange("p (g e) -> p g e", e=E)
        payloads = v_blocks_room[:, 0:NG * TOPK * XW].rearrange("p (g k e) -> p g k e", g=NG, k=TOPK)
        x2 = payloads[:, :, 0, 0:E]
        cq_proj = x2_pre
        acc = xT[:, :].rearrange("p (g e) -> p g e", e=E)
        ctx_kv_room = ctx_kv[:, :, :, :].rearrange("p h g e -> p (h g e)")
        v_pairs_room = v_pairs[:, :, :, :, :].rearrange("p g a b c -> p (g a b c)")
        routed_y = [ctx_kv_room[:, 0:2048].rearrange("p (g e) -> p g e", e=E),
                    ctx_kv_room[:, 2048:4096].rearrange("p (g e) -> p g e", e=E),
                    v_pairs_room[:, 0:2048].rearrange("p (g e) -> p g e", e=E)]
        x2T = ctxT
        gatesT = ctx_kv_room[0:NE + 1, 3072:4096].rearrange("p (a b) -> p a b", a=2)
        x_rows_room = x_rows[:, :, :].rearrange("p g e -> p (g e)")
        h_shared = x_rows_room[:, 0:2048].rearrange("p (a b c) -> p a b c", a=2, b=2)
        table_room = k_heads_room[0:1, 3072:3072 + TABLE * NE]
        stage = ctx_kv_room[:, 0:NS * EW].rearrange("p (a b) -> p a b", a=NS)
        x_tile = k_heads_room[:, 0:NB * XW].rearrange("p (a b) -> p a b", a=NB)
        o = NB * XW
        x_tileT = k_heads_room[:, o:o + 2 * P].rearrange("p (a b) -> p a b", a=2)
        o += 2 * P
        h_tile = k_heads_room[:, o:o + 4 * P].rearrange("p (a f b) -> p a f b", a=2, f=2)
        o += 4 * P
        y_tile = k_heads_room[:, o:o + NB * E].rearrange("p (a b) -> p a b", a=NB)
        ident = consts[:, C_ID:C_ID + P]
        m_n2 = consts[:, C_N2:C_N2 + 2]
        m_hg = consts[:, C_HG:C_HG + 4]
        m_h4 = consts[:, C_H4:C_H4 + 4]

        s_const = sem("s_const")
        s_xT = [sem(f"s_xT{c}") for c in range(NC)]
        s_x_rows = sem("s_x_rows")
        s_prep = sem("s_prep")
        s_x_biased = sem("s_x_biased")
        s_bias_rows = sem("s_bias_rows")
        s_v_zero = sem("s_v_zero")
        s_v_proj = sem("s_v_proj")
        s_v_rows = sem("s_v_rows")
        s_v_stored = [sem(f"s_v_stored{c}") for c in range(NC)]
        s_v_blocks = [sem(f"s_v_blocks{c}") for c in range(NC)]
        s_q_proj = sem("s_q_proj")
        s_k_proj = sem("s_k_proj")
        s_q_heads = sem("s_q_heads")
        s_k_heads = sem("s_k_heads")
        s_scores = sem("s_scores")
        s_maxes = sem("s_maxes")
        s_shifted = sem("s_shifted")
        s_exps = sem("s_exps")
        s_inv_sums = sem("s_inv_sums")
        s_probs = sem("s_probs")
        s_probs_turned = sem("s_probs_turned")
        s_head_psum = sem("s_head_psum")
        s_head_out = sem("s_head_out")
        s_attn_proj = sem("s_attn_proj")
        s_ln1 = sem("s_ln1")
        s_rstd1 = sem("s_rstd1")
        s_x1 = sem("s_x1")
        s_x1_stored = [sem(f"s_x1_stored{c}") for c in range(2)]

        s_expert_w = sem("s_expert_w")
        s_small = sem("s_small")
        s_router_ready = sem("s_router_ready")
        s_x2_turned = sem("s_x2_turned")
        s_x2T = sem("s_x2T")
        s_logits = sem("s_logits")
        s_logits_shifted = sem("s_logits_shifted")
        s_logit_exps = sem("s_logit_exps")
        s_routed = sem("s_routed")
        s_chosen = sem("s_chosen")
        s_ranks = sem("s_ranks")
        s_slots = sem("s_slots")
        s_payloads = sem("s_payloads")
        s_scattered = sem("s_scattered")
        s_counts = sem("s_counts")
        s_ends = sem("s_ends")
        s_filled = sem("s_filled")
        s_tables = sem("s_tables")
        s_x_tile = [sem(f"s_x_tile{k}") for k in range(NB)]
        s_tile_turned = sem("s_tile_turned")
        s_x_tileT = sem("s_x_tileT")
        s_staged = sem("s_staged")
        s_tile_psum = sem("s_tile_psum")
        s_h_tile = sem("s_h_tile")
        s_tile_out = sem("s_tile_out")
        s_y_rows = sem("s_y_rows")
        s_y_tile = sem("s_y_tile")
        s_y_scattered = [sem(f"s_y_scattered{k}") for k in range(NB)]
        s_y_loaded = [sem(f"s_y_loaded{c}") for c in range(NC)]
        s_y_sum = sem("s_y_sum")
        s_y12 = sem("s_y12")
        s_y3 = sem("s_y3")
        s_gates = sem("s_gates")
        s_gates_turned = sem("s_gates_turned")
        s_gatesT = sem("s_gatesT")
        s_acc = sem("s_acc")
        s_shared_psum = sem("s_shared_psum")
        s_h_shared = sem("s_h_shared")
        s_shared_out = sem("s_shared_out")
        s_ln3 = sem("s_ln3")
        s_rstd3 = sem("s_rstd3")
        s_final = sem("s_final")
        s_out = sem("s_out")
        s_ctx = sem("s_ctx")
        s_ctx_proj = sem("s_ctx_proj")
        s_ctx_kv = sem("s_ctx_kv")
        s_ctx_stored = [sem(f"s_ctx_stored{c}") for c in range(NC)]
        s_ctx_loaded = [sem(f"s_ctx_loaded{c}") for c in range(NC)]
        s_v_pairs = sem("s_v_pairs")
        s_x1_loaded = [sem(f"s_x1_loaded{c}") for c in range(NC)]
        s_x1_turned = sem("s_x1_turned")
        s_x1T = sem("s_x1T")
        s_cq_proj = sem("s_cq_proj")
        s_cq = sem("s_cq")
        s_cq_stored = [sem(f"s_cq_stored{c}") for c in range(NC)]
        s_cq_loaded = [sem(f"s_cq_loaded{p}") for p in range(NP // 2)]
        s_kq_turned = sem("s_kq_turned")
        s_kq_copied = sem("s_kq_copied")
        s_q_heads2 = sem("s_q_heads2")
        s_scores2 = sem("s_scores2")
        s_maxes2 = sem("s_maxes2")
        s_shifted2 = sem("s_shifted2")
        s_exps2 = sem("s_exps2")
        s_inv_sums2 = sem("s_inv_sums2")
        s_probs2 = sem("s_probs2")
        s_out_psum = sem("s_out_psum")
        s_out_cols = sem("s_out_cols")
        s_out_turned = sem("s_out_turned")
        s_out_rows = sem("s_out_rows")
        s_o_stored = [sem(f"s_o_stored{k}") for k in range(2)]
        s_o_loaded = [sem(f"s_o_loaded{c}") for c in range(NC)]
        s_o_turned = sem("s_o_turned")
        s_o_rowsT = sem("s_o_rowsT")
        s_cross_proj = sem("s_cross_proj")
        s_x1_biased = sem("s_x1_biased")
        s_ln2 = sem("s_ln2")
        s_rstd2 = sem("s_rstd2")
        s_x2 = sem("s_x2")

        block = ctx.enter_context(nc.Block())
        SP = mybir.EngineType.SP
        SCALE1 = float(D) ** -0.5
        SCALE2 = float(E) ** -0.5
        CTX_STEPS = (1, 2, 3, 5, 6, 7, 9, 10)
        CHAIN_BANK = (5, 5, 6, 7)
        GATE_BANK = (4, 5, 5, 5)

        def km_count(p, q_too):
            if p < 2:
                return p + 1 + 2 * q_too
            return p + 3

        def by_token(scratch, n):
            return scratch[n * B * E:(n + 1) * B * E].rearrange("(h t d) -> t h d", t=B, d=D)

        def by_row(scratch):
            return scratch.rearrange("(g p e) -> p g e", p=P, e=E)

        @block.sync
        def _(sp):
            sp.dma_start(weights[:, 0:4 * E], w_pack[:, 0:4 * E]).then_inc(s_const, 16)
            for c in range(NC):
                sp.dma_start(xT[:, 512 * c:512 * c + 512], x_t[:, 512 * c:512 * c + 512]).then_inc(s_xT[c], 16)
            sp.dma_start(x_rows[:, :, :], x_n).then_inc(s_x_rows, 16)
            sp.dma_start(weights[:, 4 * E:8 * E], w_pack[:, 4 * E:8 * E]).then_inc(s_ctx, 16)
            sp.dma_start(ctxT[:, :], ctx_t).then_inc(s_ctx, 16)

            def v_stored(c):
                sp.wait_ge(s_v_rows, c + 1)
                sp.dma_start(v_scr.rearrange("(g p) e -> p g e", p=P)[:, 4 * c:4 * c + 4, :],
                             v_rows[:, 4 * c:4 * c + 4, :]).then_inc(s_v_stored[c], 16)

            def v_by_batch(c):
                sp.wait_ge(s_v_stored[c], 16)
                for g in range(4):
                    src = v_scr.rearrange("(b t) e -> t b e", t=S)[:, 16 * c:16 * c + 16, 32 * g:32 * g + 32]
                    sp.dma_start(v_blocks[32 * g:32 * g + 32, 16 * c:16 * c + 16, 32 * g:32 * g + 32],
                                 src).then_inc(s_v_blocks[c], 16)

            v_stored(0)
            v_stored(1)
            sp.wait_ge(s_v_zero, 2)
            v_by_batch(0)
            v_stored(2)
            v_by_batch(1)
            v_stored(3)
            v_by_batch(2)
            v_by_batch(3)

            def kv_by_token(c):
                for h in range(2):
                    sp.wait_ge(s_ctx_kv, 2 * c + h + 1)
                    sp.dma_start(by_row((ck_scr, cv_scr)[h])[:, 4 * c:4 * c + 4, :],
                                 ctx_kv[:, h, 4 * c:4 * c + 4, :]).then_inc(s_ctx_stored[c], 16)
                sp.wait_ge(s_ctx_stored[c], 32)
                for p in range(4 * c, 4 * c + 4):
                    for h in range(2):
                        for n in range(2):
                            sp.dma_start(ctx_kv[64 * n:64 * n + 64, h, p, :].rearrange("t (h d) -> t h d", d=D),
                                         by_token((ck_scr, cv_scr)[h], 2 * p + n)).then_inc(s_ctx_loaded[c], 16)

            def cq_to_rows(c):
                sp.wait_ge(s_cq, c + 1)
                for j in range(4):
                    g = 4 * c + j
                    dst_rows = cq_scr.rearrange("(s b e) -> b s e", b=B, e=E)[4 * g:4 * g + 4, :, :]
                    sp.dma_start(dst_rows, cq_proj[:, c % 2, j, :]).then_inc(s_cq_stored[c], 16)

            kv_by_token(0)
            kv_by_token(1)
            kv_by_token(2)
            cq_to_rows(0)
            kv_by_token(3)
            for c in range(1, NC):
                cq_to_rows(c)
            for c in range(NC):
                sp.wait_ge(s_cq_stored[c], 64)
            for p in range(NP):
                for n in range(2):
                    sp.dma_start(cq_rows[64 * n:64 * n + 64, p, :].rearrange("t (h d) -> t h d", d=D),
                                 by_token(cq_scr, 2 * p + n)).then_inc(s_cq_loaded[p // 2], 16)
                if p == 3:
                    for c in range(2):
                        sp.wait_ge(s_x1_stored[c], 64 * NC // 2)
                    for c in range(NC):
                        sp.dma_start(x1[:, 4 * c:4 * c + 4, :],
                                     x1_scr.rearrange("(g p) e -> p g e", p=P)[:, 4 * c:4 * c + 4, :]).then_inc(s_x1_loaded[c], 16)
            sp.dma_start(expert_w[:, :, :], e_w.rearrange("x p f -> p x f")).then_inc(s_expert_w, 16)
            for p in range(NP + 1):
                if p < NP:
                    sp.wait_ge(s_out_rows, p + 1)
                    for n in range(2):
                        sp.dma_start(by_token(o_scr, 2 * p + n),
                                     out_rows[0:64, p % 2, 128 * n:128 * n + 128].rearrange("t (h d) -> t h d", d=D)
                                     ).then_inc(s_o_stored[p % 2], 16)
                if p >= 1:
                    sp.wait_ge(s_o_stored[(p - 1) % 2], 32 * ((p - 1) // 2 + 1))
                    if p - 1 >= 8:
                        sp.wait_ge(s_o_turned, (p - 1) // 4 - 1)
                    sp.dma_start(o_rows[:, (p - 1) % 8, :], by_row(o_scr)[:, p - 1, :]).then_inc(s_o_loaded[(p - 1) // 4], 16)
            sp.wait_ge(s_router_ready, 5)
            sp.dma_start(x_srt[NE * ROOM:ROWS, :], pad[:, :]).then_inc(s_filled, 16)
            sp.wait_ge(s_ends, 1)
            for e in range(0, NE, 4):
                k = min(4, NE - e)
                ends_of = nc.values_load_multi_w_load_instructions(
                    ends[0:1, e:e + k], engines=[SP], min_val=0, max_val=NE * ROOM - P,
                    skip_runtime_bounds_check_because="an expert has room for every token")[1]
                for j in range(k):
                    sp.dma_start(x_srt[bass.ds(ends_of[j], P), :], pad[:, :]).then_inc(s_filled, 16)
            sp.wait_ge(s_tables, 1)
            for t in range(NT):
                if t % 4 == 0:
                    row_of = nc.values_load_multi_w_load_instructions(
                        t_row[0:1, t:t + 4], engines=[SP], min_val=0, max_val=NE * ROOM,
                        skip_runtime_bounds_check_because="the table ends at the last tile's row")[1]
                if t == 0:
                    sp.wait_ge(s_filled, 16 * (NE + 1))
                    sp.wait_ge(s_scattered, 16 * NG * TOPK)
                if t >= NB:
                    sp.wait_ge(s_y_tile, t - NB + 1)
                    sp.wait_ge(s_y_rows, (t - NB) // 4 + 1)
                sp.dma_start(x_tile[:, t % NB, :], x_srt[bass.ds(row_of[t % 4], P), :]).then_inc(s_x_tile[t % NB], 16)
            for k in range(NB):
                sp.wait_ge(s_y_scattered[k], 16 * ((NT + NB - 1 - k) // NB))
            for c in range(NC):
                for k in range(TOPK):
                    sp.dma_start(routed_y[k][:, 4 * c:4 * c + 4, :],
                                 y_tok[NT * P:NT * P + TOPK * T, :].rearrange("(k g p) e -> k p g e", g=NG, p=P)[k][:, 4 * c:4 * c + 4, :]
                                 ).then_inc(s_y_loaded[c], 16)
            for c in range(NC):
                sp.wait_ge(s_final, c + 1)
                if c == NC - 1:
                    sp.wait_ge(s_y_sum, NC + 3)
                sp.dma_start(out.rearrange("s b e -> (s b) e").rearrange("(g p) e -> p g e", p=P)[:, 4 * c:4 * c + 4, :],
                             acc[:, 4 * c:4 * c + 4, :]).then_inc(s_out, 16)
            sp.wait_ge(s_out, 16 * NC)

        @block.tensor
        def _(pe):
            pe.wait_ge(s_const, 48)

            def proj_v(c):
                pe.wait_ge(s_xT[c], 16)
                if c >= 2:
                    pe.wait_ge(s_v_rows, c - 1)
                for j in range(4):
                    g = 4 * c + j
                    mm = pe.matmul(bank[6 + c % 2][:, E * j:E * j + E], xT[:, P * g:P * g + P], weights[:, W_V:W_V + E],
                                   start=True, stop=True)
                mm.then_inc(s_v_proj, 1)

            bank0_reader = [None]

            def bank0_free():
                if bank0_reader[0]:
                    pe.wait_ge(*bank0_reader[0])

            def proj_q(c):
                bank0_free()
                bank0_reader[0] = (s_q_heads, c + 1)
                pe.matmul(bank[0][:, :], weights[:, W_Q:W_Q + E], xT[:, 512 * c:512 * c + 512],
                          start=True, stop=True).then_inc(s_q_proj, 1)

            def proj_k(c):
                if c >= 1:
                    pe.wait_ge(s_k_heads, c)
                pe.matmul(bank[1][:, :], weights[:, W_K:W_K + E], xT[:, 512 * c:512 * c + 512],
                          start=True, stop=True).then_inc(s_k_proj, 1)

            def scores(g):
                c, j = g // 4, g % 4
                pe.wait_ge(s_q_heads, c + 1)
                pe.wait_ge(s_k_heads, c + 1)
                if g >= 2:
                    pe.wait_ge(s_exps, g - 1)
                for b in range(4):
                    o = 128 * j + 32 * b
                    mm = pe.matmul(bank[2 + g % 2][:, 128 * b:128 * b + 128], q_heads[:, c % 2, 4 * j + b, :],
                                   k_heads[:, c % 2, :, o:o + 32], start=(b == 0), stop=False, skip_group_check=True)
                mm.then_inc(s_scores, 1)

            def subtract_max(g):
                pe.wait_ge(s_maxes, g + 1)
                pe.matmul(bank[2 + g % 2][:, :], neg_id[:, :], maxes[:, g % 2, :].unsqueeze(2).broadcast_to([P, 16, 32]),
                          start=False, stop=True, skip_group_check=True).then_inc(s_shifted, 1)

            def weighted(g):
                pe.wait_ge(s_probs_turned, g + 1)
                pe.wait_ge(s_v_blocks[g // 4], 64)
                if g >= 2:
                    pe.wait_ge(s_head_out, g - 1)
                for b in range(4):
                    mm = pe.matmul(bank[4 + g % 2][:, 128 * b:128 * b + 128], v_blocks[:, 4 * g + b, :],
                                   probs_turned[:, g % 2, 128 * b:128 * b + 128], start=True, stop=True)
                mm.then_inc(s_head_psum, 1)

            def out_proj(g):
                c, j = g // 4, g % 4
                pe.wait_ge(s_head_out, g + 1)
                if g == 0:
                    pe.wait_ge(s_v_rows, NC)
                if j == 0 and c >= 2:
                    pe.wait_ge(s_cq, c - 1)
                u = head_out[:, g % 2, :].rearrange("p (h t) -> p h t", h=4)
                for h in range(4):
                    mm = pe.matmul(bank[6 + c % 2][:, E * j:E * j + E], u[:, h, :], w_out_masked[:, h, :],
                                   start=(h == 0), stop=(h == 3))
                mm.then_inc(s_attn_proj, 1)

            def proj_ctx(c):
                i, h = c // 2, c % 2
                bank0_free()
                bank0_reader[0] = (s_ctx_kv, c + 1)
                for j in range(4):
                    g = 4 * i + j
                    mm = pe.matmul(bank[0][:, E * j:E * j + E], ctxT[:, P * g:P * g + P],
                                   weights[:, (X_K, X_V)[h]:(X_K, X_V)[h] + E], start=True, stop=True)
                mm.then_inc(s_ctx_proj, 1)

            def x1_turned(c):
                pe.wait_ge(s_x1, 4 * c + 4)
                for j in range(4):
                    mm = pe.transpose(bank[6 + c % 2][:, P * j:P * j + P], x1_pre[:, c % 2, j, :], ident)
                mm.then_inc(s_x1_turned, 1)

            def proj_cq(c):
                pe.wait_ge(s_x1T, c + 1)
                for j in range(4):
                    mm = pe.matmul(bank[6 + c % 2][:, E * j:E * j + E], x1T[:, c, P * j:P * j + P],
                                   weights[:, X_Q:X_Q + E], start=True, stop=True)
                mm.then_inc(s_cq_proj, 1)

            pe.wait_ge(s_xT[0], 16)
            proj_q(0)
            proj_k(0)
            proj_v(0)
            proj_v(1)
            pe.wait_ge(s_prep, 3)
            for i in range(STEPS1):
                if i == 0:
                    scores(0)
                if i + 1 < NG:
                    scores(i + 1)
                if i == 0:
                    proj_v(2)
                if i < NG:
                    subtract_max(i)
                if i == 0:
                    proj_v(3)
                if 3 <= i < NG + 3:
                    weighted(i - 3)
                if i % 4 == 0 and i // 4 + 1 < NC:
                    proj_q(i // 4 + 1)
                if i % 4 == 1 and i // 4 + 1 < NC:
                    proj_k(i // 4 + 1)
                if i == CTX_STEPS[0]:
                    pe.wait_ge(s_ctx, 32)
                if i in CTX_STEPS:
                    proj_ctx(CTX_STEPS.index(i))
                if 4 <= i < NG + 4:
                    out_proj(i - 4)
                if i >= 10 and i % 4 == 2:
                    x1_turned(i // 4 - 2)
                if i >= 11 and i % 4 == 3:
                    proj_cq(i // 4 - 2)

            def k_turned(p):
                pe.wait_ge(s_ctx_loaded[p // 4], 256)
                if p >= 1:
                    pe.wait_ge(s_kq_copied, km_count(p - 1, p >= 2))
                ins = pe.transpose(bank[4][:, 0:P], ctx_kv[:, 0, p, :], ident)
                if p < 2:
                    ins.then_inc(s_kq_turned, 1)

            def q_turned(p):
                pe.wait_ge(s_cq_loaded[p // 2], 64)
                if p == 0:
                    pe.wait_ge(s_kq_copied, km_count(1, False))
                if p == 1:
                    pe.wait_ge(s_kq_copied, km_count(0, True))
                pe.transpose(bank[4][:, P:2 * P], cq_rows[:, p, :], ident).then_inc(s_kq_turned, 1)

            def scores2(p):
                pe.wait_ge(s_kq_copied, km_count(p, True))
                pe.wait_ge(s_q_heads2, p + 1)
                if p >= 2:
                    pe.wait_ge(s_exps2, p - 1)
                for h in range(4):
                    for n in range(2):
                        o = 256 * (h % 2)
                        mm = pe.matmul(bank[2 * (p % 2) + h // 2][64 * n:64 * n + 64, o:o + 256],
                                       k_heads2[:, p % 2, h, 64 * n:64 * n + 64], q_heads2[:, p % 2, :, 64 * n:64 * n + 64],
                                       start=(h % 2 == 0), stop=False, skip_group_check=True)
                mm.then_inc(s_scores2, 1)

            def subtract_max2(p):
                pe.wait_ge(s_maxes2, p + 1)
                for k in range(2):
                    mm = pe.matmul(bank[2 * (p % 2) + k], neg_id[:, :], maxes2[:, p % 2, :].unsqueeze(1).broadcast_to([P, 8, B]),
                                   start=False, stop=True, skip_group_check=True)
                mm.then_inc(s_shifted2, 1)

            def weighted2(p):
                pe.wait_ge(s_probs2, p + 1)
                pe.wait_ge(s_v_pairs, p + 1)
                if p >= 1:
                    pe.wait_ge(s_out_cols, p)
                for j in range(8):
                    mm = pe.matmul(bank[6][32 * (j % 4):32 * (j % 4) + 32, 128 * (j // 4):128 * (j // 4) + 128],
                                   v_pairs[:, p, j, :, :].rearrange("p a b -> p (a b)"), probs2[:, p % 3, 128 * j:128 * j + 128],
                                   start=True, stop=True)
                mm.then_inc(s_out_psum, 1)

            chain_reader = {}

            def chain_bank(c, reader):
                b = CHAIN_BANK[c]
                if b in chain_reader:
                    pe.wait_ge(*chain_reader[b])
                chain_reader[b] = reader
                return bank[b]

            def o_by_token(p):
                pe.wait_ge(s_out_cols, p + 1)
                if p >= 1:
                    pe.wait_ge(s_out_rows, p)
                for h in range(2):
                    for j in range(2):
                        mm = pe.transpose(bank[7][0:64, 2 * P * h + P * j:2 * P * h + P * j + P],
                                          out_cols[:, p % 2, P * j + B * h:P * j + B * h + B], ident)
                mm.then_inc(s_out_turned, 1)

            def orow_turned(c):
                pe.wait_ge(s_o_loaded[c], 64)
                bk = chain_bank(c, (s_o_rowsT, c + 1))
                for j in range(4):
                    mm = pe.transpose(bk[:, P * j:P * j + P], o_rows[:, (4 * c + j) % 8, :], ident)
                mm.then_inc(s_o_turned, 1)

            def out_proj2(c):
                bk = chain_bank(c, (s_ln2, 3 * c + 1))
                for j in range(4):
                    mm = pe.matmul(bk[:, E * j:E * j + E], o_rowsT[:, c % 2, P * j:P * j + P], weights[:, X_O:X_O + E],
                                   start=True, stop=True)
                mm.then_inc(s_cross_proj, 1)

            def x2_turned(c):
                pe.wait_ge(s_x2, 4 * c + 4)
                bk = chain_bank(c, (s_x2T, c + 1))
                for j in range(4):
                    mm = pe.transpose(bk[:, P * j:P * j + P], x2[:, 4 * c + j, :], ident)
                mm.then_inc(s_x2_turned, 1)

            def logits(c):
                bk = chain_bank(c, (s_logits_shifted, 3 * c + 1))
                for j in range(4):
                    g = 4 * c + j
                    mm = pe.matmul(bk[:, 16 * j:16 * j + NE], x2T[:, P * g:P * g + P], router_w[:, :], start=True, stop=True)
                mm.then_inc(s_logits, 1)

            def ranks(c):
                pe.wait_ge(s_chosen, c + 1)
                bk = chain_bank(c, (s_slots, 3 * c + 1))
                for j in range(4):
                    o = bk[:, 16 * j:16 * j + NE]
                    pe.matmul(o, tri[:, :], chosen[:, 4 * c + j, :], start=True, stop=False)
                    for i in range(j):
                        pe.matmul(o, ones[:, :], chosen[:, 4 * c + i, :], start=False, stop=False)
                    mm = pe.matmul(o, ones[:, :], carry[:, c, :], start=False, stop=True)
                mm.then_inc(s_ranks, 1)

            def gates_turned(c):
                pe.wait_ge(s_gates, c + 1)
                if c == 1:
                    pe.wait_ge(s_slots, 6)
                if c >= 2:
                    pe.wait_ge(s_gatesT, c)
                for j in range(4):
                    mm = pe.transpose(bank[GATE_BANK[c]][0:NE + 1, P * j:P * j + P], gates[:, 4 * c + j, :], ident)
                mm.then_inc(s_gates_turned, 1)

            def shared_in(k):
                c, h = k // 2, k % 2
                if k >= 2:
                    pe.wait_ge(s_h_shared, 2 * (k - 1))
                for a in range(2):
                    pe.matmul(bank[2 * (k % 2) + a], expert_w[:, NE + h, P * a:P * a + P], x2T[:, 512 * c:512 * c + 512],
                              start=True, stop=True).then_inc(s_shared_psum, 1)

            def shared_out(c, j):
                if j == 0:
                    pe.wait_ge(s_h_shared, 4 * c + 4)
                    pe.wait_ge(s_gatesT, c + 1)
                    if c >= 1:
                        pe.wait_ge(s_acc, c)
                o = bank[4][:, E * j:E * j + E]
                for k in range(2 * c, 2 * c + 2):
                    for a in range(2):
                        pe.matmul(o, h_shared[:, k % 2, a, P * j:P * j + P],
                                  expert_w[:, NE + k % 2, FE + E * a:FE + E * a + E], start=(k % 2 == 0 and a == 0), stop=False)
                mm = pe.matmul(o, gatesT[:, c % 2, P * j:P * j + P], expert_b2[:, :], start=False, stop=True)
                if j == 3:
                    mm.then_inc(s_shared_out, 1)

            pe.wait_ge(s_q_heads, NC)
            pe.wait_ge(s_k_heads, NC)
            pe.wait_ge(s_ctx_kv, 2 * NC)
            pe.wait_ge(s_exps, NG)
            pe.wait_ge(s_head_out, NG)
            pe.wait_ge(s_cq, NC)
            k_turned(0)
            k_turned(1)
            q_turned(0)
            q_turned(1)
            scores2(0)
            for i in range(STEPS2):
                if 3 <= i < NP + 3:
                    weighted2(i - 3)
                if i + 2 < NP:
                    k_turned(i + 2)
                    q_turned(i + 2)
                if i >= 4:
                    o_by_token(i - 4)
                if i + 1 < NP:
                    scores2(i + 1)
                if i < NP:
                    subtract_max2(i)
                for c, turn in enumerate(TURN):
                    if i == turn:
                        orow_turned(c)
                    if i == turn + 1:
                        out_proj2(c)
                    if i == turn + 3 and c == 0:
                        x2_turned(c)
                    if i == turn + 4 and c == 0:
                        logits(c)
                    if i == turn + 6:
                        ranks(c)

            def shared_outs(c, js):
                for j in js:
                    shared_out(c, j)

            o_by_token(NP - 1)
            pe.wait_ge(s_exps2, NP)
            pe.wait_ge(s_kq_copied, NP + 2)
            pe.wait_ge(s_out_cols, NP)
            x2_turned(1)
            orow_turned(2)
            logits(1)
            out_proj2(2)
            gates_turned(0)
            pe.wait_ge(s_expert_w, 16)
            shared_in(0)
            shared_in(1)
            pe.wait_ge(s_out_rows, NP)
            orow_turned(3)
            ranks(1)
            out_proj2(3)
            shared_outs(0, range(2))
            x2_turned(2)
            shared_outs(0, range(2, 3))
            logits(2)
            shared_outs(0, range(3, 4))
            shared_in(2)
            gates_turned(1)
            x2_turned(3)
            shared_in(3)
            logits(3)
            ranks(2)
            shared_outs(1, range(4))
            gates_turned(2)
            shared_in(4)
            shared_in(5)
            ranks(3)
            pe.matmul(bank[7][:, 64:64 + NE], ones[:, :], carry[:, NC, :], start=True, stop=True).then_inc(s_counts, 1)
            shared_outs(2, range(4))

            gates_turned(NC - 1)
            for k in (6, 7):
                shared_in(k)
            for j in range(4):
                shared_out(NC - 1, j)

            def tile_turned(t):
                pe.wait_ge(s_x_tile[t % NB], 16 * (t // NB + 1))
                if t >= 2:
                    pe.wait_ge(s_x_tileT, t - 1)
                pe.transpose(bank[t % 2][:, 0:P], x_tile[:, t % NB, 0:E], ident).then_inc(s_tile_turned, 1)

            def tile_in(t):
                pe.wait_ge(s_x_tileT, t + 1)
                pe.wait_ge(s_staged, t + 1)
                if t >= 2:
                    pe.wait_ge(s_h_tile, t - 1)
                for a in range(2):
                    mm = pe.matmul(bank[2 + t % 2][:, P * a:P * a + P], stage[:, t % NS, P * a:P * a + P],
                                   x_tileT[:, t % 2, :], start=True, stop=True)
                mm.then_inc(s_tile_psum, 1)

            def tile_out(t):
                pe.wait_ge(s_h_tile, t + 1)
                if t >= 2:
                    pe.wait_ge(s_y_tile, t - 1)
                for a in range(2):
                    mm = pe.matmul(bank[6 + t % 2][:, 0:E], h_tile[:, t % 2, a, :],
                                   stage[:, t % NS, FE + E * a:FE + E * a + E], start=(a == 0), stop=(a == 1))
                mm.then_inc(s_tile_out, 1)

            pe.wait_ge(s_h_shared, 4 * NC)
            for i in range(NT + 2):
                if i < NT:
                    tile_turned(i)
                if 1 <= i < NT + 1:
                    tile_in(i - 1)
                if i >= 2:
                    tile_out(i - 2)

            pe.wait_ge(s_y_tile, NT)
            pe.wait_ge(s_x_tileT, NT)
            for c in range(NC):
                pe.wait_ge(s_y_loaded[c], 16 * TOPK)
                for k in range(2):
                    mm = pe.matmul(bank[c], ident, routed_y[k][:, 4 * c:4 * c + 4, :].rearrange("p g e -> p (g e)"),
                                   start=(k == 0), stop=(k == 1))
                mm.then_inc(s_y12, 1)

        @block.scalar
        def _(act):
            act.dma_start(consts[:, :], c_pack).then_inc(s_const, 16)
            act.dma_start(bias_cols[:, :], b_col).then_inc(s_const, 16)
            act.dma_start(bias_rows[:, :], b_row.partition_broadcast(P)).then_inc(s_bias_rows, 16)
            act.dma_start(expert_b2[:, :], e_b2).then_inc(s_small, 16)
            act.dma_start(router_w[:, :], g_w).then_inc(s_small, 16)
            act.dma_start(router_b[:, :], g_b.partition_broadcast(P)).then_inc(s_small, 16)
            act.dma_start(row_consts[:, :], k_row.partition_broadcast(P)).then_inc(s_small, 16)
            act.dma_start(result_rows[:, :], dst_rows).then_inc(s_small, 16)

            def q_masked(c):
                act.wait_ge(s_q_proj, c + 1)
                if c >= 2:
                    act.wait_ge(s_scores, 4 * (c - 1))
                for h in range(4):
                    a = act.activation(q_heads[:, c % 2, :, 32 * h:32 * h + 32],
                                       bank[0][:, :].rearrange("p (b s) -> p b s", s=S), ACT.Identity,
                                       bias=bias_q_masked[:, h:h + 1], scale=m_hg[:, h:h + 1])
                a.then_inc(s_q_heads, 1)

            def k_masked(c):
                act.wait_ge(s_k_proj, c + 1)
                if c >= 2:
                    act.wait_ge(s_scores, 4 * (c - 1))
                for h in range(4):
                    a = act.activation(k_heads[:, c % 2, h, :], bank[1][:, :], ACT.Identity, bias=bias_k_masked[:, h:h + 1],
                                       scale=m_h4[:, h:h + 1])
                a.then_inc(s_k_heads, 1)

            def exps(g):
                act.wait_ge(s_shifted, g + 1)
                if g >= 3:
                    act.wait_ge(s_probs_turned, g - 2)
                act.activation(probs[:, g % 3, :], bank[2 + g % 2][:, :], ACT.Exp, scale=SCALE1).then_inc(s_exps, 1)

            def u_out(g):
                act.wait_ge(s_head_psum, g + 1)
                if g >= 2:
                    act.wait_ge(s_attn_proj, g - 1)
                act.activation(head_out[:, g % 2, :].rearrange("p (h b s) -> p b h s", h=4, b=4),
                               bank[4 + g % 2][:, :].rearrange("p (b h s) -> p b h s", b=4, h=4), ACT.Identity, bias=bias_cols[:, 2:3]).then_inc(s_head_out, 1)

            act.wait_ge(s_const, 48)
            act.mul(neg_id[:, :], ident, -1.0).then_inc(s_prep, 1)
            act.wait_ge(s_prep, 3)
            q_masked(0)

            def v_out(c):
                act.wait_ge(s_v_proj, c + 1)
                act.copy(v_rows[:, 4 * c:4 * c + 4, :].rearrange("p g e -> p (g e)"), bank[6 + c % 2][:, :]).then_inc(s_v_rows, 1)

            for c in range(NC - 1):
                v_out(c)

            def x1T_out(c):
                act.wait_ge(s_x1_turned, c + 1)
                act.copy(x1T[:, c, :], bank[6 + c % 2]).then_inc(s_x1T, 1)

            for i in range(STEPS1):
                if i < NG:
                    exps(i)
                if i == 0:
                    v_out(NC - 1)
                if i % 4 == 0 and i // 4 + 1 < NC:
                    q_masked(i // 4 + 1)
                if i % 4 == 1 and i // 4 + 1 < NC:
                    k_masked(i // 4 + 1)
                if 3 <= i < NG + 3:
                    u_out(i - 3)
                if i >= 10 and i % 4 == 2:
                    x1T_out(i // 4 - 2)

            def k_masked2(p):
                act.wait_ge(s_kq_turned, km_count(p, p >= 2))
                if p >= 2:
                    act.wait_ge(s_scores2, p - 1)
                for h in range(4):
                    ins = act.activation(k_heads2[:, p % 2, h, :], bank[4][:, 0:P], ACT.Copy, scale=m_hg[:, h:h + 1])
                if p < 2:
                    ins.then_inc(s_kq_copied, 1)

            def q_out(p):
                if p < 2:
                    act.wait_ge(s_kq_turned, km_count(p, True))
                else:
                    act.wait_ge(s_q_heads2, p - 1)
                act.copy(qT[:, p % 2, :], bank[4][:, P:2 * P]).then_inc(s_kq_copied, 1)

            def exps2(p):
                act.wait_ge(s_shifted2, p + 1)
                if p >= 3:
                    act.wait_ge(s_out_psum, p - 2)
                act.activation(probs2[:, p % 3, :], psum[:, 1024 * (p % 2):1024 * (p % 2) + 1024], ACT.Exp,
                               scale=SCALE2).then_inc(s_exps2, 1)

            def u2_out(p):
                act.wait_ge(s_out_psum, p + 1)
                if p >= 2:
                    act.wait_ge(s_out_turned, p - 1)
                act.copy(out_cols[:, p % 2, :], bank[6][:, 0:256]).then_inc(s_out_cols, 1)

            def on_out(p):
                act.wait_ge(s_out_turned, p + 1)
                if p >= 2:
                    act.wait_ge(s_o_stored[p % 2], 32 * (p // 2))
                for h in range(2):
                    ins = act.copy(out_rows[0:64, p % 2, :].rearrange("t (n j h d) -> t h j n d", n=2, j=8, h=2)[:, h, :, :, :],
                                   bank[7][0:64, 256 * h:256 * h + 256].rearrange(
                                       "t (j n h d) -> t h j n d", n=2, j=8, h=2)[:, h, :, :, :])
                ins.then_inc(s_out_rows, 1)

            def x2T_out(c):
                act.wait_ge(s_x2_turned, c + 1)
                act.copy(x2T[:, 512 * c:512 * c + 512], bank[CHAIN_BANK[c]]).then_inc(s_x2T, 1)

            def exp_logits(c):
                act.wait_ge(s_logits_shifted, 3 * c + 3)
                act.activation(router_probs[:, :, :], router_probs[:, :, :], ACT.Exp).then_inc(s_logit_exps, 1)

            def payload(c):
                act.wait_ge(s_x2, 4 * c + 4)
                for k in range(1, TOPK):
                    act.copy(payloads[:, 4 * c:4 * c + 4, k, 0:E], x2[:, 4 * c:4 * c + 4, :]).then_inc(s_payloads, 1)

            def orT_out(c):
                act.wait_ge(s_o_turned, c + 1)
                if c >= 2:
                    act.wait_ge(s_cross_proj, c - 1)
                act.copy(o_rowsT[:, c % 2, :], bank[CHAIN_BANK[c]]).then_inc(s_o_rowsT, 1)

            def gates_out(c):
                act.wait_ge(s_gates_turned, c + 1)
                if c >= 2:
                    act.wait_ge(s_shared_out, c - 1)
                act.copy(gatesT[:, c % 2, :], bank[GATE_BANK[c]][0:NE + 1, :]).then_inc(s_gatesT, 1)

            def shared_gelu(k):
                for a in range(2):
                    act.wait_ge(s_shared_psum, 2 * k + a + 1)
                    if k >= 2 and a == 0:
                        act.wait_ge(s_shared_out, k // 2)
                    act.activation(h_shared[:, k % 2, a, :], bank[2 * (k % 2) + a], ACT.Gelu,
                                   bias=expert_w[:, NE + k % 2, EW - 2 + a:EW - 1 + a]).then_inc(s_h_shared, 1)

            k_masked2(0)
            k_masked2(1)
            q_out(0)
            q_out(1)
            for i in range(STEPS2):
                if 3 <= i < NP + 3:
                    u2_out(i - 3)
                if i + 2 < NP:
                    k_masked2(i + 2)
                    q_out(i + 2)
                if i >= 4:
                    on_out(i - 4)
                if i < NP:
                    exps2(i)
                for c, turn in enumerate(TURN):
                    if i == turn:
                        orT_out(c)
                    if i == turn + 3 and c == 0:
                        x2T_out(c)
                        payload(c)
                    if i == turn + 4 and c == 0:
                        exp_logits(c)

            on_out(NP - 1)
            x2T_out(1)
            orT_out(2)
            payload(1)
            exp_logits(1)
            gates_out(0)
            shared_gelu(0)
            shared_gelu(1)
            orT_out(3)
            x2T_out(2)
            payload(2)
            exp_logits(2)
            shared_gelu(2)
            gates_out(1)
            x2T_out(3)
            payload(3)
            shared_gelu(3)
            exp_logits(3)
            gates_out(2)
            shared_gelu(4)
            shared_gelu(5)
            gates_out(3)
            shared_gelu(6)
            shared_gelu(7)

            for i in range(NT + 1):
                if i < NT:
                    t = i
                    act.wait_ge(s_tile_psum, t + 1)
                    if t >= 2:
                        act.wait_ge(s_tile_out, t - 1)
                    for a in range(2):
                        ins = act.activation(h_tile[:, t % 2, a, :], bank[2 + t % 2][:, P * a:P * a + P], ACT.Gelu,
                                             bias=stage[:, t % NS, EW - 2 + a:EW - 1 + a])
                    ins.then_inc(s_h_tile, 1)
                if i >= 1:
                    t = i - 1
                    act.wait_ge(s_tile_out, t + 1)
                    if t >= NB:
                        act.wait_ge(s_y_scattered[t % NB], 16 * (t // NB))
                    act.activation(y_tile[:, t % NB, :], bank[6 + t % 2][:, 0:E], ACT.Copy,
                                   scale=x_tile[:, t % NB, E:E + 1]).then_inc(s_y_tile, 1)

            for c in range(NC):
                act.wait_ge(s_rstd3, 4 * c + 4)
                for g in range(4 * c, 4 * c + (4 if c < NC - 1 else 2)):
                    ins = act.activation(acc[:, g, :], acc[:, g, :], ACT.Identity, bias=nmean3[:, g:g + 1],
                                         scale=rstd3[:, g:g + 1])
                ins.then_inc(s_final, 1)

        @block.vector
        def _(dve):
            dve.memset(v_blocks[:, 0:B // 2, :].rearrange("p b e -> p (b e)"), 0.0).then_inc(s_v_zero, 1)
            dve.wait_ge(s_const, 48)
            dve.tensor_scalar(bias_q_masked[:, :], m_hg, bias_cols[:, 0:1], None, ALU.mult)
            dve.tensor_scalar(bias_k_masked[:, :], m_h4, bias_cols[:, 1:2], None, ALU.mult).then_inc(s_prep, 1)
            for h in range(4):
                ins = dve.tensor_scalar(w_out_masked[:, h, :], weights[:, W_O:W_O + E], m_h4[:, h:h + 1], None, ALU.mult)
            ins.then_inc(s_prep, 1)

            dve.wait_ge(s_prep, 3)
            dve.wait_ge(s_k_proj, 1)
            for h in range(4):
                ins = dve.tensor_scalar(k_heads[:, 0, h, :], bank[1][:, :], m_h4[:, h:h + 1], bias_k_masked[:, h:h + 1],
                                        ALU.mult, ALU.add)
            ins.then_inc(s_k_heads, 1)

            def ctx_out(c):
                i, h = c // 2, c % 2
                dve.wait_ge(s_ctx_proj, c + 1)
                r = (R_XK, R_XV)[h]
                dve.tensor_tensor(ctx_kv[:, h, 4 * i:4 * i + 4, :],
                                  bank[0].rearrange("p (g e) -> p g e", e=E),
                                  bias_rows[:, r:r + E].unsqueeze(1).broadcast_to([P, 4, E]), ALU.add).then_inc(s_ctx_kv, 1)

            def row_max(g):
                dve.wait_ge(s_scores, g + 1)
                if g >= 2:
                    dve.wait_ge(s_shifted, g - 1)
                with nc.allow_low_precision(reason="any shift near the maximum serves the softmax"):
                    dve.tensor_reduce(maxes[:, g % 2, :], bank[2 + g % 2][:, :].rearrange("p (a t) -> p a t", t=S),
                                      AX_X, ALU.max).then_inc(s_maxes, 1)

            def row_sum(g):
                dve.wait_ge(s_exps, g + 1)
                dve.tensor_reduce(prob_sums[:, g % 2, :], probs[:, g % 3, :].rearrange("p (a t) -> p a t", t=S),
                                  AX_X, ALU.add).then_inc(s_inv_sums, 1)
                dve.wait_ge(s_inv_sums, 2 * (g + 1) - 1)
                if g >= 2:
                    dve.wait_ge(s_probs, g - 1)
                dve.reciprocal(inv_sums[:, g % 2, :], prob_sums[:, g % 2, :]).then_inc(s_inv_sums, 1)

            def turn(g):
                dve.wait_ge(s_probs, g + 1)
                if g >= 2:
                    dve.wait_ge(s_head_psum, g - 1)
                dve.transpose(probs_turned[:, g % 2, :], probs[:, g % 3, :]).then_inc(s_probs_turned, 1)

            def ln1_stats(c):
                dve.wait_ge(s_attn_proj, 4 * c + 4)
                if c >= 2:
                    dve.wait_ge(s_x1, 4 * (c - 1))
                    dve.wait_ge(s_x1_stored[c % 2], 64 * (c // 2))
                    dve.wait_ge(s_x1_turned, c - 1)
                dve.tensor_tensor(x1_pre[:, c % 2, :, :].rearrange("p g e -> p (g e)"), bank[6 + c % 2][:, :],
                                  x_rows[:, 4 * c:4 * c + 4, :].rearrange("p g e -> p (g e)"), ALU.add).then_inc(s_ln1, 1)
                dve.wait_ge(s_ln1, 3 * (c + 1) - 2)
                for j in range(4):
                    ins = dve.bn_stats(bn1[:, c % 2, j, :], x1_pre[:, c % 2, j, :])
                ins.then_inc(s_ln1, 1)
                dve.wait_ge(s_ln1, 3 * (c + 1) - 1)
                for j in range(4):
                    ins = dve.bn_aggr(mean_var1[:, c % 2, j, :], bn1[:, c % 2, j, :])
                ins.then_inc(s_ln1, 1)

            def ln1_apply(c):
                dve.wait_ge(s_rstd1, 2 * (c + 1))
                for j in range(4):
                    dve.tensor_scalar(x1_pre[:, c % 2, j, :], x1_pre[:, c % 2, j, :], mean_var1[:, c % 2, j, 0:1],
                                      rstd1[:, c % 2, j:j + 1], ALU.subtract, ALU.mult).then_inc(s_x1, 1)

            def cq_out(c):
                dve.wait_ge(s_cq_proj, c + 1)
                if c >= 2:
                    dve.wait_ge(s_cq_stored[c - 2], 64)
                dve.tensor_tensor(cq_proj[:, c % 2, :, :], bank[6 + c % 2].rearrange("p (g e) -> p g e", e=E),
                                  bias_rows[:, R_XQ:R_XQ + E].unsqueeze(1).broadcast_to([P, 4, E]), ALU.add).then_inc(s_cq, 1)

            for i in range(STEPS1):
                if i == 0:
                    row_max(0)
                if 1 <= i < NG + 1:
                    row_sum(i - 1)
                if i + 1 < NG:
                    row_max(i + 1)
                if 2 <= i < NG + 2:
                    turn(i - 2)
                if i == CTX_STEPS[0]:
                    dve.wait_ge(s_bias_rows, 16)
                if i in CTX_STEPS:
                    ctx_out(CTX_STEPS.index(i))
                if i >= 8 and i % 4 == 0 and i // 4 - 2 < NC - 1:
                    ln1_stats(i // 4 - 2)
                if i == NG + 3:
                    ln1_stats(NC - 1)
                if i >= 9 and i % 4 == 1 and i // 4 - 2 < NC:
                    ln1_apply(i // 4 - 2)
                if i >= 11 and i % 4 == 3:
                    cq_out(i // 4 - 2)

            def q_masked2(p):
                dve.wait_ge(s_kq_copied, km_count(p, True))
                if p >= 2:
                    dve.wait_ge(s_scores2, p - 1)
                dve.tensor_tensor(q_heads2[:, p % 2, :, :], qT[:, p % 2, :].unsqueeze(1).broadcast_to([P, 4, P]),
                                  m_h4.unsqueeze(2).broadcast_to([P, 4, P]), ALU.mult).then_inc(s_q_heads2, 1)

            def head_max(p):
                dve.wait_ge(s_scores2, p + 1)
                if p >= 2:
                    dve.wait_ge(s_shifted2, p - 1)
                with nc.allow_low_precision(reason="any shift near the maximum serves the softmax"):
                    dve.tensor_reduce(maxes2[:, p % 2, :],
                                      psum[:, 1024 * (p % 2):1024 * (p % 2) + 1024].rearrange("p (h t) -> p t h", t=B),
                                      AX_X, ALU.max).then_inc(s_maxes2, 1)

            def head_sum(p):
                dve.wait_ge(s_exps2, p + 1)
                dve.tensor_reduce(prob_sums2[:, p % 2, :], probs2[:, p % 3, :].rearrange("p (h t) -> p t h", t=B),
                                  AX_X, ALU.add).then_inc(s_inv_sums2, 1)
                dve.wait_ge(s_inv_sums2, 2 * (p + 1) - 1)
                if p >= 2:
                    dve.wait_ge(s_probs2, p - 1)
                dve.reciprocal(inv_sums2[:, p % 2, :], prob_sums2[:, p % 2, :]).then_inc(s_inv_sums2, 1)

            def ln2_stats(c):
                dve.wait_ge(s_cross_proj, c + 1)
                dve.wait_ge(s_x1_biased, c + 1)
                if c >= 2:
                    dve.wait_ge(s_x2, 4 * (c - 1))
                dve.tensor_tensor(x2_pre[:, c % 2, :, :].rearrange("p g e -> p (g e)"), bank[CHAIN_BANK[c]],
                                  x1[:, 4 * c:4 * c + 4, :].rearrange("p g e -> p (g e)"), ALU.add).then_inc(s_ln2, 1)
                dve.wait_ge(s_ln2, 3 * (c + 1) - 2)
                for j in range(4):
                    ins = dve.bn_stats(bn2[:, c % 2, j, :], x2_pre[:, c % 2, j, :])
                ins.then_inc(s_ln2, 1)
                dve.wait_ge(s_ln2, 3 * (c + 1) - 1)
                for j in range(4):
                    ins = dve.bn_aggr(mean_var2[:, c % 2, j, :], bn2[:, c % 2, j, :])
                ins.then_inc(s_ln2, 1)

            def ln2_apply(c):
                dve.wait_ge(s_rstd2, 2 * (c + 1))
                for j in range(4):
                    dve.tensor_scalar(x2[:, 4 * c + j, :], x2_pre[:, c % 2, j, :], mean_var2[:, c % 2, j, 0:1],
                                      rstd2[:, c % 2, j:j + 1], ALU.subtract, ALU.mult).then_inc(s_x2, 1)

            step = [0]

            def routed(ins):
                step[0] += 1
                ins.then_inc(s_routed, 1)
                dve.wait_ge(s_routed, step[0])

            def route_logits(c):
                lc = router_probs[:, 0:4, :]
                dve.wait_ge(s_logits, c + 1)
                dve.tensor_tensor(lc, bank[CHAIN_BANK[c]][:, 0:64].rearrange("p (g e) -> p g e", e=16)[:, :, 0:NE],
                                  router_b[:, :].unsqueeze(1).broadcast_to([P, 4, NE]), ALU.add).then_inc(s_logits_shifted, 1)
                dve.wait_ge(s_logits_shifted, 3 * c + 1)
                dve.tensor_reduce(logit_max[:, 4 * c:4 * c + 4], lc, AX_X, ALU.max).then_inc(s_logits_shifted, 1)
                dve.wait_ge(s_logits_shifted, 3 * c + 2)
                dve.tensor_tensor(lc, lc, logit_max[:, 4 * c:4 * c + 4].unsqueeze(2).broadcast_to([P, 4, NE]),
                                  ALU.subtract).then_inc(s_logits_shifted, 1)

            def route_top(c):
                lc = router_probs[:, 0:4, :]
                lsc = logit_sum[:, 4 * c:4 * c + 4]
                dve.wait_ge(s_logit_exps, c + 1)
                routed(dve.tensor_reduce(lsc, lc, AX_X, ALU.add))
                routed(dve.reciprocal(lsc, lsc))
                routed(dve.tensor_tensor(lc, lc, lsc.unsqueeze(2).broadcast_to([P, 4, NE]), ALU.mult))
                for g in range(4 * c, 4 * c + 4):
                    ins = dve.max(top_gates[:, g % 4, :], router_probs[:, g % 4, :])
                routed(ins)
                for g in range(4 * c, 4 * c + 4):
                    ins = dve.max_index(top_experts[:, g % 4, :], top_gates[:, g % 4, :], router_probs[:, g % 4, :])
                routed(ins)
                o4 = one_hot[:, :, :, :]
                routed(dve.tensor_tensor(o4, row_consts[:, K_IOTA:K_IOTA + NE].unsqueeze(1).unsqueeze(1).broadcast_to([P, 4, TOPK, NE]),
                                         top_experts[:, :, 0:TOPK].unsqueeze(3).broadcast_to([P, 4, TOPK, NE]), ALU.is_equal))
                with nc.allow_low_precision(reason="zeros and ones"):
                    routed(dve.tensor_reduce(chosen[:, 4 * c:4 * c + 4, :], o4.rearrange("p g k e -> p g e k"), AX_X, ALU.add))
                with nc.allow_low_precision(reason="small whole numbers"):
                    routed(dve.tensor_reduce(chosen_sum[:, :], chosen[:, 4 * c:4 * c + 4, :].rearrange("p g e -> p e g"), AX_X, ALU.add))
                    dve.tensor_tensor(carry[:, c + 1, :], carry[:, c, :], chosen_sum[:, :], ALU.add).then_inc(s_chosen, 1)

            def route_slots(c):
                o4 = one_hot[:, 0:4, :, :]
                dve.wait_ge(s_ranks, c + 1)
                if c == NC - 1:
                    dve.wait_ge(s_counts, 1)
                    routed(dve.tensor_copy(counts[:, :], bank[7][:, 64:64 + NE]))
                    dve.tensor_tensor(ends[:, :], counts[:, :], row_consts[:, K_BASE:K_BASE + NE], ALU.add).then_inc(s_ends, 1)
                dve.tensor_tensor(sorted_rank[:, :, :], bank[CHAIN_BANK[c]][:, 0:64].rearrange("p (g e) -> p g e", e=16)[:, :, 0:NE],
                                  row_consts[:, K_BASE:K_BASE + NE].unsqueeze(1).broadcast_to([P, 4, NE]), ALU.add).then_inc(s_slots, 1)
                dve.wait_ge(s_slots, 3 * c + 1)
                routed(dve.tensor_tensor(selected[:, :, :].rearrange("p (g k) e -> p g k e", k=TOPK), o4,
                                         sorted_rank[:, :, :].unsqueeze(2).broadcast_to([P, 4, TOPK, NE]), ALU.mult))
                dve.tensor_copy(payloads[:, 4 * c:4 * c + 4, :, E], top_gates[:, 0:4, 0:TOPK]).then_inc(s_slots, 1)
                with nc.allow_low_precision(reason="whole numbers below 2**24"):
                    dve.tensor_reduce(slot[:, 12 * c:12 * c + 12], selected[:, :, :], AX_X, ALU.add).then_inc(s_slots, 1)
                routed(dve.tensor_tensor(o4, o4, top_gates[:, :, 0:TOPK].unsqueeze(3).broadcast_to([P, 4, TOPK, NE]), ALU.mult))
                dve.tensor_reduce(gates[:, 4 * c:4 * c + 4, 0:NE], o4.rearrange("p g k e -> p g e k"),
                                  AX_X, ALU.add).then_inc(s_gates, 1)

            dve.tensor_copy(tri[:, :], consts[:, C_TRI:C_TRI + P]).then_inc(s_router_ready, 1)
            dve.memset(ones[:, :], 1.0).then_inc(s_router_ready, 1)
            dve.memset(gates[:, :, NE:NE + 1], 1.0)
            dve.memset(carry[:, 0, :], 0.0).then_inc(s_router_ready, 1)
            dve.memset(pad[:, :], 0.0).then_inc(s_router_ready, 1)
            dve.wait_ge(s_small, 80)
            dve.wait_ge(s_head_psum, NG)
            dve.tensor_copy(payloads[:, :, :, E + 1].bitcast(I32),
                            result_rows[:, 0:NG * TOPK].rearrange("p (g k) -> p g k", k=TOPK)).then_inc(s_router_ready, 1)
            dve.wait_ge(s_router_ready, 5)
            def shared_result(c):
                dve.wait_ge(s_shared_out, c + 1)
                dve.scalar_tensor_tensor(out=acc[:, 4 * c:4 * c + 4, :],
                                         in0=x2[:, 4 * c:4 * c + 4, :], scalar=2.0,
                                         in1=bank[4].rearrange("p (g e) -> p g e", e=E),
                                         op0=ALU.mult, op1=ALU.add).then_inc(s_acc, 1)

            for i in range(STEPS2):
                if i == 0:
                    q_masked2(0)
                    q_masked2(1)
                    head_max(0)
                if 1 <= i < NP + 1:
                    head_sum(i - 1)
                if i + 2 < NP:
                    q_masked2(i + 2)
                if i + 1 < NP:
                    head_max(i + 1)
                turn = TURN[0]
                if i == turn + 1:
                    ln2_stats(0)
                if i == turn + 2:
                    ln2_apply(0)
                if i == turn + 4:
                    route_logits(0)
                if i == turn + 5:
                    route_top(0)
                if i == turn + 6:
                    ln2_stats(1)
                    route_slots(0)
                    ln2_apply(1)
            route_logits(1)
            route_top(1)
            ln2_stats(2)
            route_slots(1)
            ln2_apply(2)
            ln2_stats(3)
            ln2_apply(3)
            route_logits(2)
            route_top(2)
            shared_result(0)
            route_slots(2)
            route_logits(3)
            shared_result(1)
            route_top(3)
            route_slots(3)

            NJ = T // P
            routed(dve.tensor_tensor(table_room[:, 0:NE * NJ].rearrange("p (e j) -> p e j", j=NJ),
                                     counts[0:1, :].unsqueeze(2).broadcast_to([1, NE, NJ]),
                                     row_consts[0:1, K_J:K_J + NJ].unsqueeze(1).broadcast_to([1, NE, NJ]), ALU.is_gt))
            routed(dve.tensor_reduce(tiles_of[0:1, :], table_room[:, 0:NE * NJ].rearrange("p (e j) -> p e j", j=NJ), AX_X, ALU.add))
            routed(dve.tensor_tensor(table_room[:, 0:NE * NE].rearrange("p (e j) -> p e j", j=NE),
                                     tiles_of[0:1, :].unsqueeze(1).broadcast_to([1, NE, NE]),
                                     row_consts[0:1, K_L:K_END].rearrange("p (e j) -> p e j", j=NE), ALU.mult))
            routed(dve.tensor_reduce(counts[0:1, :], table_room[:, 0:NE * NE].rearrange("p (e j) -> p e j", j=NE), AX_X, ALU.add))
            shared_result(2)
            big_te = table_room[:, 0:TABLE * NE].rearrange("p (t e) -> p t e", e=NE)
            routed(dve.tensor_tensor(big_te, counts[0:1, :].unsqueeze(1).broadcast_to([1, TABLE, NE]),
                                     row_consts[0:1, K_T:K_T + TABLE].unsqueeze(2).broadcast_to([1, TABLE, NE]), ALU.is_le))
            routed(dve.tensor_reduce(tile_expert_f[0:1, :], big_te, AX_X, ALU.add))
            routed(dve.tensor_tensor(big_te, big_te, tiles_of[0:1, :].unsqueeze(1).broadcast_to([1, TABLE, NE]), ALU.mult))
            routed(dve.tensor_reduce(tile_row_f[0:1, :], big_te, AX_X, ALU.add))
            routed(dve.scalar_tensor_tensor(out=tile_row_f[0:1, :], in0=tile_row_f[0:1, :], scalar=-float(P),
                                            in1=row_consts[0:1, K_TP:K_TP + TABLE], op0=ALU.mult, op1=ALU.add))
            routed(dve.scalar_tensor_tensor(out=tile_row_f[0:1, :], in0=tile_expert_f[0:1, :], scalar=float(ROOM),
                                            in1=tile_row_f[0:1, :], op0=ALU.mult, op1=ALU.add))
            routed(dve.tensor_scalar(tile_row_f[0:1, :], tile_row_f[0:1, :], float(NE * ROOM), None, ALU.min))
            routed(dve.tensor_copy(t_row[:, :], tile_row_f[0:1, :]))
            dve.tensor_copy(t_expert[:, :], tile_expert_f[0:1, :]).then_inc(s_tables, 1)

            shared_result(3)
            dve.wait_ge(s_tables, 1)

            def expert_staged(t, expert_of):
                if t % 4 == 0:
                    expert_of = nc.values_load_multi_w_load_instructions(
                        t_expert[0:1, t:t + 4], engines=[mybir.EngineType.DVE], min_val=0, max_val=NE,
                        skip_runtime_bounds_check_because="the table counts the experts that end before the tile")[1]
                if t >= NS:
                    dve.wait_ge(s_tile_out, t - NS + 1)
                dve.tensor_copy(stage[:, t % NS, :],
                                expert_w[:, bass.ds(expert_of[t % 4], 1), :].rearrange("p a b -> p (a b)")).then_inc(s_staged, 1)
                return expert_of

            def tile_rows(first):
                n = min(4, NT - first)
                for t in range(first, first + n):
                    dve.wait_ge(s_x_tile[t % NB], 16 * (t // NB + 1))
                dve.tensor_tensor(y_rows[:, first:first + n], x_tile[:, first % NB:first % NB + n, E + 1].bitcast(I32),
                                  result_rows[:, NG * TOPK + first:NG * TOPK + first + n], ALU.max).then_inc(s_y_rows, 1)

            def xinT_out(t):
                dve.wait_ge(s_tile_turned, t + 1)
                if t >= 2:
                    dve.wait_ge(s_tile_psum, t - 1)
                dve.tensor_copy(x_tileT[:, t % 2, :], bank[t % 2][:, 0:P]).then_inc(s_x_tileT, 1)

            expert_of = None
            for t in range(NS):
                expert_of = expert_staged(t, expert_of)
            for t in range(NT):
                xinT_out(t)
                if t % 4 == 1:
                    tile_rows(t - 1)
                if NS <= t + 2 < NT:
                    expert_of = expert_staged(t + 2, expert_of)

            for c in range(2):
                dve.wait_ge(s_y_loaded[c], 16 * TOPK)
                dve.tensor_tensor(acc[:, 4 * c:4 * c + 4, :], acc[:, 4 * c:4 * c + 4, :],
                                  routed_y[2][:, 4 * c:4 * c + 4, :], ALU.add).then_inc(s_y_sum, 1)
            for c in range(NC):
                if c < 2:
                    dve.wait_ge(s_y_sum, 2)
                else:
                    dve.wait_ge(s_y3, c - 1)
                dve.wait_ge(s_y12, c + 1)
                dve.tensor_tensor(acc[:, 4 * c:4 * c + 4, :], acc[:, 4 * c:4 * c + 4, :],
                                  bank[c].rearrange("p (g e) -> p g e", e=E), ALU.add).then_inc(s_y_sum, 1)
                dve.wait_ge(s_y_sum, c + 3)
                for j in range(4):
                    ins = dve.bn_stats(bn3[:, 4 * c + j, :], acc[:, 4 * c + j, :])
                ins.then_inc(s_ln3, 1)
                dve.wait_ge(s_ln3, 2 * c + 1)
                for j in range(4):
                    ins = dve.bn_aggr(mean_var3[:, 4 * c + j, :], bn3[:, 4 * c + j, :])
                ins.then_inc(s_ln3, 1)
            dve.wait_ge(s_rstd3, 4 * NC)
            for g in range(NG - 2, NG):
                ins = dve.tensor_scalar(acc[:, g, :], acc[:, g, :], rstd3[:, g:g + 1], nmean3[:, g:g + 1],
                                        ALU.mult, ALU.add)
            ins.then_inc(s_y_sum, 1)

        @block.gpsimd
        def _(pool):
            pool.memset(v_blocks[:, B // 2:B, :].rearrange("p b e -> p (b e)"), 0.0).then_inc(s_v_zero, 1)
            pool.memset(minus_half[:, :], -0.5)
            pool.wait_ge(s_x_rows, 16)
            pool.wait_ge(s_bias_rows, 16)
            pool.tensor_tensor(x_rows[:, :, :], x_rows[:, :, :],
                               bias_rows[:, R_BO:R_BO + E].unsqueeze(1).broadcast_to([P, NG, E]), ALU.add).then_inc(s_x_biased, 1)

            def normalise(g):
                pool.wait_ge(s_inv_sums, 2 * (g + 1))
                pool.tensor_tensor(probs[:, g % 3, :].rearrange("p (a t) -> p a t", t=S),
                                   probs[:, g % 3, :].rearrange("p (a t) -> p a t", t=S),
                                   inv_sums[:, g % 2, :].unsqueeze(2).broadcast_to([P, 16, S]), ALU.mult).then_inc(s_probs, 1)

            def rsqrt1(c):
                pool.wait_ge(s_ln1, 3 * (c + 1))
                pool.tensor_scalar(rstd1[:, c % 2, :], mean_var1[:, c % 2, :, 1], EPS, None, ALU.add).then_inc(s_rstd1, 1)
                pool.wait_ge(s_rstd1, 2 * (c + 1) - 1)
                pool.tensor_tensor(rstd1[:, c % 2, :], rstd1[:, c % 2, :], minus_half[:, :], ALU.pow).then_inc(s_rstd1, 1)

            def v_apart(p):
                pool.wait_ge(s_ctx_loaded[p // 4], 256)
                pool.tensor_tensor(v_pairs[:, p, :, :, :],
                                   ctx_kv[:, 1, p, :].rearrange("p (j c) -> p j c", j=8).unsqueeze(2).broadcast_to([P, 8, 2, 16]),
                                   m_n2.unsqueeze(1).unsqueeze(3).broadcast_to([P, 8, 2, 16]), ALU.mult).then_inc(s_v_pairs, 1)

            def x1_out(g):
                pool.wait_ge(s_x1, g + 1)
                pool.dma_start(x1_scr.rearrange("(s b) e -> b s e", b=B)[4 * g:4 * g + 4, :, :],
                               x1_pre[:, g // 4 % 2, g % 4, :]).then_inc(s_x1_stored[g // 4 % 2], 16)

            def normalise2(p):
                pool.wait_ge(s_inv_sums2, 2 * (p + 1))
                pool.tensor_tensor(probs2[:, p % 3, :].rearrange("p (h t) -> p h t", t=B),
                                   probs2[:, p % 3, :].rearrange("p (h t) -> p h t", t=B),
                                   inv_sums2[:, p % 2, :].unsqueeze(1).broadcast_to([P, 16, B]), ALU.mult).then_inc(s_probs2, 1)

            def x1_biased(c):
                pool.wait_ge(s_x1_loaded[c], 16)
                pool.tensor_tensor(x1[:, 4 * c:4 * c + 4, :], x1[:, 4 * c:4 * c + 4, :],
                                   bias_rows[:, R_XO:R_XO + E].unsqueeze(1).broadcast_to([P, 4, E]), ALU.add).then_inc(s_x1_biased, 1)

            def rsqrt2(c):
                pool.wait_ge(s_ln2, 3 * (c + 1))
                pool.tensor_scalar(rstd2[:, c % 2, :], mean_var2[:, c % 2, :, 1], EPS, None, ALU.add).then_inc(s_rstd2, 1)
                pool.wait_ge(s_rstd2, 2 * (c + 1) - 1)
                pool.tensor_tensor(rstd2[:, c % 2, :], rstd2[:, c % 2, :], minus_half[:, :], ALU.pow).then_inc(s_rstd2, 1)

            for i in range(1, NG + 4):
                if i <= NG:
                    normalise(i - 1)
                if i >= 8 and i % 4 == 0:
                    rsqrt1(i // 4 - 2)
                if 6 <= i < 18:
                    v_apart(i - 6)
                if i >= 10 and i % 4 in (2, 3):
                    for j in range(2):
                        x1_out(4 * (i // 4 - 2) + 2 * (i % 4 - 2) + j)
            rsqrt1(NC - 1)
            for g in range(4 * (NC - 1), NG):
                x1_out(g)
            for p in range(12, NP):
                v_apart(p)

            def scatter(first, count):
                for n in range(first, first + count):
                    g, k = n // TOPK, n % TOPK
                    if n % 12 == 0 or n == first:
                        pool.wait_ge(s_slots, 3 * (g // 4) + 3)
                        pool.wait_ge(s_payloads, 2 * (g // 4) + 2)
                    pool.indirect_dma_start(out=x_srt, out_offset=bass.IndirectOffsetOnAxis(
                        ap=slot[:, n:n + 1], axis=0), in_=payloads[:, g, k, :], in_offset=None).then_inc(s_scattered, 16)

            for c in range(NC):
                x1_biased(c)
            for i in range(1, STEPS2):
                if i <= NP:
                    normalise2(i - 1)
                if i - 1 == TURN[0]:
                    rsqrt2(0)
            rsqrt2(1)
            scatter(0, 12)
            rsqrt2(2)
            scatter(12, 4)
            rsqrt2(3)
            scatter(16, 32)
            for t in range(NT):
                pool.wait_ge(s_y_tile, t + 1)
                pool.wait_ge(s_y_rows, t // 4 + 1)
                pool.indirect_dma_start(out=y_tok, out_offset=bass.IndirectOffsetOnAxis(
                    ap=y_rows[:, t:t + 1].bitcast(mybir.dt.uint32), axis=0),
                    in_=y_tile[:, t % NB, :], in_offset=None).then_inc(s_y_scattered[t % NB], 16)

            def third_added(c):
                pool.wait_ge(s_y_loaded[c], 16 * TOPK)
                pool.wait_ge(s_acc, NC)
                pool.tensor_tensor(acc[:, 4 * c:4 * c + 4, :], acc[:, 4 * c:4 * c + 4, :],
                                   routed_y[2][:, 4 * c:4 * c + 4, :], ALU.add).then_inc(s_y3, 1)

            for c in range(NC):
                if c < 2:
                    third_added(c + 2)
                pool.wait_ge(s_ln3, 2 * c + 2)
                r = rstd3[:, 4 * c:4 * c + 4]
                nm = nmean3[:, 4 * c:4 * c + 4]
                pool.tensor_scalar(r, mean_var3[:, 4 * c:4 * c + 4, 1], EPS, None, ALU.add).then_inc(s_rstd3, 1)
                pool.tensor_scalar(nm, mean_var3[:, 4 * c:4 * c + 4, 0], -1.0, None, ALU.mult).then_inc(s_rstd3, 1)
                pool.wait_ge(s_rstd3, 4 * c + 2)
                pool.tensor_tensor(r, r, minus_half[:, :], ALU.pow).then_inc(s_rstd3, 1)
                pool.wait_ge(s_rstd3, 4 * c + 3)
                pool.tensor_tensor(nm, nm, r, ALU.mult).then_inc(s_rstd3, 1)


def layout(inputs):
    import numpy as np

    def f(name):
        return np.asarray(inputs[name])

    x, c = f("x"), f("ctx_1024")
    p = np.arange(P)
    w_in = f("L0_attn_in_proj_w").T
    a = {}
    a["x_t"] = x.transpose(2, 1, 0).reshape(E, T)
    a["x_n"] = x.transpose(1, 0, 2).reshape(NG, P, E).transpose(1, 0, 2)
    a["ctx_t"] = c.reshape(T, E).T
    a["w_pack"] = np.concatenate([w_in, f("L0_attn_out_proj_w").T, f("L0_xattn_Wq"), f("L0_xattn_Wk"),
                                  f("L0_xattn_Wv"), f("L0_xattn_Wo")], axis=1)
    a["c_pack"] = np.concatenate(
        [np.eye(P)] + [(p // 32 == g)[:, None] for g in range(4)] + [((p // 8) % 4 == h)[:, None] for h in range(4)]
        + [(p // 64 == n)[:, None] for n in range(2)]
        + [p[:, None] < p[None, :]],
        axis=1).astype(np.float32)
    bi = f("L0_attn_in_proj_b")
    a["b_col"] = np.stack([bi[0:E], bi[E:2 * E], bi[2 * E:3 * E]], axis=1)
    a["b_row"] = np.concatenate([f("L0_attn_out_proj_b"), f("L0_xattn_bq"), f("L0_xattn_bk"), f("L0_xattn_bv"),
                                 f("L0_xattn_bo")])
    w1 = np.concatenate([f("L0_ffn_rW1"), f("L0_ffn_sW1").reshape(E, 2, FE).transpose(1, 0, 2)])
    w2 = np.concatenate([f("L0_ffn_rW2"), f("L0_ffn_sW2").reshape(2, FE, E)])
    w2 = w2.reshape(NX, 2, P, E).transpose(0, 2, 1, 3).reshape(NX, P, 2 * E)
    b1 = np.concatenate([f("L0_ffn_rb1"), f("L0_ffn_sb1").reshape(2, FE)]).reshape(NX, 2, P).transpose(0, 2, 1)
    a["e_w"] = np.concatenate([w1, w2, b1], axis=2)
    a["e_b2"] = np.concatenate([f("L0_ffn_rb2"), f("L0_ffn_sb2")])
    a["g_w"] = f("L0_ffn_gW")
    a["g_b"] = f("L0_ffn_gb")
    e, t = np.arange(NE), np.arange(TABLE)
    a["k_row"] = np.concatenate([e, ROOM * e, t, P * t, P * np.arange(T // P),
                                 (e[None, :] <= e[:, None]).ravel()]).astype(np.float32)
    rows = NT * P + np.arange(TOPK)[None, None, :] * T + P * np.arange(NG)[None, :, None] + p[:, None, None]
    a["dst_rows"] = np.concatenate([rows.reshape(P, NG * TOPK), P * t[None, :] + p[:, None]], axis=1).astype(np.int32)
    return {k: np.ascontiguousarray(v) for k, v in a.items()}


def kernel(**inputs):
    import numpy as np
    import concourse.bacc as bacc
    from concourse.bass_utils import run_bass_kernel_spmd

    nc = bacc.Bacc("TRN2", target_bir_lowering=False, num_devices=1)
    arrays = layout(inputs)
    args = [nc.dram_tensor(n, a.shape, mybir.dt.from_np(a.dtype), kind="ExternalInput").ap()
            for n, a in arrays.items()]
    out = nc.dram_tensor("out", (S, B, E), F32, kind="ExternalOutput").ap()
    build(nc, *args, out)
    r = run_bass_kernel_spmd(nc, [arrays], core_ids=[0])
    return r.results[0]["out"]
```
